# Optimizing a Trainium2 kernel written in Bass

```python
import numpy as np
import jax
import jax.numpy as jnp

def _softmax(x, axis=-1):
    return jax.nn.softmax(x, axis=axis)

def _gelu(x):
    return jax.nn.gelu(x, approximate=True)

def _silu(x):
    return jax.nn.silu(x)

def _sigmoid(x):
    return jax.nn.sigmoid(x)

def _layernorm(x, axis=-1, eps=1e-05):
    m = jnp.mean(x, axis=axis, keepdims=True)
    v = jnp.var(x, axis=axis, keepdims=True)
    return (x - m) / jnp.sqrt(v + eps)

def _scatter_add(tgt, idx, src, axis=0):
    return tgt.at[idx].add(src)

def _segment_sum(src, seg, n):
    return jax.ops.segment_sum(src, seg, n)
kernel_name = 'mk_seq_preln_d1_jaxref_r4_b820ba'

def setup_inputs(seed: int=0):
    np.random.seed(seed)
    _w = jnp.asarray

    def _L0_attn_setup():
        import jax, jax.numpy as jnp
        import numpy as np
        B, T, D, H = (4, 512, 256, 16)
        HD = D // H
        NEG = -np.finfo(np.float32).max
        key = jax.random.key(seed)
        ks = jax.random.split(key, 9)
        s = 1.0 / np.sqrt(D)
        return {'x': jax.random.normal(ks[0], (B, T, D), jnp.float32), 'wq': jax.random.normal(ks[1], (D, D), jnp.float32) * s, 'bq': jax.random.normal(ks[2], (D,), jnp.float32) * 0.02, 'wk': jax.random.normal(ks[3], (D, D), jnp.float32) * s, 'bk': jax.random.normal(ks[4], (D,), jnp.float32) * 0.02, 'wv': jax.random.normal(ks[5], (D, D), jnp.float32) * s, 'bv': jax.random.normal(ks[6], (D,), jnp.float32) * 0.02, 'wo': jax.random.normal(ks[7], (D, D), jnp.float32) * s, 'bo': jax.random.normal(ks[8], (D,), jnp.float32) * 0.02}
    _L0_attn_in = _L0_attn_setup()

    def _L0_ffn_setup():
        import jax, jax.numpy as jnp
        import numpy as np
        DIM = 256
        DEPTH = 2
        HEADS = 8
        DIM_HEAD = 64
        WINDOW = 128
        INNER = HEADS * DIM_HEAD
        HID = int(DIM * 4 * 2 / 3)
        B, N = (2, 2048)
        QK_SCALE = 8.0

        def shift_token(t):
            t1, t2 = jnp.split(t, 2, axis=-1)
            t2 = jnp.pad(t2, ((0, 0), (1, 0), (0, 0)))[:, :-1]
            return jnp.concatenate([t1, t2], axis=-1)

        def l2norm(t):
            return t / jnp.clip(jnp.linalg.norm(t, axis=-1, keepdims=True), 1e-12)

        def rotate_half(x):
            x1, x2 = jnp.split(x, 2, axis=-1)
            return jnp.concatenate([-x2, x1], axis=-1)

        def rotary_xpos(q, k):
            n = q.shape[-2]
            half_idx = jnp.arange(0, DIM_HEAD, 2, dtype=jnp.float32)
            inv_freq = 1.0 / 10000.0 ** (half_idx / DIM_HEAD)
            t = jnp.arange(n, dtype=jnp.float32)
            freqs = t[:, None] * inv_freq[None, :]
            freqs = jnp.concatenate([freqs, freqs], axis=-1)
            base = (half_idx + 0.4 * DIM_HEAD) / (1.4 * DIM_HEAD)
            power = (t - n // 2) / float(WINDOW // 2)
            scale = base[None, :] ** power[:, None]
            scale = jnp.concatenate([scale, scale], axis=-1)
            cos, sin = (jnp.cos(freqs), jnp.sin(freqs))
            q = q * cos * scale + rotate_half(q) * sin * scale
            k = k * cos / scale + rotate_half(k) * sin / scale
            return (q, k)

        def local_attention(q, k, v):
            b, h, n, d = q.shape
            w = n // WINDOW
            bq = q.reshape(b, h, w, WINDOW, d) * QK_SCALE
            bk = k.reshape(b, h, w, WINDOW, d)
            bv = v.reshape(b, h, w, WINDOW, d)

            def look_around(t):
                p = jnp.pad(t, ((0, 0), (0, 0), (1, 0), (0, 0), (0, 0)))
                return jnp.concatenate([p[:, :, :w], p[:, :, 1:]], axis=3)
            bk, bv = (look_around(bk), look_around(bv))
            bt = jnp.arange(n).reshape(w, WINDOW)
            btp = jnp.pad(bt, ((1, 0), (0, 0)), constant_values=-1)
            btk = jnp.concatenate([btp[:w], btp[1:]], axis=1)
            sim = jnp.einsum('bhwid,bhwjd->bhwij', bq, bk)
            i = bt[:, :, None]
            j = btk[:, None, :]
            mask = (i < j) | (i > j + WINDOW) | (j == -1)
            sim = jnp.where(mask, -jnp.finfo(sim.dtype).max, sim)
            attn = jax.nn.softmax(sim, axis=-1)
            out = jnp.einsum('bhwij,bhwjd->bhwid', attn, bv)
            return out.reshape(b, h, n, d)

        def _layer(x, wqkv, qs, ksc, wo, lg, lb, w1, b1, w2, b2):
            b, n, _ = x.shape
            h = shift_token(x)
            qkv = h @ wqkv
            q, k, v = jnp.split(qkv, 3, axis=-1)
            to_heads = lambda t: t.reshape(b, n, HEADS, DIM_HEAD).transpose(0, 2, 1, 3)
            q, k, v = (to_heads(q), to_heads(k), to_heads(v))
            q = l2norm(q) * qs
            k = l2norm(k) * ksc
            q, k = rotary_xpos(q, k)
            o = local_attention(q, k, v)
            o = o.transpose(0, 2, 1, 3).reshape(b, n, INNER)
            x = x + o @ wo
            h = shift_token(x)
            mu = h.mean(-1, keepdims=True)
            var = h.var(-1, keepdims=True)
            h = (h - mu) / jnp.sqrt(var + 1e-05) * lg + lb
            h = h @ w1 + b1
            a, g = jnp.split(h, 2, axis=-1)
            h = a * jax.nn.gelu(g, approximate=False)
            x = x + h @ w2 + b2
            return x
        key = jax.random.key(seed)
        ks = jax.random.split(key, 6)
        return {'x': jax.random.normal(ks[0], (B, N, DIM), jnp.float32), 'wqkv': jax.random.normal(ks[1], (DEPTH, DIM, 3 * INNER), jnp.float32) * 0.02, 'q_scale': jnp.ones((DEPTH, DIM_HEAD), jnp.float32), 'k_scale': jnp.ones((DEPTH, DIM_HEAD), jnp.float32), 'wo': jax.random.normal(ks[2], (DEPTH, INNER, DIM), jnp.float32) * 0.02, 'ln_g': jnp.ones((DEPTH, DIM), jnp.float32), 'ln_b': jnp.zeros((DEPTH, DIM), jnp.float32), 'w1': jax.random.normal(ks[3], (DEPTH, DIM, 2 * HID), jnp.float32) * 0.02, 'b1': jnp.zeros((DEPTH, 2 * HID), jnp.float32), 'w2': jax.random.normal(ks[4], (DEPTH, HID, DIM), jnp.float32) * 0.02, 'b2': jnp.zeros((DEPTH, DIM), jnp.float32)}
    _L0_ffn_in = _L0_ffn_setup()
    _d = {'L0_attn_x': _L0_attn_in['x'], 'L0_attn_wq': _L0_attn_in['wq'], 'L0_attn_bq': _L0_attn_in['bq'], 'L0_attn_wk': _L0_attn_in['wk'], 'L0_attn_bk': _L0_attn_in['bk'], 'L0_attn_wv': _L0_attn_in['wv'], 'L0_attn_bv': _L0_attn_in['bv'], 'L0_attn_wo': _L0_attn_in['wo'], 'L0_attn_bo': _L0_attn_in['bo'], 'L0_ffn_wqkv': _L0_ffn_in['wqkv'], 'L0_ffn_q_scale': _L0_ffn_in['q_scale'], 'L0_ffn_k_scale': _L0_ffn_in['k_scale'], 'L0_ffn_wo': _L0_ffn_in['wo'], 'L0_ffn_ln_g': _L0_ffn_in['ln_g'], 'L0_ffn_ln_b': _L0_ffn_in['ln_b'], 'L0_ffn_w1': _L0_ffn_in['w1'], 'L0_ffn_b1': _L0_ffn_in['b1'], 'L0_ffn_w2': _L0_ffn_in['w2'], 'L0_ffn_b2': _L0_ffn_in['b2']}
    _x0 = _d['L0_attn_x']
    _d['L0_attn_x'] = jax.random.normal(jax.random.fold_in(jax.random.key(seed), 1), (4, 1024, 256), dtype=_x0.dtype)
    del _x0
    return _d

def reference(L0_attn_x, L0_attn_wq, L0_attn_bq, L0_attn_wk, L0_attn_bk, L0_attn_wv, L0_attn_bv, L0_attn_wo, L0_attn_bo, L0_ffn_wqkv, L0_ffn_q_scale, L0_ffn_k_scale, L0_ffn_wo, L0_ffn_ln_g, L0_ffn_ln_b, L0_ffn_w1, L0_ffn_b1, L0_ffn_w2, L0_ffn_b2):

    def _L0_attn_ref(x, wq, bq, wk, bk, wv, bv, wo, bo):
        import jax, jax.numpy as jnp
        import numpy as np
        B, T, D, H = (4, 512, 256, 16)
        HD = D // H
        NEG = -np.finfo(np.float32).max
        b, t, d = x.shape

        def proj(w, bias):
            y = x @ w + bias
            return y.reshape(b, t, H, HD).transpose(0, 2, 1, 3)
        q = proj(wq, bq)
        k = proj(wk, bk)
        v = proj(wv, bv)
        scale = 1.0 / np.sqrt(HD).astype(np.float32)
        scores = jnp.einsum('bhqd,bhkd->bhqk', q, k) * scale
        mask = jnp.triu(jnp.full((t, t), NEG, jnp.float32), k=1)
        attn = jax.nn.softmax(scores + mask, axis=-1)
        out = jnp.einsum('bhqk,bhkd->bhqd', attn, v)
        out = out.transpose(0, 2, 1, 3).reshape(b, t, d)
        return out @ wo + bo

    def _L0_ffn_ref(x, wqkv, q_scale, k_scale, wo, ln_g, ln_b, w1, b1, w2, b2):
        import jax, jax.numpy as jnp
        import numpy as np
        DIM = 256
        DEPTH = 2
        HEADS = 8
        DIM_HEAD = 64
        WINDOW = 128
        INNER = HEADS * DIM_HEAD
        HID = int(DIM * 4 * 2 / 3)
        B, N = (2, 2048)
        QK_SCALE = 8.0

        def shift_token(t):
            t1, t2 = jnp.split(t, 2, axis=-1)
            t2 = jnp.pad(t2, ((0, 0), (1, 0), (0, 0)))[:, :-1]
            return jnp.concatenate([t1, t2], axis=-1)

        def l2norm(t):
            return t / jnp.clip(jnp.linalg.norm(t, axis=-1, keepdims=True), 1e-12)

        def rotate_half(x):
            x1, x2 = jnp.split(x, 2, axis=-1)
            return jnp.concatenate([-x2, x1], axis=-1)

        def rotary_xpos(q, k):
            n = q.shape[-2]
            half_idx = jnp.arange(0, DIM_HEAD, 2, dtype=jnp.float32)
            inv_freq = 1.0 / 10000.0 ** (half_idx / DIM_HEAD)
            t = jnp.arange(n, dtype=jnp.float32)
            freqs = t[:, None] * inv_freq[None, :]
            freqs = jnp.concatenate([freqs, freqs], axis=-1)
            base = (half_idx + 0.4 * DIM_HEAD) / (1.4 * DIM_HEAD)
            power = (t - n // 2) / float(WINDOW // 2)
            scale = base[None, :] ** power[:, None]
            scale = jnp.concatenate([scale, scale], axis=-1)
            cos, sin = (jnp.cos(freqs), jnp.sin(freqs))
            q = q * cos * scale + rotate_half(q) * sin * scale
            k = k * cos / scale + rotate_half(k) * sin / scale
            return (q, k)

        def local_attention(q, k, v):
            b, h, n, d = q.shape
            w = n // WINDOW
            bq = q.reshape(b, h, w, WINDOW, d) * QK_SCALE
            bk = k.reshape(b, h, w, WINDOW, d)
            bv = v.reshape(b, h, w, WINDOW, d)

            def look_around(t):
                p = jnp.pad(t, ((0, 0), (0, 0), (1, 0), (0, 0), (0, 0)))
                return jnp.concatenate([p[:, :, :w], p[:, :, 1:]], axis=3)
            bk, bv = (look_around(bk), look_around(bv))
            bt = jnp.arange(n).reshape(w, WINDOW)
            btp = jnp.pad(bt, ((1, 0), (0, 0)), constant_values=-1)
            btk = jnp.concatenate([btp[:w], btp[1:]], axis=1)
            sim = jnp.einsum('bhwid,bhwjd->bhwij', bq, bk)
            i = bt[:, :, None]
            j = btk[:, None, :]
            mask = (i < j) | (i > j + WINDOW) | (j == -1)
            sim = jnp.where(mask, -jnp.finfo(sim.dtype).max, sim)
            attn = jax.nn.softmax(sim, axis=-1)
            out = jnp.einsum('bhwij,bhwjd->bhwid', attn, bv)
            return out.reshape(b, h, n, d)

        def _layer(x, wqkv, qs, ksc, wo, lg, lb, w1, b1, w2, b2):
            b, n, _ = x.shape
            h = shift_token(x)
            qkv = h @ wqkv
            q, k, v = jnp.split(qkv, 3, axis=-1)
            to_heads = lambda t: t.reshape(b, n, HEADS, DIM_HEAD).transpose(0, 2, 1, 3)
            q, k, v = (to_heads(q), to_heads(k), to_heads(v))
            q = l2norm(q) * qs
            k = l2norm(k) * ksc
            q, k = rotary_xpos(q, k)
            o = local_attention(q, k, v)
            o = o.transpose(0, 2, 1, 3).reshape(b, n, INNER)
            x = x + o @ wo
            h = shift_token(x)
            mu = h.mean(-1, keepdims=True)
            var = h.var(-1, keepdims=True)
            h = (h - mu) / jnp.sqrt(var + 1e-05) * lg + lb
            h = h @ w1 + b1
            a, g = jnp.split(h, 2, axis=-1)
            h = a * jax.nn.gelu(g, approximate=False)
            x = x + h @ w2 + b2
            return x
        for l in range(DEPTH):
            x = _layer(x, wqkv[l], q_scale[l], k_scale[l], wo[l], ln_g[l], ln_b[l], w1[l], b1[l], w2[l], b2[l])
        return x
    x = L0_attn_x
    x = x + _L0_attn_ref(_layernorm(x, axis=-1), L0_attn_wq, L0_attn_bq, L0_attn_wk, L0_attn_bk, L0_attn_wv, L0_attn_bv, L0_attn_wo, L0_attn_bo)
    x = x + _L0_ffn_ref(_layernorm(x, axis=-1), L0_ffn_wqkv, L0_ffn_q_scale, L0_ffn_k_scale, L0_ffn_wo, L0_ffn_ln_g, L0_ffn_ln_b, L0_ffn_w1, L0_ffn_b1, L0_ffn_w2, L0_ffn_b2)
    return x

_drawn_inputs = setup_inputs


def setup_inputs(seed=0):
    import zlib

    import numpy as np

    out = dict(_drawn_inputs(seed))
    spreads = {'L0_ffn_q_scale': (1.0, 0.6),
     'L0_ffn_k_scale': (1.0, 0.6),
     'L0_ffn_ln_g': (1.0, 0.6),
     'L0_ffn_ln_b': (0.0, 0.8),
     'L0_ffn_b1': (0.0, 0.8),
     'L0_ffn_b2': (0.0, 0.1)}
    factors = {'L0_attn_bq': 8.0,
     'L0_attn_bk': 8.0,
     'L0_attn_bv': 2.699,
     'L0_attn_bo': 2.947,
     'L0_ffn_wqkv': 3.035,
     'L0_ffn_wo': 2.948}
    for name, (base, spread) in spreads.items():
        noise = np.random.default_rng([zlib.crc32(name.encode()), seed]).standard_normal(out[name].shape)
        drawn = base * np.exp(spread * noise) if base else spread * noise
        out[name] = jnp.asarray(drawn.astype(out[name].dtype))
    for name, factor in factors.items():
        out[name] = (out[name] * factor).astype(out[name].dtype)
    return out
```

```python
import concourse.bass as bass
import numpy as np
from concourse import mybir
from contextlib import ExitStack

F32 = mybir.dt.float32
BF16 = mybir.dt.bfloat16
ALU = mybir.AluOpType
ACT = mybir.ActivationFunctionType
AX = mybir.AxisListType

P = 128
B, T, D = 4, 1024, 256
KD = D // P
NT = T // P
CH = 512
NC = T // CH
TC = CH // P

H1, HD1 = 16, 16
HG = 4
NG = H1 // HG
GF = HG * HD1
VW = 32
TERMS = ((0, 0), (0, 1), (0, 2), (1, 0), (1, 1), (2, 0))
STK = len(TERMS) * HD1

DEPTH, H2, HD2, WIN = 2, 8, 64, 128
INNER = H2 * HD2
HID = int(D * 4 * 2 / 3)
QK_SCALE = 8.0
EPS = 1e-5
BIG = 3.0e38


class Count:

    def __init__(self, sem, per, credit=0):
        self.sem, self.per, self.credit = sem, per, credit

    def of(self, iteration, item):
        return iteration * self.per + (item + 1 + self.credit)


def wait_apart(eng, passed, sem, value):
    eng.wait_ge(sem, value)
    eng.sem_inc(passed, 1)


def prepare(nc, x_all, ident, neg_half, passed, a):
    with ExitStack() as ctx:
        sb = lambda name, shape, dt=F32: ctx.enter_context(nc.sbuf_tensor(name, shape, dt))
        ps = lambda name, shape: ctx.enter_context(nc.psum_tensor(name, shape, F32))
        sem = lambda name: ctx.enter_context(nc.semaphore(name))

        w_qk = sb("w_qk", [P, KD, 2 * D])
        w_v = sb("w_v", [P, KD, D])
        b_qk = sb("b_qk", [P, 2 * KD])
        b_v = sb("b_v", [P, D])
        stats = sb("stats", [P, NT, 6])
        mean_var = sb("mean_var", [P, NT, 2])
        var_eps = sb("var_eps", [P, NT])
        rstd = sb("rstd", [P, NT])
        xn = sb("xn", [P, 2, D])
        xn_t = sb("xn_t", [P, KD, T])
        full = sb("full", [P, 2, CH])
        rest = sb("rest", [P, 2, CH])
        parts = sb("parts", [P, 4, 3, CH], BF16)
        v_out = sb("v_out", [P, 2, H1, VW])
        turned = [ps(f"turned{i}", [P, CH]) for i in range(2)]
        v_ps = [ps(f"v_ps{i}", [P, CH]) for i in range(2)]
        qk_ps = [ps(f"qk_ps{i}", [P, CH]) for i in range(2)]

        weights_in = sem("weights_in")
        x_in = sem("x_in")
        scaled_bias = sem("scaled_bias")
        ones_set = sem("ones_set")
        counted = Count(sem("counted"), NT)
        averaged = Count(sem("averaged"), NT)
        var_ready = Count(sem("var_ready"), 1)
        rstd_ready = Count(sem("rstd_ready"), 1)
        xn_ready = Count(sem("xn_ready"), NT, 8)
        turned_ready = Count(sem("turned_ready"), NT, 2)
        xn_t_ready = Count(sem("xn_t_ready"), NT, 2)
        v_ready = Count(sem("v_ready"), NT, 8)
        v_copied = Count(sem("v_copied"), NT, 2)
        NI = NC * 2 * KD
        qk_ready = Count(sem("qk_ready"), NI, 8)
        full_ready = Count(sem("full_ready"), NI, 2)
        high_ready = Count(sem("high_ready"), NI, 2)
        rest_ready = Count(sem("rest_ready"), NI, 2)
        mid_ready = Count(sem("mid_ready"), NI, 2)
        low_ready = Count(sem("low_ready"), NI, 2)
        v_stored = [sem(f"v_stored{i}") for i in range(2)]
        parts_stored = [sem(f"parts_stored{i}") for i in range(4)]
        block = ctx.enter_context(nc.Block())

        @block.sync
        def _(sp):
            w_dma = [
                sp.dma_start(w_qk[:, :, 0:D], a["wq"].rearrange("(k p) n -> p k n", p=P)),
                sp.dma_start(w_qk[:, :, D:2 * D], a["wk"].rearrange("(k p) n -> p k n", p=P)),
                sp.dma_start(w_v[:, :, :], a["wv"].rearrange("(k p) n -> p k n", p=P)),
                sp.dma_start(b_qk[:, 0:KD], a["bq"].rearrange("(m p) -> p m", p=P), allow_slow_non_contiguous=True),
                sp.dma_start(b_qk[:, KD:2 * KD], a["bk"].rearrange("(m p) -> p m", p=P), allow_slow_non_contiguous=True),
                sp.dma_start(b_v[:, :], a["bv"].partition_broadcast(P)),
            ]
            for d in w_dma:
                d.then_inc(weights_in, 16)

            def load_x(b):
                if b >= 1:
                    sp.wait_ge(x_in, 16 * b)
                sp.dma_start(x_all[:, b * NT:(b + 1) * NT, :],
                             a["x"][b].rearrange("(t p) d -> p t d", p=P)).then_inc(x_in, 16)

            for s in v_stored:
                sp.sem_inc(s, 16)
            for s in parts_stored:
                sp.sem_inc(s, 32)
            load_x(0)
            load_x(1)
            for b in range(B):
                for t in range(NT):
                    sp.wait_ge(v_copied.sem, v_copied.of(b, t))
                    sp.dma_start(a["v_scratch"][b * NG:(b + 1) * NG, :, t, :].rearrange("g p n -> p g n"),
                                 v_out[:, t % 2].rearrange("p (g h) w -> p g (h w)", g=NG)).then_inc(v_stored[t % 2], 16)
                    if t % 4 == 3:
                        if t == 3 and b + 2 < B:
                            load_x(b + 2)
                        for m in range(2 * KD):
                            i = (t // 4) * 2 * KD + m
                            sp.wait_ge(low_ready.sem, low_ready.of(b, i))
                            c0 = (t // 4) * CH
                            for half in range(2):
                                g = b * NG + (m % KD) * 2 + half
                                sp.dma_start(a["qk_scratch"][m // KD, g, :, :, c0:c0 + CH].rearrange("s f t -> f s t"),
                                             parts[half * GF:(half + 1) * GF, i % 4]).then_inc(parts_stored[i % 4], 16)
            for s in v_stored:
                sp.wait_ge(s, 16 * (B * NT // 2 + 1))
            for s in parts_stored:
                sp.wait_ge(s, 32 * (B * NI // 4 + 1))

        @block.vector
        def _(dve):
            dve.sem_inc(xn_ready.sem, xn_ready.credit)
            dve.sem_inc(v_copied.sem, v_copied.credit)
            dve.sem_inc(high_ready.sem, high_ready.credit)
            dve.sem_inc(mid_ready.sem, mid_ready.credit)
            dve.memset(v_out[:, :, :, HD1:VW], 1.0).then_inc(ones_set, 1)
            dve.wait_ge(weights_in, 96)
            dve.tensor_scalar(b_qk[:, 0:KD], b_qk[:, 0:KD], HD1 ** -0.5, None, ALU.mult).then_inc(scaled_bias, 1)
            with dve.Fori(0, B) as b:
                dve.wait_ge(x_in, b * 16 + 16)
                for t in range(NT):
                    dve.bn_stats(stats[:, t, :], x_all[:, bass.ds(b * NT + t, 1), :]).then_inc(counted.sem, 1)
                wait_apart(dve, passed, counted.sem, counted.of(b, NT - 1))
                for t in range(NT):
                    dve.bn_aggr(mean_var[:, t, :], stats[:, t, :]).then_inc(averaged.sem, 1)
                dve.wait_ge(averaged.sem, averaged.of(b, NT - 1))
                dve.wait_ge(rstd_ready.sem, rstd_ready.of(b, 0))

                def normalise(t):
                    dve.wait_ge(turned_ready.sem, turned_ready.of(b, t - 2))
                    dve.tensor_scalar(xn[:, t % 2, :], x_all[:, bass.ds(b * NT + t, 1), :], mean_var[:, t, 0:1],
                                      rstd[:, t:t + 1], ALU.subtract, ALU.mult).then_inc(xn_ready.sem, 1)

                def copy_v(t):
                    dve.wait_ge(v_ready.sem, v_ready.of(b, t))
                    dve.wait_ge(v_stored[t % 2], b * (16 * NT // 2) + 16 * (t // 2 + 1))
                    dve.tensor_tensor(v_out[:, t % 2, :, 0:HD1], v_ps[t % 2][:, 0:D].rearrange("p (h d) -> p h d", h=H1),
                                      b_v[:, :].rearrange("p (h d) -> p h d", h=H1), ALU.add).then_inc(v_copied.sem, 1)

                def high(i):
                    dve.wait_ge(full_ready.sem, full_ready.of(b, i))
                    dve.wait_ge(parts_stored[i % 4], b * (32 * NI // 4) + 32 * (i // 4 + 1))
                    dve.tensor_copy(parts[:, i % 4, 0, :], full[:, i % 2, :]).then_inc(high_ready.sem, 1)

                def mid(i):
                    dve.wait_ge(rest_ready.sem, rest_ready.of(b, i))
                    dve.tensor_copy(parts[:, i % 4, 1, :], rest[:, i % 2, :]).then_inc(mid_ready.sem, 1)

                for t in range(6):
                    normalise(t)
                    if t >= 2:
                        copy_v(t - 2)
                for i in range(4):
                    high(i)
                    if i >= 1:
                        mid(i - 1)
                mid(3)
                for t in range(6, NT + 2):
                    if t < NT:
                        normalise(t)
                    copy_v(t - 2)
                for i in range(4, 8):
                    high(i)
                    if i >= 5:
                        mid(i - 1)
                mid(7)

        @block.gpsimd
        def _(pool):
            pool.sem_inc(rest_ready.sem, rest_ready.credit)
            pool.sem_inc(low_ready.sem, low_ready.credit)
            with pool.Fori(0, B) as b:
                pool.wait_ge(averaged.sem, averaged.of(b, NT - 1))
                wait_apart(pool, passed, xn_ready.sem, xn_ready.of(b, -1))
                pool.tensor_scalar(var_eps[:, :], mean_var[:, :, 1], EPS, None, ALU.add).then_inc(var_ready.sem, 1)
                pool.wait_ge(var_ready.sem, var_ready.of(b, 0))
                pool.tensor_tensor(rstd[:, :], var_eps[:, :], neg_half[:, 0:NT], ALU.pow).then_inc(rstd_ready.sem, 1)

                def low(i):
                    pool.wait_ge(mid_ready.sem, mid_ready.of(b, i))
                    pool.tensor_tensor(parts[:, i % 4, 2, :], rest[:, i % 2, :], parts[:, i % 4, 1, :],
                                       ALU.subtract).then_inc(low_ready.sem, 1)

                for i in range(NI):
                    pool.wait_ge(high_ready.sem, high_ready.of(b, i))
                    pool.wait_ge(low_ready.sem, low_ready.of(b, i - 2))
                    pool.tensor_tensor(rest[:, i % 2, :], full[:, i % 2, :], parts[:, i % 4, 0, :],
                                       ALU.subtract).then_inc(rest_ready.sem, 1)
                    if i % 4 >= 1:
                        low(i - 1)
                    if i % 4 == 3:
                        low(i)

        @block.scalar
        def _(act):
            act.sem_inc(xn_t_ready.sem, xn_t_ready.credit)
            act.sem_inc(full_ready.sem, full_ready.credit)
            act.wait_ge(scaled_bias, 1)
            with act.Fori(0, B) as b:
                def copy_turned(t):
                    act.wait_ge(turned_ready.sem, turned_ready.of(b, t))
                    act.wait_ge(qk_ready.sem, qk_ready.of(b, (t // TC + 1) * 2 * KD - 1 - NI))
                    act.copy(xn_t[:, :, t * P:(t + 1) * P],
                             turned[t % 2][:, 0:D].rearrange("p (k t) -> p k t", k=KD)).then_inc(xn_t_ready.sem, 1)

                def copy_qk(i):
                    m = i % (2 * KD)
                    act.wait_ge(qk_ready.sem, qk_ready.of(b, i))
                    act.wait_ge(rest_ready.sem, rest_ready.of(b, i - 2))
                    act.activation(full[:, i % 2, :], qk_ps[i % 2][:, :], ACT.Identity, bias=b_qk[:, m:m + 1],
                                   scale=HD1 ** -0.5 if m < KD else 1.0).then_inc(full_ready.sem, 1)

                for c in range(NC):
                    for t in range(c * TC, (c + 1) * TC):
                        copy_turned(t)
                    for i in range(c * 2 * KD, (c + 1) * 2 * KD):
                        copy_qk(i)

        @block.tensor
        def _(pe):
            pe.sem_inc(turned_ready.sem, turned_ready.credit)
            pe.sem_inc(v_ready.sem, v_ready.credit)
            pe.sem_inc(qk_ready.sem, qk_ready.credit)
            pe.wait_ge(weights_in, 96)
            with pe.Fori(0, B) as b:
                def turn(t):
                    pe.wait_ge(xn_ready.sem, xn_ready.of(b, t))
                    pe.wait_ge(xn_t_ready.sem, xn_t_ready.of(b, t - 2))
                    for k in range(KD):
                        mm = pe.transpose(turned[t % 2][:, k * P:(k + 1) * P], xn[:, t % 2, k * P:(k + 1) * P], ident[:, :])
                    mm.then_inc(turned_ready.sem, 1)

                def project_v(t):
                    pe.wait_ge(xn_t_ready.sem, xn_t_ready.of(b, t))
                    pe.wait_ge(v_copied.sem, v_copied.of(b, t - 2))
                    for k in range(KD):
                        mm = pe.matmul(v_ps[t % 2][:, 0:D], xn_t[:, k, t * P:(t + 1) * P], w_v[:, k, :],
                                       start=k == 0, stop=k == KD - 1)
                    mm.then_inc(v_ready.sem, 1)

                def project_qk(c, m):
                    i = c * 2 * KD + m
                    pe.wait_ge(full_ready.sem, full_ready.of(b, i - 2))
                    for k in range(KD):
                        mm = pe.matmul(qk_ps[i % 2][:, :], w_qk[:, k, m * P:(m + 1) * P], xn_t[:, k, c * CH:(c + 1) * CH],
                                       start=k == 0, stop=k == KD - 1)
                    mm.then_inc(qk_ready.sem, 1)

                for c in range(NC):
                    turn(c * TC)
                    for t in range(c * TC + 1, (c + 1) * TC):
                        turn(t)
                        project_v(t - 1)
                    project_v((c + 1) * TC - 1)
                    for m in range(2 * KD):
                        project_qk(c, m)


SETS = [(c, kt) for c in range(NC) for kt in range((c + 1) * TC)]
NS = len(SETS)
DIAGONAL = [n for n, (c, kt) in enumerate(SETS) if kt >= c * TC]


def first_query(c, kt):
    return max(0, kt - c * TC) * P


PIECES = [(qt, k0, min(CH, (qt + 1) * P - k0)) for qt in range(NT) for k0 in range(0, (qt + 1) * P, CH)]
NP = len(PIECES)
SHIFT = 2
SLOTS = 4
PIECES_AT = [5] * 8 + [4] * 2 + [0] * 2
SHIFT_AT = {4: 0, 6: 1, 9: 2, 11: 3}


def causal_attention(nc, ident, ident_b, causal_b, passed, a):
    with ExitStack() as ctx:
        sb = lambda name, shape, dt=F32: ctx.enter_context(nc.sbuf_tensor(name, shape, dt))
        ps = lambda name: ctx.enter_context(nc.psum_tensor(name, [P, CH], F32))
        sem = lambda name: ctx.enter_context(nc.semaphore(name))

        q_stack = sb("q_stack", [P, SLOTS, HG, T], BF16)
        k_stack = sb("k_stack", [P, SLOTS, HG, T], BF16)
        v_sb = sb("v_sb", [P, SLOTS, NT, HG * VW])
        probs = sb("probs", [P, 2, HG, CH])
        piece_negmax = sb("piece_negmax", [P, HG, NP])
        negmax = sb("negmax", [P, HG, NT])
        negmax_parts = sb("negmax_parts", [P, HG, NT, SHIFT], BF16)
        o_sb = sb("o_sb", [P, NC, CH])
        inv_sum = sb("inv_sum", [P, NC, TC, HG])
        att = sb("att", [P, NC, TC, HG, HD1])
        st_ps = [ps(f"st_ps{i}") for i in range(3)]
        s_ps = [ps(f"s_ps{i}") for i in range(2)]
        o_ps, ot_ps, shift_ps = ps("o_ps"), ps("ot_ps"), ps("shift_ps")

        def count(name, items, credit=0):
            return Count(sem(name), SLOTS * items, credit)

        st_ready = count("st_ready", NS * HG)
        exp_done = count("exp_done", NS * HG, 8)
        masked = count("masked", len(DIAGONAL))
        pv_done = count("pv_done", NS, 2)
        s_ready = count("s_ready", NP * HG)
        piece_done = count("piece_done", NP * HG, 2)
        joined = count("joined", 2 * HG)
        parts_done = count("parts_done", 2 * HG)
        shift_ready = count("shift_ready", HG * NC, HG * NC)
        shift_done = count("shift_done", HG * NC, 1)
        o_copied = count("o_copied", NC, 1)
        ot_ready = count("ot_ready", NC)
        summed = count("summed", NC)
        att_ready = count("att_ready", NC, 1)
        att_stored = [sem(f"att_stored{c}") for c in range(NC)]
        stack_in = [sem(f"stack_in{s}") for s in range(SLOTS)]
        shift_ones = sem("shift_ones")
        LOAD = 16 * (2 * len(TERMS) + 1)
        block = ctx.enter_context(nc.Block())

        def groups(eng, group, first):
            first((0, 0))
            group((0, 0), None, (0, 1))
            with eng.Fori(0, B - 1) as r:
                for s in range(1, SLOTS + 1):
                    at = lambda s: (r + s // SLOTS, s % SLOTS)
                    group(at(s), at(s - 1), at(s + 1))
            for s in range(1, SLOTS):
                group((B - 1, s), (B - 1, s - 1), (B - 1, s + 1) if s + 1 < SLOTS else None)

        def when(count, group, items, i):
            return count.of(group[0], group[1] * items + i)

        @block.sync
        def _(sp):
            for c in range(NC):
                sp.sem_inc(att_stored[c], 16)

            def load(g):
                slot = g % SLOTS
                if g >= SLOTS:
                    sp.wait_ge(pv_done.sem, when(pv_done, (g // SLOTS - 1, slot), NS, NS - 1))
                for r, (qp, kp) in enumerate(TERMS):
                    for stack, which, part in ((q_stack, 0, qp), (k_stack, 1, kp)):
                        sp.dma_start(stack[r * HD1:(r + 1) * HD1, slot, :, :],
                                     a["qk_scratch"][which, g, part].rearrange("(h d) t -> d h t", d=HD1))\
                            .then_inc(stack_in[slot], 16)
                sp.dma_start(v_sb[:, slot], a["v_scratch"][g]).then_inc(stack_in[slot], 16)

            def store(g, c):
                sp.wait_ge(att_ready.sem, when(att_ready, (g // SLOTS, g % SLOTS), NC, c))
                sp.dma_start(a["att_scratch"][g, c * CH:(c + 1) * CH, :].rearrange("(t p) n -> p t n", p=P),
                             att[:, c].rearrange("p t h d -> p t (h d)")).then_inc(att_stored[c], 16)

            for g in range(SLOTS):
                load(g)
            for g in range(B * NG):
                store(g, 0)
                if g + SLOTS < B * NG:
                    load(g + SLOTS)
                store(g, 1)
            for c in range(NC):
                sp.wait_ge(att_stored[c], 16 * (B * NG + 1))

        @block.tensor
        def _(pe):
            for c in (pv_done, shift_ready):
                pe.sem_inc(c.sem, c.credit)
            pe.wait_ge(shift_ones, 1)

            def loaded(group):
                pe.wait_ge(stack_in[group[1]], group[0] * LOAD + LOAD)

            def score_pieces(group, items):
                r, slot = group
                for i in items:
                    h, (qt, k0, kw) = i // NP, PIECES[i % NP]
                    pe.wait_ge(piece_done.sem, when(piece_done, group, NP * HG, i - 2))
                    last = k0 + kw == (qt + 1) * P
                    mm = pe.matmul(s_ps[i % 2][:, 0:kw], q_stack[0:STK, slot, h, qt * P:(qt + 1) * P],
                                   k_stack[0:STK, slot, h, k0:k0 + kw], start=True, stop=not last)
                    if last:
                        mm = pe.matmul(s_ps[i % 2][:, kw - P:kw], ident_b[:, :], causal_b[:, :], start=False, stop=True)
                    mm.then_inc(s_ready.sem, 1)

            def shift_rows(group, h, c):
                pe.wait_ge(parts_done.sem, when(parts_done, group, 2 * HG, 2 * h + 1))
                pe.wait_ge(shift_done.sem, when(shift_done, group, HG * NC, h * NC + c - 1))
                for j in range(TC):
                    mm = pe.matmul(shift_ps[STK:STK + SHIFT, j * P:(j + 1) * P], negmax_parts[:, h, c * TC + j, :],
                                   ident_b[:, :], start=True, stop=True, tile_position=(0, STK))
                mm.then_inc(shift_ready.sem, 1)

            def shifted_scores(group, n):
                r, slot = group
                c, kt = SETS[n]
                q0 = first_query(c, kt)
                for h in range(HG):
                    i = n * HG + h
                    pe.wait_ge(exp_done.sem, when(exp_done, group, NS * HG, i - 3))
                    pe.wait_ge(shift_done.sem, when(shift_done, group, HG * NC, h * NC + c))
                    pe.matmul(st_ps[i % 3][:, q0:CH], k_stack[0:STK + SHIFT, slot, h, kt * P:(kt + 1) * P],
                              q_stack[0:STK + SHIFT, slot, h, c * CH + q0:(c + 1) * CH],
                              start=True, stop=True).then_inc(st_ready.sem, 1)

            def add_values(group, n):
                r, slot = group
                c, kt = SETS[n]
                q0 = first_query(c, kt)
                pe.wait_ge(exp_done.sem, when(exp_done, group, NS * HG, n * HG + HG - 1))
                if n in DIAGONAL:
                    pe.wait_ge(masked.sem, when(masked, group, len(DIAGONAL), DIAGONAL.index(n)))
                if kt == 0:
                    pe.wait_ge(o_copied.sem, when(o_copied, group, NC, c - 1))
                for h in range(HG):
                    mm = pe.matmul(o_ps[h * VW:(h + 1) * VW, q0:CH], v_sb[:, slot, kt, h * VW:(h + 1) * VW],
                                   probs[:, n % 2, h, q0:CH], start=kt == 0, stop=kt == (c + 1) * TC - 1,
                                   tile_position=(0, h * VW))
                mm.then_inc(pv_done.sem, 1)

            def turn_output(group, c):
                pe.wait_ge(o_copied.sem, when(o_copied, group, NC, c))
                pe.wait_ge(att_ready.sem, when(att_ready, group, NC, c - 1))
                for j in range(TC):
                    mm = pe.transpose(ot_ps[:, j * P:(j + 1) * P], o_sb[:, c, j * P:(j + 1) * P], ident[:, :])
                mm.then_inc(ot_ready.sem, 1)

            def first(group):
                loaded(group)
                score_pieces(group, range(NP * HG))
                for h in range(HG):
                    for c in range(NC):
                        shift_rows(group, h, c)

            def group_work(group, previous, following):
                if following:
                    loaded(following)
                i = 0
                for n in range(NS):
                    shifted_scores(group, n)
                    if following:
                        if n in SHIFT_AT:
                            shift_rows(following, SHIFT_AT[n], 0)
                        score_pieces(following, range(i, i + PIECES_AT[n]))
                        i += PIECES_AT[n]
                    if n >= 1:
                        add_values(group, n - 1)
                    elif previous:
                        add_values(previous, NS - 1)
                    if n == 2 and previous:
                        turn_output(previous, 1)
                    if n == 7:
                        turn_output(group, 0)
                    if following and n in SHIFT_AT:
                        shift_rows(following, SHIFT_AT[n], 1)
                if not following:
                    add_values(group, NS - 1)
                    turn_output(group, 1)

            groups(pe, group_work, first)

        @block.scalar
        def _(act):
            for c in (exp_done, shift_done, o_copied):
                act.sem_inc(c.sem, c.credit)

            def copy_shift(group, h, c):
                act.wait_ge(shift_ready.sem, when(shift_ready, group, HG * NC, h * NC + c))
                act.copy(q_stack[STK:STK + SHIFT, group[1], h, c * CH:(c + 1) * CH],
                         shift_ps[STK:STK + SHIFT, :]).then_inc(shift_done.sem, 1)

            def exponentials(group, n):
                c, kt = SETS[n]
                q0 = first_query(c, kt)
                act.wait_ge(pv_done.sem, when(pv_done, group, NS, n - 2))
                for h in range(HG):
                    i = n * HG + h
                    act.wait_ge(st_ready.sem, when(st_ready, group, NS * HG, i))
                    act.activation(probs[:, n % 2, h, q0:CH], st_ps[i % 3][:, q0:CH], ACT.Exp).then_inc(exp_done.sem, 1)

            def copy_output(group, c):
                act.wait_ge(pv_done.sem, when(pv_done, group, NS, (NS if c else TC) - 1))
                act.copy(o_sb[:, c, :], o_ps[:, :]).then_inc(o_copied.sem, 1)

            def first(group):
                for h in range(HG):
                    for c in range(NC):
                        copy_shift(group, h, c)

            def group_work(group, previous, following):
                for n in range(NS):
                    if n == 1 and previous:
                        copy_output(previous, 1)
                    if n == 5:
                        copy_output(group, 0)
                    exponentials(group, n)
                    if following and n in SHIFT_AT:
                        copy_shift(following, SHIFT_AT[n], 0)
                        copy_shift(following, SHIFT_AT[n], 1)
                if not following:
                    copy_output(group, 1)

            groups(act, group_work, first)

        @block.vector
        def _(dve):
            for c in (piece_done, att_ready):
                dve.sem_inc(c.sem, c.credit)

            def reduce_pieces(group, items):
                for i in items:
                    h, (qt, k0, kw) = i // NP, PIECES[i % NP]
                    dve.wait_ge(s_ready.sem, when(s_ready, group, NP * HG, i))
                    dve.tensor_reduce(piece_negmax[:, h, i % NP:i % NP + 1], s_ps[i % 2][:, 0:kw], AX.X, ALU.max,
                                      negate=True).then_inc(piece_done.sem, 1)
                    if i % NP == NP - 1:
                        join(group, h)

            def join(group, h):
                dve.wait_ge(piece_done.sem, when(piece_done, group, NP * HG, (h + 1) * NP - 1))
                dve.tensor_copy(negmax[:, h, 0:TC], piece_negmax[:, h, 0:TC]).then_inc(joined.sem, 1)
                dve.tensor_tensor(negmax[:, h, TC:NT], piece_negmax[:, h, TC:NP:2], piece_negmax[:, h, TC + 1:NP:2],
                                  ALU.min).then_inc(joined.sem, 1)
                dve.wait_ge(joined.sem, when(joined, group, 2 * HG, 2 * h + 1))
                dve.wait_ge(shift_ready.sem, when(shift_ready, group, HG * NC, h * NC + NC - 1 - HG * NC))
                dve.tensor_copy(negmax_parts[:, h, :, 0], negmax[:, h, :]).then_inc(parts_done.sem, 1)
                dve.wait_ge(parts_done.sem, when(parts_done, group, 2 * HG, 2 * h))
                dve.tensor_tensor(negmax_parts[:, h, :, 1], negmax[:, h, :], negmax_parts[:, h, :, 0],
                                  ALU.subtract).then_inc(parts_done.sem, 1)

            def normalise(group, c):
                ot = ot_ps[:, :].rearrange("p (t h w) -> p t h w", t=TC, h=HG)
                dve.wait_ge(ot_ready.sem, when(ot_ready, group, NC, c))
                dve.reciprocal(inv_sum[:, c], ot[:, :, :, HD1]).then_inc(summed.sem, 1)
                dve.wait_ge(summed.sem, when(summed, group, NC, c))
                dve.wait_ge(att_stored[c], (group[0] * SLOTS + group[1]) * 16 + 16)
                dve.tensor_tensor(att[:, c], ot[:, :, :, 0:HD1],
                                  inv_sum[:, c].unsqueeze(3).to_broadcast([P, TC, HG, HD1]),
                                  ALU.mult).then_inc(att_ready.sem, 1)

            def first(group):
                reduce_pieces(group, range(NP * HG))

            def group_work(group, previous, following):
                i = 0
                for n in range(NS):
                    if following:
                        reduce_pieces(following, range(i, i + PIECES_AT[n]))
                        i += PIECES_AT[n]
                    if n == 2 and previous:
                        normalise(previous, 1)
                    if n == 7:
                        normalise(group, 0)
                if not following:
                    normalise(group, 1)

            groups(dve, group_work, first)

        @block.gpsimd
        def _(pool):
            pool.memset(k_stack[STK:STK + SHIFT, :, :, :], 1.0).then_inc(shift_ones, 1)

            def group_work(group, previous, following):
                for n in DIAGONAL:
                    q0 = first_query(*SETS[n])
                    wait_apart(pool, passed, exp_done.sem, when(exp_done, group, NS * HG, n * HG + HG - 1))
                    diagonal = probs[:, n % 2, :, q0:q0 + P]
                    pool.affine_select(out=diagonal, in_=diagonal, compare_op=ALU.is_ge, fill=0.0, base=0,
                                       pattern=[[0, HG], [1, P]], channel_multiplier=-1).then_inc(masked.sem, 1)

            groups(pool, group_work, lambda group: None)


def project_causal(nc, x_all, ident, neg_half, passed, a):
    with ExitStack() as ctx:
        sb = lambda name, shape, dt=F32: ctx.enter_context(nc.sbuf_tensor(name, shape, dt))
        ps = lambda name: ctx.enter_context(nc.psum_tensor(name, [P, CH], F32))
        sem = lambda name: ctx.enter_context(nc.semaphore(name))
        count = lambda name, credit=0, per=NT: Count(sem(name), per, credit)

        w_o = sb("w_o", [P, KD, D])
        b_o = sb("b_o", [P, D])
        att = sb("att_in", [P, 4, NG, GF])
        att_t = sb("att_t", [P, 2, KD, P])
        x_bias = sb("x_bias", [P, 2, D])
        x1 = sb("x1", [P, 4, D])
        stats = sb("stats1", [P, 2, 6])
        mean_var = sb("mean_var1", [P, 4, 2])
        var_eps = sb("var_eps1", [P, 2])
        rstd = sb("rstd1", [P, 4])
        xn = sb("xn1", [P, 2, D])
        xn_t = sb("xn1_t", [P, NC, KD, CH])
        at_ps = [ps(f"at_ps{i}") for i in range(2)]
        y_ps = [ps(f"y_ps{i}") for i in range(2)]
        xt_ps = [ps(f"xt_ps{i}") for i in range(2)]

        weights_in = sem("w_o_in")
        att_in = [sem(f"att_in{i}") for i in range(4)]
        at_ready = count("at_ready", 4)
        att_t_ready = count("att_t_ready", 2)
        y_ready = count("y_ready", 2)
        x_bias_ready = count("x_bias_ready")
        x1_ready = count("x1_ready", 2)
        counted = count("counted1")
        averaged = count("averaged1")
        var_ready = count("var_ready1")
        rstd_ready = count("rstd_ready1")
        xn_ready = count("xn1_ready", 4)
        xt_ready = count("xt_ready", 2)
        xt_copied = count("xt_copied", 2)
        x1_stored = [sem(f"x1_stored{i}") for i in range(4)]
        xt_stored = [sem(f"xt_stored{i}") for i in range(NC)]
        block = ctx.enter_context(nc.Block())

        @block.sync
        def _(sp):
            sp.dma_start(w_o[:, :, :], a["wo"].rearrange("(k p) n -> p k n", p=P)).then_inc(weights_in, 16)
            sp.dma_start(b_o[:, :], a["bo"].partition_broadcast(P)).then_inc(weights_in, 16)
            for s in x1_stored + xt_stored:
                sp.sem_inc(s, 16)

            def load(i):
                b, t = i // NT, i % NT
                sp.wait_ge(at_ready.sem, at_ready.of(b, t - 4))
                sp.dma_start(att[:, t % 4], a["att_scratch"][b * NG:(b + 1) * NG, t * P:(t + 1) * P, :]
                             .rearrange("g p n -> p g n")).then_inc(att_in[t % 4], 16)

            for i in range(4):
                load(i)
            for i in range(B * NT):
                b, t = i // NT, i % NT
                sp.wait_ge(x1_ready.sem, x1_ready.of(b, t))
                sp.dma_start(a["x1_scratch"][b, t * P:(t + 1) * P, :], x1[:, t % 4]).then_inc(x1_stored[t % 4], 16)
                if i + 4 < B * NT:
                    load(i + 4)
                if t % TC == TC - 1:
                    c = t // TC
                    sp.wait_ge(xt_copied.sem, xt_copied.of(b, t))
                    sp.dma_start(a["xt_scratch"][b, :, :, c * CH:(c + 1) * CH].rearrange("k p t -> p k t"),
                                 xn_t[:, c]).then_inc(xt_stored[c], 16)
            for s in x1_stored:
                sp.wait_ge(s, 16 * (B * NT // 4 + 1))
            for s in xt_stored:
                sp.wait_ge(s, 16 * (B + 1))

        @block.tensor
        def _(pe):
            for c in (at_ready, y_ready, xt_ready):
                pe.sem_inc(c.sem, c.credit)
            pe.wait_ge(weights_in, 32)
            with pe.Fori(0, B) as b:
                def turn_att(t):
                    pe.wait_ge(att_in[t % 4], b * (16 * NT // 4) + 16 * (t // 4 + 1))
                    pe.wait_ge(att_t_ready.sem, att_t_ready.of(b, t - 2))
                    for k in range(KD):
                        mm = pe.transpose(at_ps[t % 2][:, k * P:(k + 1) * P], att[:, t % 4, 2 * k:2 * k + 2, :], ident[:, :])
                    mm.then_inc(at_ready.sem, 1)

                def project(t):
                    pe.wait_ge(att_t_ready.sem, att_t_ready.of(b, t))
                    pe.wait_ge(x1_ready.sem, x1_ready.of(b, t - 2))
                    for k in range(KD):
                        mm = pe.matmul(y_ps[t % 2][:, 0:D], att_t[:, t % 2, k, :], w_o[:, k, :],
                                       start=k == 0, stop=k == KD - 1)
                    mm.then_inc(y_ready.sem, 1)

                def turn_x(t):
                    pe.wait_ge(xn_ready.sem, xn_ready.of(b, t))
                    pe.wait_ge(xt_copied.sem, xt_copied.of(b, t - 2))
                    for k in range(KD):
                        mm = pe.transpose(xt_ps[t % 2][:, k * P:(k + 1) * P], xn[:, t % 2, k * P:(k + 1) * P], ident[:, :])
                    mm.then_inc(xt_ready.sem, 1)

                for s in range(NT + 3):
                    if s < NT:
                        turn_att(s)
                    if 1 <= s <= NT:
                        project(s - 1)
                    if s >= 3:
                        turn_x(s - 3)

        @block.scalar
        def _(act):
            for c in (att_t_ready, xt_copied):
                act.sem_inc(c.sem, c.credit)
            with act.Fori(0, B) as b:
                for s in range(NT + 3):
                    if s < NT:
                        act.wait_ge(at_ready.sem, at_ready.of(b, s))
                        act.wait_ge(y_ready.sem, y_ready.of(b, s - 2))
                        act.copy(att_t[:, s % 2], at_ps[s % 2][:, 0:D].rearrange("p (k t) -> p k t", k=KD))\
                           .then_inc(att_t_ready.sem, 1)
                    if s >= 3:
                        t = s - 3
                        c = t // TC
                        act.wait_ge(xt_ready.sem, xt_ready.of(b, t))
                        act.wait_ge(xt_stored[c], b * 16 + 16)
                        act.copy(xn_t[:, c, :, (t % TC) * P:(t % TC + 1) * P],
                                 xt_ps[t % 2][:, 0:D].rearrange("p (k t) -> p k t", k=KD)).then_inc(xt_copied.sem, 1)

        @block.gpsimd
        def _(pool):
            pool.wait_ge(weights_in, 32)
            with pool.Fori(0, B) as b:
                for s in range(NT + 1):
                    if s < NT:
                        pool.wait_ge(x1_ready.sem, x1_ready.of(b, s - 2))
                        pool.tensor_tensor(x_bias[:, s % 2, :].unsqueeze(1), x_all[:, bass.ds(b * NT + s, 1), :],
                                           b_o[:, :].unsqueeze(1), ALU.add).then_inc(x_bias_ready.sem, 1)
                    if s >= 1:
                        t = s - 1
                        wait_apart(pool, passed, averaged.sem, averaged.of(b, t))
                        pool.tensor_scalar(var_eps[:, t % 2:t % 2 + 1], mean_var[:, t % 4, 1:2], EPS, None, ALU.add)\
                            .then_inc(var_ready.sem, 1)
                        pool.wait_ge(xn_ready.sem, xn_ready.of(b, t - 4))
                        pool.wait_ge(var_ready.sem, var_ready.of(b, t))
                        pool.tensor_tensor(rstd[:, t % 4:t % 4 + 1], var_eps[:, t % 2:t % 2 + 1], neg_half[:, 0:1],
                                           ALU.pow).then_inc(rstd_ready.sem, 1)

        @block.vector
        def _(dve):
            for c in (x1_ready, xn_ready):
                dve.sem_inc(c.sem, c.credit)
            with dve.Fori(0, B) as b:
                def residual(t):
                    dve.wait_ge(x_bias_ready.sem, x_bias_ready.of(b, t))
                    dve.wait_ge(y_ready.sem, y_ready.of(b, t))
                    dve.wait_ge(x1_stored[t % 4], b * (16 * NT // 4) + 16 * (t // 4 + 1))
                    dve.tensor_tensor(x1[:, t % 4, :], y_ps[t % 2][:, 0:D], x_bias[:, t % 2, :], ALU.add)\
                       .then_inc(x1_ready.sem, 1)
                    dve.wait_ge(x1_ready.sem, x1_ready.of(b, t))
                    dve.bn_stats(stats[:, t % 2, :], x1[:, t % 4, :]).then_inc(counted.sem, 1)
                    wait_apart(dve, passed, counted.sem, counted.of(b, t))
                    dve.bn_aggr(mean_var[:, t % 4, :], stats[:, t % 2, :]).then_inc(averaged.sem, 1)

                def normalise(t):
                    dve.wait_ge(rstd_ready.sem, rstd_ready.of(b, t))
                    dve.wait_ge(xt_ready.sem, xt_ready.of(b, t - 2))
                    dve.tensor_scalar(xn[:, t % 2, :], x1[:, t % 4, :], mean_var[:, t % 4, 0:1], rstd[:, t % 4:t % 4 + 1],
                                      ALU.subtract, ALU.mult).then_inc(xn_ready.sem, 1)

                for s in range(NT + 1):
                    if s < NT:
                        residual(s)
                    if s >= 1:
                        normalise(s - 1)


WPC = CH // WIN
PAIRS = H2 // 2
PW = 2 * WIN
UNITS = NT * PAIRS
HT = -(-HID // P)
HL = HID - (HT - 1) * P


def place(u, h):
    q = u % PAIRS
    return q // 2 * 2 + h, q % 2


def layers(nc, ident, neg_half, passed, a):
    with ExitStack() as ctx:
        sb = lambda name, shape, dt=F32: ctx.enter_context(nc.sbuf_tensor(name, shape, dt))
        sem = lambda name: ctx.enter_context(nc.semaphore(name))
        count = lambda name, per, credit=0: Count(sem(name), per, credit)
        bank = [ctx.enter_context(nc.psum_tensor(f"bank{i}", [P, CH], F32)) for i in range(3, 8)]
        qkv_ps = ctx.enter_context(nc.psum_tensor("qkv_ps", [P, 3 * CH], F32))
        q_ps, v_ps = qkv_ps[:, 0:2 * CH], qkv_ps[:, 2 * CH:3 * CH]
        turn_ps, s_ps, pt_ps, o_ps = bank[0], bank[1:3], bank[3], bank[4]
        wo_ps = [[qkv_ps[:, 0:CH], qkv_ps[:, CH:2 * CH]], [v_ps, bank[0][:, :]]]
        ln_ps, back_ps = bank[1:3], bank[3:5]
        up_ps = wo_ps
        down_ps = bank[1:3]

        w_qkv = sb("w_qkv", [P, KD, 3 * INNER])
        w_out = sb("w_out", [P, INNER // P, D])
        w_up = sb("w_up", [P, KD, 2 * HID])
        w_down = sb("w_down", [P, HT, D])
        b_up = sb("b_up", [P, 2, HT])
        b_down = sb("b_down", [P, KD])
        ln_g = sb("ln_g", [P, KD])
        ln_b = sb("ln_b", [P, KD])
        head_scale = sb("head_scale", [P, 4, HD2])
        rotary = sb("rotary", [P, NT, 4, HD2])
        band = sb("band", [P, PW])
        x_in = sb("x_in", [P, KD, T + 1])
        x_mid = sb("x_mid", [P, KD, T + 1])
        squares = sb("squares", [P, 2 * INNER])
        inv_norm = sb("inv_norm", [P, 2, 2 * H2])
        sum_sq = sb("sum_sq", [P, 2, 2 * H2])
        qn = sb("qn", [P, 2 * INNER])
        rot_c = sb("rot_c", [P, 2 * INNER])
        rot_s = sb("rot_s", [P, 2 * INNER])
        q_t = sb("q_t", [P, 2, PAIRS, P])
        k_t = sb("k_t", [P, PAIRS, T])
        v_sb = sb("v_tok", [P, NT, INNER])
        p_sb = sb("p_sb", [P, 4, 2, PW])
        negmax = sb("negmax2", [P, 4, 2])
        total = sb("total", [P, 4, 2])
        inv_total = sb("inv_total", [P, 4, 2])
        p_t = sb("p_t", [P, 2, 2, 2, P])
        o_t = sb("o_t", [P, PAIRS, T])
        stats = sb("stats2", [P, TC, 6])
        mean_var = sb("mean_var2", [P, TC, 2])
        var_eps = sb("var_eps2", [P, TC])
        rstd = sb("rstd2", [P, TC])
        hn = sb("hn", [P, TC, D])
        hn_t = sb("hn_t", [P, KD, CH])
        gate = sb("gate", [P, 2, CH])
        hidden = sb("hidden", [P, HT, CH])
        x_out = sb("x_out", [P, KD, CH])

        weights_in = sem("weights_in2")
        x_loaded = sem("x_loaded")
        pads = sem("pads")
        rotary_ready = sem("rotary_ready")
        q_ready = count("q_ready", NT)
        v_ready = count("v_ready2", NT, 1)
        squared = count("squared", NT, 1)
        v_copied = count("v_copied2", NT, 1)
        summed = count("summed2", NT)
        clamped = count("clamped", NT)
        inv_ready = count("inv_ready", NT)
        qn_ready = count("qn_ready", NT, 1)
        cos_ready = count("cos_ready", NT, 1)
        sin_ready = count("sin_ready", 4 * NT)
        rot_ready = count("rot_ready", NT, 2)
        turned = count("turned2", 2 * NT, 4)
        turn_copied = count("turn_copied", 2 * NT, 1)
        s_ready = count("s_ready2", UNITS, 8)
        s_masked = count("s_masked", 2 * UNITS, 4)
        exp_done = count("exp_done2", 2 * UNITS)
        inv_sum = count("inv_sum", UNITS)
        scaled = count("scaled", 2 * UNITS)
        pt_ready = count("pt_ready", UNITS, 4)
        pt_copied = count("pt_copied", UNITS, 1)
        pv_done = count("pv_done2", UNITS, 2)
        o_copied = count("o_copied2", NT, 1)
        wo_ready = count("wo_ready", NC * KD, 4)
        mid_ready = count("mid_ready2", NC * KD, 4)
        ln_ready = count("ln_ready", NC * 2)
        counted = count("counted2", NC * TC)
        averaged = count("averaged2", NC * TC)
        var_ready = count("var_ready2", NC)
        rstd_ready = count("rstd_ready2", NC)
        hn_ready = count("hn_ready", NC * TC, TC)
        back_ready = count("back_ready", NC * KD, 2)
        hn_t_ready = count("hn_t_ready", NC * KD, 2)
        up_ready = count("up_ready", NC * HT, 2)
        gelu_done = count("gelu_done", NC * HT, 2)
        hidden_ready = count("hidden_ready", NC * HT, 2)
        down_ready = count("down_ready", NC * KD, 4)
        out_ready = count("out_ready", NC * KD, 4)
        out_stored = [sem(f"out_stored{k}") for k in range(KD)]
        N_WEIGHT_DMAS = 19
        block = ctx.enter_context(nc.Block())

        @block.sync
        def _(sp):
            def small(dst, src):
                sp.dma_start(dst, src, allow_slow_non_contiguous=True).then_inc(weights_in, 16)

            def load_weights(l):
                if l:
                    sp.wait_ge(out_ready.sem, out_ready.of(l * B - 1, NC * KD - 1))
                big = lambda dst, src: sp.dma_start(dst, src).then_inc(weights_in, 16)
                big(w_qkv[:, :, :], a["wqkv"][l].rearrange("(k p) n -> p k n", p=P))
                big(rotary[:, :, :, :].rearrange("p t j d -> p t (j d)"),
                    a["rotary"].rearrange("(t p) j d -> p t (j d)", p=P))
                half = HD2 // 2
                for j, name in ((0, "q_scale"), (2, "k_scale")):
                    big(head_scale[:, j, :], a[name][l].partition_broadcast(P))
                    big(head_scale[:, j + 1, 0:half], a[name][l, half:HD2].partition_broadcast(P))
                    big(head_scale[:, j + 1, half:HD2], a[name][l, 0:half].partition_broadcast(P))
                big(w_out[:, :, :], a["wo2"][l].rearrange("(k p) n -> p k n", p=P))
                big(w_up[:, :, :], a["w1"][l].rearrange("(k p) n -> p k n", p=P))
                big(w_down[:, 0:HT - 1, :], a["w2"][l, 0:(HT - 1) * P, :].rearrange("(k p) n -> p k n", p=P))
                big(w_down[0:HL, HT - 1, :], a["w2"][l, (HT - 1) * P:HID, :])
                for j in range(2):
                    full = a["b1"][l, j * HID:j * HID + (HT - 1) * P]
                    small(b_up[:, j, 0:HT - 1], full.rearrange("(k p) -> p k", p=P))
                    small(b_up[0:HL, j, HT - 1:HT], a["b1"][l, j * HID + (HT - 1) * P:(j + 1) * HID].rearrange("(p k) -> p k", k=1))
                small(b_down[:, :], a["b2"][l].rearrange("(k p) -> p k", p=P))
                small(ln_g[:, :], a["ln_g"][l].rearrange("(k p) -> p k", p=P))
                small(ln_b[:, :], a["ln_b"][l].rearrange("(k p) -> p k", p=P))

            def load_x(it):
                b = it % B
                if it:
                    sp.wait_ge(mid_ready.sem, mid_ready.of(it - 1, NC * KD - 1))
                if it >= B:
                    for s in out_stored:
                        sp.wait_ge(s, 16 * (NC * (it - B + 1) + 1))
                for k in range(KD):
                    sp.dma_start(x_in[:, k, k:k + T], a["xt_scratch"][b, k]).then_inc(x_loaded, 16)

            for s in out_stored:
                sp.sem_inc(s, 16)
            for it in range(DEPTH * B):
                if it % B == 0:
                    load_weights(it // B)
                if it == 0:
                    load_x(0)
                if it + 1 < DEPTH * B:
                    load_x(it + 1)
                for c in range(NC):
                    for k in range(KD):
                        sp.wait_ge(out_ready.sem, out_ready.of(it, c * KD + k))
                        sp.dma_start(a["xt_scratch"][it % B, k, :, c * CH:(c + 1) * CH], x_out[:, k, :])\
                            .then_inc(out_stored[k], 16)
            for s in out_stored:
                sp.wait_ge(s, 16 * (NC * DEPTH * B + 1))

        @block.tensor
        def _(pe):
            for c in (v_ready, turned, s_ready, pt_ready, pv_done, wo_ready, back_ready, up_ready, down_ready):
                pe.sem_inc(c.sem, c.credit)
            pe.wait_ge(pads, 3)

            def batch(l, it):
                def project(w):
                    if w == 0:
                        pe.wait_ge(hidden_ready.sem, hidden_ready.of(it, -1))
                    pe.wait_ge(qn_ready.sem, qn_ready.of(it, w - 1))
                    for j in range(3):
                        if j == 2:
                            pe.wait_ge(v_copied.sem, v_copied.of(it, w - 1))
                        for k in range(KD):
                            mm = pe.matmul(qkv_ps[:, j * CH:(j + 1) * CH], x_in[:, k, w * P:(w + 1) * P],
                                           w_qkv[:, k, j * INNER:(j + 1) * INNER], start=k == 0, stop=k == KD - 1)
                        if j == 1:
                            mm.then_inc(q_ready.sem, 1)
                    mm.then_inc(v_ready.sem, 1)

                def turn(w, j):
                    pe.wait_ge(rot_ready.sem, rot_ready.of(it, w))
                    pe.wait_ge(turn_copied.sem, turn_copied.of(it, 2 * w + j - 1))
                    for p in range(PAIRS):
                        mm = pe.transpose(turn_ps[:, p * P:(p + 1) * P],
                                          rot_c[:, j * INNER + p * P:j * INNER + (p + 1) * P], ident[:, :])
                    mm.then_inc(turned.sem, 1)

                def scores(u):
                    w = u // PAIRS
                    pe.wait_ge(turn_copied.sem, turn_copied.of(it, 2 * w + 1))
                    pe.wait_ge(s_masked.sem, s_masked.of(it, 2 * u - 3))
                    if u == 0:
                        pe.wait_ge(out_ready.sem, out_ready.of(it, -1))
                    k0 = max(0, w - 1) * P
                    for h in range(2):
                        p, side = place(u, h)
                        r = slice(side * HD2, (side + 1) * HD2)
                        mm = pe.matmul(s_ps[u % 2][:, (h + 1) * PW - ((w + 1) * P - k0):(h + 1) * PW],
                                       q_t[r, w % 2, p, :], k_t[r, p, k0:(w + 1) * P], start=True, stop=True)
                    mm.then_inc(s_ready.sem, 1)

                def turn_probs(u):
                    w = u // PAIRS
                    pe.wait_ge(scaled.sem, scaled.of(it, 2 * u + 1))
                    pe.wait_ge(pt_copied.sem, pt_copied.of(it, u - 1))
                    if u == 0:
                        pe.wait_ge(hn_t_ready.sem, hn_t_ready.of(it, -1))
                    for h in range(2):
                        for kt in range(0 if w else 1, 2):
                            mm = pe.transpose(pt_ps[:, (h * 2 + kt) * P:(h * 2 + kt + 1) * P],
                                              p_sb[:, u % 4, h, kt * P:(kt + 1) * P], ident[:, :])
                    mm.then_inc(pt_ready.sem, 1)

                def values(u):
                    w = u // PAIRS
                    pe.wait_ge(pt_copied.sem, pt_copied.of(it, u))
                    pe.wait_ge(v_copied.sem, v_copied.of(it, w))
                    if u % PAIRS == 0:
                        pe.wait_ge(o_copied.sem, o_copied.of(it, w - 1))
                    for h in range(2):
                        p, side = place(u, h)
                        head = 2 * p + side
                        for kt in range(0 if w else 1, 2):
                            mm = pe.matmul(o_ps[side * HD2:(side + 1) * HD2, p * P:(p + 1) * P],
                                           v_sb[:, w - 1 + kt, head * HD2:(head + 1) * HD2], p_t[:, u % 2, h, kt, :],
                                           start=kt == (0 if w else 1), stop=kt == 1, tile_position=(0, side * HD2))
                    mm.then_inc(pv_done.sem, 1)

                def project_out(c, m):
                    pe.wait_ge(o_copied.sem, o_copied.of(it, (c + 1) * WPC - 1))
                    if c == 0:
                        pe.wait_ge(qn_ready.sem, qn_ready.of(it, NT - 1))
                    else:
                        pe.wait_ge(v_copied.sem, v_copied.of(it, NT - 1))
                        pe.wait_ge(turn_copied.sem, turn_copied.of(it, 2 * NT - 1))
                    for k in range(INNER // P):
                        mm = pe.matmul(wo_ps[c][m], w_out[:, k, m * P:(m + 1) * P], o_t[:, k, c * CH:(c + 1) * CH],
                                       start=k == 0, stop=k == INNER // P - 1)
                    mm.then_inc(wo_ready.sem, 1)

                def tokens_first(c):
                    if c == 0:
                        pe.wait_ge(s_masked.sem, s_masked.of(it, 2 * UNITS - 1))
                    else:
                        pe.wait_ge(hn_ready.sem, hn_ready.of(it, c * TC - 1))
                    pe.wait_ge(mid_ready.sem, mid_ready.of(it, (c + 1) * KD - 1))
                    for t in range(TC):
                        for k in range(KD):
                            mm = pe.transpose(ln_ps[t // 2][:, (t % 2) * D + k * P:(t % 2) * D + (k + 1) * P],
                                              x_mid[:, k, c * CH + t * P:c * CH + (t + 1) * P], ident[:, :])
                        if t % 2:
                            mm.then_inc(ln_ready.sem, 1)

                def features_first(c):
                    pe.wait_ge(hn_ready.sem, hn_ready.of(it, (c + 1) * TC - 1))
                    if c == 0:
                        pe.wait_ge(pt_copied.sem, pt_copied.of(it, UNITS - 1))
                        pe.wait_ge(o_copied.sem, o_copied.of(it, NT - 1))
                    else:
                        pe.wait_ge(hn_t_ready.sem, hn_t_ready.of(it, c * KD - 1))
                    for k in range(KD):
                        for t in range(TC):
                            mm = pe.transpose(back_ps[k][:, t * P:(t + 1) * P], hn[:, t, k * P:(k + 1) * P], ident[:, :])
                        mm.then_inc(back_ready.sem, 1)

                def up(c, j):
                    i = c * HT + j
                    pe.wait_ge(hn_t_ready.sem, hn_t_ready.of(it, (c + 1) * KD - 1))
                    if i < 2:
                        pe.wait_ge(mid_ready.sem, mid_ready.of(it, (i + 1) * KD - 1))
                    else:
                        pe.wait_ge(hidden_ready.sem, hidden_ready.of(it, i - 2))
                    rows = P if j < HT - 1 else HL
                    for part in range(2):
                        f0 = part * HID + j * P
                        for k in range(KD):
                            mm = pe.matmul(up_ps[i % 2][part][0:rows, :], w_up[:, k, f0:f0 + rows], hn_t[:, k, :],
                                           start=k == 0, stop=k == KD - 1)
                    mm.then_inc(up_ready.sem, 1)

                def down(c, m):
                    pe.wait_ge(hidden_ready.sem, hidden_ready.of(it, (c + 1) * HT - 1))
                    if c == 0:
                        pe.wait_ge(hn_ready.sem, hn_ready.of(it, NC * TC - 1))
                    else:
                        pe.wait_ge(out_ready.sem, out_ready.of(it, (c - 1) * KD + m))
                    for j in range(HT):
                        rows = P if j < HT - 1 else HL
                        mm = pe.matmul(down_ps[m][:, :], w_down[0:rows, j, m * P:(m + 1) * P], hidden[0:rows, j, :],
                                       start=j == 0, stop=j == HT - 1)
                    mm.then_inc(down_ready.sem, 1)

                pe.wait_ge(x_loaded, it * (16 * KD) + 16 * KD)
                project(0)
                project(1)
                turn(0, 0)
                turn(0, 1)
                for u in range(UNITS + 3):
                    w, p = u // PAIRS, u % PAIRS
                    if u < UNITS:
                        scores(u)
                    if p == 0 and w + 2 < NT:
                        project(w + 2)
                    if 2 <= u < UNITS + 2:
                        turn_probs(u - 2)
                    if p >= 2 and w + 1 < NT:
                        turn(w + 1, p - 2)
                    if u >= 3:
                        values(u - 3)
                for c in range(NC):
                    for m in range(KD):
                        project_out(c, m)
                tokens_first(0)
                tokens_first(1)
                features_first(0)
                for j in range(HT):
                    up(0, j)
                features_first(1)
                for m in range(KD):
                    down(0, m)
                for j in range(HT):
                    up(1, j)
                for m in range(KD):
                    down(1, m)

            with pe.Fori(0, DEPTH) as l:
                wait_apart(pe, passed, weights_in, l * (16 * N_WEIGHT_DMAS) + 16 * N_WEIGHT_DMAS)
                with pe.Fori(0, B) as b:
                    batch(l, l * B + b)

        @block.scalar
        def _(act):
            for c in (squared, v_copied, turn_copied, o_copied, hn_t_ready, gelu_done):
                act.sem_inc(c.sem, c.credit)

            def batch(it):
                def square(w):
                    act.wait_ge(q_ready.sem, q_ready.of(it, w))
                    act.wait_ge(summed.sem, summed.of(it, w - 1)) if w else act.wait_ge(qn_ready.sem, qn_ready.of(it, -1))
                    act.activation(squares[:, :], q_ps, ACT.Square).then_inc(squared.sem, 1)
                    act.wait_ge(v_ready.sem, v_ready.of(it, w))
                    if w == 0:
                        act.wait_ge(wo_ready.sem, wo_ready.of(it, -1))
                    act.copy(v_sb[:, w, :], v_ps).then_inc(v_copied.sem, 1)

                def copy_turned(w, j):
                    act.wait_ge(turned.sem, turned.of(it, 2 * w + j))
                    if j == 0:
                        act.wait_ge(s_ready.sem, s_ready.of(it, (w - 1) * PAIRS - 1))
                    dst = q_t[:, w % 2, :, :] if j == 0 else k_t[:, :, w * P:(w + 1) * P]
                    act.copy(dst, turn_ps[:, :].rearrange("p (h t) -> p h t", h=PAIRS)).then_inc(turn_copied.sem, 1)

                def exponentials(u):
                    w = u // PAIRS
                    k0 = 0 if w else WIN
                    for h in range(2):
                        act.wait_ge(s_masked.sem, s_masked.of(it, 2 * u + h))
                        act.activation(p_sb[:, u % 4, h, k0:PW], p_sb[:, u % 4, h, k0:PW], ACT.Exp, scale=-1.0,
                                       bias=negmax[:, u % 4, h:h + 1],
                                       accum_out=total[:, u % 4, h:h + 1]).then_inc(exp_done.sem, 1)

                def copy_output(w):
                    act.wait_ge(pv_done.sem, pv_done.of(it, (w + 1) * PAIRS - 1))
                    if w == 0:
                        act.wait_ge(wo_ready.sem, wo_ready.of(it, -1))
                    act.copy(o_t[:, :, w * P:(w + 1) * P], o_ps[:, :].rearrange("p (h t) -> p h t", h=PAIRS))\
                       .then_inc(o_copied.sem, 1)

                def scale_norm(c):
                    for k in range(KD):
                        act.wait_ge(back_ready.sem, back_ready.of(it, c * KD + k))
                        act.wait_ge(up_ready.sem, up_ready.of(it, c * HT - 1))
                        act.activation(hn_t[:, k, :], back_ps[k][:, :], ACT.Identity, bias=ln_b[:, k:k + 1],
                                       scale=ln_g[:, k:k + 1]).then_inc(hn_t_ready.sem, 1)

                def gelu(c, j):
                    i = c * HT + j
                    rows = P if j < HT - 1 else HL
                    act.wait_ge(up_ready.sem, up_ready.of(it, i))
                    act.wait_ge(hidden_ready.sem, hidden_ready.of(it, i - 2))
                    act.activation(gate[0:rows, i % 2, :], up_ps[i % 2][1][0:rows, :], ACT.Gelu,
                                   bias=b_up[0:rows, 1, j:j + 1]).then_inc(gelu_done.sem, 1)

                square(0)
                square(1)
                copy_turned(0, 0)
                copy_turned(0, 1)
                for u in range(UNITS + 3):
                    w, p = u // PAIRS, u % PAIRS
                    if u < UNITS:
                        exponentials(u)
                    if p == 0 and w + 2 < NT:
                        square(w + 2)
                    if p >= 2 and w + 1 < NT:
                        copy_turned(w + 1, p - 2)
                    if u >= 3 and (u - 3) % PAIRS == PAIRS - 1:
                        copy_output((u - 3) // PAIRS)
                scale_norm(0)
                for j in range(HT):
                    gelu(0, j)
                scale_norm(1)
                for j in range(HT):
                    gelu(1, j)

            with act.Fori(0, DEPTH) as l:
                wait_apart(act, passed, weights_in, l * (16 * N_WEIGHT_DMAS) + 16 * N_WEIGHT_DMAS)
                with act.Fori(0, B) as b:
                    batch(l * B + b)

        @block.gpsimd
        def _(pool):
            pool.sem_inc(cos_ready.sem, cos_ready.credit)
            pool.memset(x_in[:, 1, 0:1], 0.0).then_inc(pads, 1)
            pool.memset(x_mid[:, 1, 0:1], 0.0).then_inc(pads, 1)
            pool.memset(band[:, :], 0.0).then_inc(pads, 1)
            pool.wait_ge(pads, 3)
            pool.affine_select(out=band[:, 0:WIN], in_=band[:, 0:WIN], compare_op=ALU.is_ge, fill=BIG, base=0,
                               pattern=[[1, WIN]], channel_multiplier=-1).then_inc(pads, 1)
            pool.affine_select(out=band[:, WIN:PW], in_=band[:, WIN:PW], compare_op=ALU.is_ge, fill=BIG, base=0,
                               pattern=[[-1, WIN]], channel_multiplier=1).then_inc(pads, 1)

            def batch(it):
                def norms(w):
                    wait_apart(pool, passed, summed.sem, summed.of(it, w))
                    pool.tensor_scalar(sum_sq[:, 1, :], sum_sq[:, 0, :], 1e-24, None, ALU.max).then_inc(clamped.sem, 1)
                    pool.wait_ge(clamped.sem, clamped.of(it, w))
                    pool.tensor_tensor(inv_norm[:, 0, :], sum_sq[:, 1, :], neg_half[:, 0:2 * H2], ALU.pow)\
                        .then_inc(inv_ready.sem, 1)

                def cosines(w):
                    pool.wait_ge(qn_ready.sem, qn_ready.of(it, w))
                    pool.wait_ge(turned.sem, turned.of(it, 2 * w - 1))
                    for j in range(2):
                        ins = pool.tensor_tensor(
                            rot_c[:, j * INNER:(j + 1) * INNER].rearrange("p (h d) -> p h d", h=H2),
                            qn[:, j * INNER:(j + 1) * INNER].rearrange("p (h d) -> p h d", h=H2),
                            rotary[:, w, 2 * j, :].unsqueeze(1).to_broadcast([P, H2, HD2]), ALU.mult)
                    ins.then_inc(cos_ready.sem, 1)

                def scale_probs(u):
                    k0 = 0 if u // PAIRS else WIN
                    wait_apart(pool, passed, inv_sum.sem, inv_sum.of(it, u))
                    for h in range(2):
                        pool.tensor_scalar(p_sb[:, u % 4, h, k0:PW], p_sb[:, u % 4, h, k0:PW],
                                           inv_total[:, u % 4, h:h + 1], None, ALU.mult).then_inc(scaled.sem, 1)

                norms(0)
                cosines(0)
                norms(1)
                cosines(1)
                for u in range(UNITS):
                    w, p = u // PAIRS, u % PAIRS
                    scale_probs(u)
                    if p == 1 and w + 2 < NT:
                        norms(w + 2)
                    if p == 3 and w + 2 < NT:
                        cosines(w + 2)
                for c in range(NC):
                    wait_apart(pool, passed, averaged.sem, averaged.of(it, (c + 1) * TC - 1))
                    pool.tensor_scalar(var_eps[:, :], mean_var[:, :, 1], EPS, None, ALU.add).then_inc(var_ready.sem, 1)
                    pool.wait_ge(var_ready.sem, var_ready.of(it, c))
                    pool.tensor_tensor(rstd[:, :], var_eps[:, :], neg_half[:, 0:TC], ALU.pow).then_inc(rstd_ready.sem, 1)

            with pool.Fori(0, DEPTH) as l:
                wait_apart(pool, passed, weights_in, l * (16 * N_WEIGHT_DMAS) + 16 * N_WEIGHT_DMAS)
                for w in range(NT):
                    ins = pool.tensor_tensor(rotary[:, w], rotary[:, w], head_scale[:, :, :], ALU.mult)
                ins.then_inc(rotary_ready, 1)
                wait_apart(pool, passed, rotary_ready, l + 1)
                with pool.Fori(0, B) as b:
                    batch(l * B + b)

        @block.vector
        def _(dve):
            for c in (qn_ready, rot_ready, s_masked, pt_copied, mid_ready, hn_ready, hidden_ready, out_ready):
                dve.sem_inc(c.sem, c.credit)
            dve.wait_ge(pads, 5)

            def batch(it):
                heads = lambda t: t.rearrange("p (h d) -> p h d", d=HD2)

                def sums(w):
                    dve.wait_ge(squared.sem, squared.of(it, w))
                    dve.wait_ge(clamped.sem, clamped.of(it, w - 1)) if w else None
                    dve.tensor_reduce(sum_sq[:, 0, :], heads(squares[:, :]), AX.X, ALU.add).then_inc(summed.sem, 1)

                def unit_vectors(w):
                    dve.wait_ge(inv_ready.sem, inv_ready.of(it, w))
                    dve.wait_ge(cos_ready.sem, cos_ready.of(it, w - 1))
                    dve.tensor_tensor(heads(qn[:, :]), heads(q_ps), inv_norm[:, 0, :].unsqueeze(2)
                                      .to_broadcast([P, 2 * H2, HD2]), ALU.mult).then_inc(qn_ready.sem, 1)

                def rotate(w):
                    dve.wait_ge(qn_ready.sem, qn_ready.of(it, w))
                    half = HD2 // 2
                    for j in range(2):
                        src = heads(qn[:, j * INNER:(j + 1) * INNER])
                        dst = heads(rot_s[:, j * INNER:(j + 1) * INNER])
                        for to in range(2):
                            o, i = slice(to * half, (to + 1) * half), slice((1 - to) * half, (2 - to) * half)
                            dve.tensor_tensor(dst[:, :, o], src[:, :, i], rotary[:, w, 2 * j + 1, o].unsqueeze(1)
                                              .to_broadcast([P, H2, half]), ALU.mult).then_inc(sin_ready.sem, 1)
                    dve.wait_ge(sin_ready.sem, sin_ready.of(it, 4 * w + 3))
                    dve.wait_ge(cos_ready.sem, cos_ready.of(it, w))
                    dve.tensor_tensor(rot_c[:, :], rot_c[:, :], rot_s[:, :], ALU.add).then_inc(rot_ready.sem, 1)

                def mask_scores(u):
                    k0 = 0 if u // PAIRS else WIN
                    for h in range(2):
                        wait_apart(dve, passed, s_ready.sem, s_ready.of(it, u))
                        if h == 0:
                            wait_apart(dve, passed, pt_ready.sem, pt_ready.of(it, u - 4))
                        dve.tensor_tensor_reduce(p_sb[:, u % 4, h, k0:PW], s_ps[u % 2][:, h * PW + k0:(h + 1) * PW],
                                                 band[:, k0:PW], 1.0, BIG, ALU.add, ALU.min,
                                                 negmax[:, u % 4, h:h + 1]).then_inc(s_masked.sem, 1)

                def invert_sums(u):
                    dve.wait_ge(exp_done.sem, exp_done.of(it, 2 * u + 1))
                    dve.reciprocal(inv_total[:, u % 4, :], total[:, u % 4, :]).then_inc(inv_sum.sem, 1)

                def copy_probs(u):
                    k0 = 0 if u // PAIRS else 1
                    dve.wait_ge(pt_ready.sem, pt_ready.of(it, u))
                    dve.wait_ge(pv_done.sem, pv_done.of(it, u - 2))
                    dve.tensor_copy(p_t[:, u % 2, :, k0:2, :],
                                    pt_ps[:, :].rearrange("p (h k t) -> p h k t", h=2, k=2)[:, :, k0:2, :])\
                       .then_inc(pt_copied.sem, 1)

                def residual(c, m):
                    dve.wait_ge(wo_ready.sem, wo_ready.of(it, c * KD + m))
                    if c == 0:
                        dve.wait_ge(out_ready.sem, out_ready.of(it, -1))
                    s = slice(m + c * CH, m + (c + 1) * CH)
                    dve.tensor_tensor(x_mid[:, m, s], wo_ps[c][m], x_in[:, m, s], ALU.add).then_inc(mid_ready.sem, 1)

                def layer_norm(c):
                    tile = lambda t: ln_ps[t // 2][:, (t % 2) * D:(t % 2 + 1) * D]
                    for t in range(TC):
                        dve.wait_ge(ln_ready.sem, ln_ready.of(it, 2 * c + t // 2))
                        dve.bn_stats(stats[:, t, :], tile(t)).then_inc(counted.sem, 1)
                    wait_apart(dve, passed, counted.sem, counted.of(it, (c + 1) * TC - 1))
                    for t in range(TC):
                        dve.bn_aggr(mean_var[:, t, :], stats[:, t, :]).then_inc(averaged.sem, 1)
                    dve.wait_ge(averaged.sem, averaged.of(it, (c + 1) * TC - 1))
                    dve.wait_ge(rstd_ready.sem, rstd_ready.of(it, c))
                    dve.wait_ge(back_ready.sem, back_ready.of(it, c * KD - 1))
                    for t in range(TC):
                        dve.tensor_scalar(hn[:, t, :], tile(t), mean_var[:, t, 0:1], rstd[:, t:t + 1],
                                          ALU.subtract, ALU.mult).then_inc(hn_ready.sem, 1)

                def gated(c, j):
                    i = c * HT + j
                    rows = P if j < HT - 1 else HL
                    dve.wait_ge(gelu_done.sem, gelu_done.of(it, i))
                    if j == 0:
                        dve.wait_ge(down_ready.sem, down_ready.of(it, c * KD - 1))
                    dve.scalar_tensor_tensor(out=hidden[0:rows, j, :], in0=up_ps[i % 2][0][0:rows, :],
                                             scalar=b_up[0:rows, 0, j:j + 1], in1=gate[0:rows, i % 2, :],
                                             op0=ALU.add, op1=ALU.mult).then_inc(hidden_ready.sem, 1)

                def output(c, m):
                    dve.wait_ge(down_ready.sem, down_ready.of(it, c * KD + m))
                    dve.wait_ge(out_stored[m], it * (16 * NC) + 16 * (c + 1))
                    s = slice(m + c * CH, m + (c + 1) * CH)
                    dve.scalar_tensor_tensor(out=x_out[:, m, :], in0=down_ps[m][:, :], scalar=b_down[:, m:m + 1],
                                             in1=x_mid[:, m, s], op0=ALU.add, op1=ALU.add).then_inc(out_ready.sem, 1)

                for w in range(2):
                    sums(w)
                    unit_vectors(w)
                    rotate(w)
                for u in range(UNITS + 3):
                    w, p = u // PAIRS, u % PAIRS
                    if u < UNITS:
                        mask_scores(u)
                        if u >= 1:
                            invert_sums(u - 1)
                    if u == UNITS:
                        invert_sums(u - 1)
                    if 2 <= u < UNITS + 2:
                        copy_probs(u - 2)
                    if p == 0 and 1 <= w < NT - 1:
                        rotate(w + 1)
                    if p == 1 and w + 2 < NT:
                        sums(w + 2)
                    if p == 2 and w + 2 < NT:
                        unit_vectors(w + 2)
                for c in range(NC):
                    for m in range(KD):
                        residual(c, m)
                layer_norm(0)
                layer_norm(1)
                for c in range(NC):
                    for j in range(HT):
                        gated(c, j)
                    for m in range(KD):
                        output(c, m)

            with dve.Fori(0, DEPTH) as l:
                wait_apart(dve, passed, weights_in, l * (16 * N_WEIGHT_DMAS) + 16 * N_WEIGHT_DMAS)
                wait_apart(dve, passed, rotary_ready, l + 1)
                with dve.Fori(0, B) as b:
                    batch(l * B + b)


def finish(nc, ident, a):
    with ExitStack() as ctx:
        sb = lambda name, shape, dt=F32: ctx.enter_context(nc.sbuf_tensor(name, shape, dt))
        sem = lambda name: ctx.enter_context(nc.semaphore(name))
        y_t = sb("y_t", [P, NC, KD, CH])
        x1 = sb("x1_f", [P, NC, TC, D])
        out = sb("out_f", [P, NC, TC, D])
        y_ps = [ctx.enter_context(nc.psum_tensor(f"yt_ps{i}", [P, CH], F32)) for i in range(4)]
        loaded = [sem(f"loaded_f{c}") for c in range(NC)]
        turned = Count(sem("turned_f"), NT, NT)
        added = Count(sem("added_f"), NT, NT)
        stored = [sem(f"stored_f{c}") for c in range(NC)]
        block = ctx.enter_context(nc.Block())

        @block.sync
        def _(sp):
            for s in stored:
                sp.sem_inc(s, 16)

            def load(i):
                b, c = i // NC, i % NC
                if b:
                    sp.wait_ge(added.sem, added.of(b - 1, (c + 1) * TC - 1))
                sp.dma_start(y_t[:, c], a["xt_scratch"][b, :, :, c * CH:(c + 1) * CH].rearrange("k p t -> p k t"))\
                    .then_inc(loaded[c], 16)
                sp.dma_start(x1[:, c], a["x1_scratch"][b, c * CH:(c + 1) * CH, :].rearrange("(t p) d -> p t d", p=P))\
                    .then_inc(loaded[c], 16)

            for i in range(NC):
                load(i)
            for i in range(B * NC):
                b, c = i // NC, i % NC
                sp.wait_ge(added.sem, added.of(b, (c + 1) * TC - 1))
                sp.dma_start(a["out"][b, c * CH:(c + 1) * CH, :].rearrange("(t p) d -> p t d", p=P), out[:, c])\
                    .then_inc(stored[c], 16)
                if i + NC < B * NC:
                    load(i + NC)
            for s in stored:
                sp.wait_ge(s, 16 * (B + 1))

        @block.tensor
        def _(pe):
            pe.sem_inc(turned.sem, turned.credit)
            with pe.Fori(0, B) as b:
                for t in range(NT):
                    if t % TC == 0:
                        pe.wait_ge(loaded[t // TC], b * 32 + 32)
                    pe.wait_ge(added.sem, added.of(b, t - 4))
                    for k in range(KD):
                        mm = pe.transpose(y_ps[t % 4][:, k * P:(k + 1) * P],
                                          y_t[:, t // TC, k, (t % TC) * P:(t % TC + 1) * P], ident[:, :])
                    mm.then_inc(turned.sem, 1)

        @block.vector
        def _(dve):
            dve.sem_inc(added.sem, added.credit)
            with dve.Fori(0, B) as b:
                for t in range(NT):
                    dve.wait_ge(turned.sem, turned.of(b, t))
                    if t % TC == 0:
                        dve.wait_ge(loaded[t // TC], b * 32 + 32)
                        dve.wait_ge(stored[t // TC], b * 16 + 16)
                    dve.tensor_tensor(out[:, t // TC, t % TC, :], y_ps[t % 4][:, 0:D], x1[:, t // TC, t % TC, :],
                                      ALU.add).then_inc(added.sem, 1)


def build(nc, a):
    with ExitStack() as ctx:
        sb = lambda name, shape, dt=F32: ctx.enter_context(nc.sbuf_tensor(name, shape, dt))
        ident = sb("ident", [P, P])
        ident_b = sb("ident_b", [P, P], BF16)
        causal_b = sb("causal_b", [P, P], BF16)
        neg_half = sb("neg_half", [P, 2 * H2])
        passed = ctx.enter_context(nc.semaphore("passed"))
        zeroed = ctx.enter_context(nc.semaphore("zeroed"))
        drawn = ctx.enter_context(nc.semaphore("drawn"))
        with nc.Block() as block:
            @block.gpsimd
            def _(pool):
                pool.memset(ident[:, :], 0.0).then_inc(zeroed, 1)
                pool.memset(ident_b[:, :], 0.0).then_inc(zeroed, 1)
                pool.memset(causal_b[:, :], 0.0).then_inc(zeroed, 1)
                pool.memset(neg_half[:, :], -0.5).then_inc(zeroed, 1)
                pool.wait_ge(zeroed, 4)
                for m in (ident, ident_b):
                    pool.affine_select(out=m[:, :], in_=m[:, :], compare_op=ALU.not_equal, fill=1.0, base=0,
                                       pattern=[[-1, P]], channel_multiplier=1).then_inc(drawn, 1)
                pool.affine_select(out=causal_b[:, :], in_=causal_b[:, :], compare_op=ALU.is_ge, fill=-1e30, base=0,
                                   pattern=[[-1, P]], channel_multiplier=1).then_inc(drawn, 1)
                pool.wait_ge(drawn, 3)
        with nc.sbuf_tensor("x_all", [P, B * NT, D], F32) as x_all:
            prepare(nc, x_all, ident, neg_half, passed, a)
            causal_attention(nc, ident, ident_b, causal_b, passed, a)
            project_causal(nc, x_all, ident, neg_half, passed, a)
        layers(nc, ident, neg_half, passed, a)
        finish(nc, ident, a)


def rotary_tables():
    f = np.float32
    half = np.arange(0, HD2, 2, dtype=f)
    inv_freq = (f(1.0) / f(10000.0) ** (half / f(HD2))).astype(f)
    t = np.arange(T, dtype=f)
    angle = t[:, None] * inv_freq[None, :]
    base = ((half + f(0.4 * HD2)) / f(1.4 * HD2)).astype(f)
    power = ((t - f(T // 2)) / f(WIN // 2)).astype(f)
    scale = base[None, :] ** power[:, None]
    twice = lambda x: np.concatenate([x, x], axis=-1)
    sign = np.where(np.arange(HD2) < HD2 // 2, f(-1), f(1))
    cos, sin, scale = np.cos(twice(angle)), np.sin(twice(angle)) * sign, twice(scale)
    q = f(-QK_SCALE)
    return np.stack([q * cos * scale, q * sin * scale, cos / scale, sin / scale], axis=1).astype(f)


_NAMES = {"x": "L0_attn_x", "wq": "L0_attn_wq", "bq": "L0_attn_bq", "wk": "L0_attn_wk", "bk": "L0_attn_bk",
          "wv": "L0_attn_wv", "bv": "L0_attn_bv", "wo": "L0_attn_wo", "bo": "L0_attn_bo", "wqkv": "L0_ffn_wqkv",
          "q_scale": "L0_ffn_q_scale", "k_scale": "L0_ffn_k_scale", "wo2": "L0_ffn_wo", "ln_g": "L0_ffn_ln_g",
          "ln_b": "L0_ffn_ln_b", "w1": "L0_ffn_w1", "b1": "L0_ffn_b1", "w2": "L0_ffn_w2", "b2": "L0_ffn_b2"}


def kernel(**inputs):
    import concourse.bacc as bacc
    from concourse.bass_utils import run_bass_kernel_spmd

    nc = bacc.Bacc("TRN2", target_bir_lowering=False, num_devices=1)
    nc.disable_value_cache = True
    arrays = {short: np.ascontiguousarray(inputs[name]) for short, name in _NAMES.items()}
    arrays["rotary"] = rotary_tables()
    a = {n: nc.dram_tensor(f"in_{n}", list(x.shape), mybir.dt.from_np(x.dtype), kind="ExternalInput").ap()
         for n, x in arrays.items()}
    scratch = {"v_scratch": ([B * NG, P, NT, HG * VW], F32), "qk_scratch": ([2, B * NG, 3, GF, T], BF16),
               "att_scratch": ([B * NG, T, GF], F32), "x1_scratch": ([B, T, D], F32), "xt_scratch": ([B, KD, P, T], F32)}
    for n, (shape, dt) in scratch.items():
        a[n] = nc.dram_tensor(n, shape, dt, kind="Internal").ap()
    a["out"] = nc.dram_tensor("out", [B, T, D], F32, kind="ExternalOutput").ap()
    build(nc, a)
    r = run_bass_kernel_spmd(nc, [{f"in_{n}": x for n, x in arrays.items()}], core_ids=[0])
    return r.results[0]["out"]
```

```python
import concourse.bass as bass
import numpy as np
from concourse import mybir
from contextlib import ExitStack

F32 = mybir.dt.float32
BF16 = mybir.dt.bfloat16
ALU = mybir.AluOpType
ACT = mybir.ActivationFunctionType
AX = mybir.AxisListType

P = 128
B, T, D = 4, 1024, 256
KD = D // P
NT = T // P
CH = 512
NC = T // CH
TC = CH // P

H1, HD1 = 16, 16
HG = 4
NG = H1 // HG
GF = HG * HD1
VW = 32
TERMS = ((0, 0), (0, 1), (0, 2), (1, 0), (1, 1), (2, 0))
STK = len(TERMS) * HD1

DEPTH, H2, HD2, WIN = 2, 8, 64, 128
INNER = H2 * HD2
HID = int(D * 4 * 2 / 3)
QK_SCALE = 8.0
EPS = 1e-5
BIG = 3.0e38


class Count:

    def __init__(self, sem, per, credit=0):
        self.sem, self.per, self.credit = sem, per, credit

    def of(self, iteration, item):
        return iteration * self.per + (item + 1 + self.credit)


def wait_apart(eng, passed, sem, value):
    eng.wait_ge(sem, value)
    eng.sem_inc(passed, 1)


def prepare(nc, x_all, ident, neg_half, passed, a):
    with ExitStack() as ctx:
        sb = lambda name, shape, dt=F32: ctx.enter_context(nc.sbuf_tensor(name, shape, dt))
        ps = lambda name, shape: ctx.enter_context(nc.psum_tensor(name, shape, F32))
        sem = lambda name: ctx.enter_context(nc.semaphore(name))

        w_qk = sb("w_qk", [P, KD, 2 * D])
        w_v = sb("w_v", [P, KD, D])
        b_qk = sb("b_qk", [P, 2 * KD])
        b_v = sb("b_v", [P, D])
        stats = sb("stats", [P, NT, 6])
        mean_var = sb("mean_var", [P, NT, 2])
        var_eps = sb("var_eps", [P, NT])
        rstd = sb("rstd", [P, NT])
        xn = sb("xn", [P, 2, D])
        xn_t = sb("xn_t", [P, KD, T])
        full = sb("full", [P, 2, CH])
        rest = sb("rest", [P, 2, CH])
        parts = sb("parts", [P, 4, 3, CH], BF16)
        v_out = sb("v_out", [P, 2, H1, VW])
        turned = [ps(f"turned{i}", [P, CH]) for i in range(2)]
        v_ps = [ps(f"v_ps{i}", [P, CH]) for i in range(2)]
        qk_ps = [ps(f"qk_ps{i}", [P, CH]) for i in range(2)]

        weights_in = sem("weights_in")
        x_in = sem("x_in")
        scaled_bias = sem("scaled_bias")
        ones_set = sem("ones_set")
        counted = Count(sem("counted"), NT)
        averaged = Count(sem("averaged"), NT)
        var_ready = Count(sem("var_ready"), 1)
        rstd_ready = Count(sem("rstd_ready"), 1)
        xn_ready = Count(sem("xn_ready"), NT, 8)
        turned_ready = Count(sem("turned_ready"), NT, 2)
        xn_t_ready = Count(sem("xn_t_ready"), NT, 2)
        v_ready = Count(sem("v_ready"), NT, 8)
        v_copied = Count(sem("v_copied"), NT, 2)
        NI = NC * 2 * KD
        qk_ready = Count(sem("qk_ready"), NI, 8)
        full_ready = Count(sem("full_ready"), NI, 2)
        high_ready = Count(sem("high_ready"), NI, 2)
        rest_ready = Count(sem("rest_ready"), NI, 2)
        mid_ready = Count(sem("mid_ready"), NI, 2)
        low_ready = Count(sem("low_ready"), NI, 2)
        v_stored = [sem(f"v_stored{i}") for i in range(2)]
        parts_stored = [sem(f"parts_stored{i}") for i in range(4)]
        block = ctx.enter_context(nc.Block())

        @block.sync
        def _(sp):
            w_dma = [
                sp.dma_start(w_qk[:, :, 0:D], a["wq"].rearrange("(k p) n -> p k n", p=P)),
                sp.dma_start(w_qk[:, :, D:2 * D], a["wk"].rearrange("(k p) n -> p k n", p=P)),
                sp.dma_start(w_v[:, :, :], a["wv"].rearrange("(k p) n -> p k n", p=P)),
                sp.dma_start(b_qk[:, 0:KD], a["bq"].rearrange("(m p) -> p m", p=P), allow_slow_non_contiguous=True),
                sp.dma_start(b_qk[:, KD:2 * KD], a["bk"].rearrange("(m p) -> p m", p=P), allow_slow_non_contiguous=True),
                sp.dma_start(b_v[:, :], a["bv"].partition_broadcast(P)),
            ]
            for d in w_dma:
                d.then_inc(weights_in, 16)

            def load_x(b):
                if b >= 1:
                    sp.wait_ge(x_in, 16 * b)
                sp.dma_start(x_all[:, b * NT:(b + 1) * NT, :],
                             a["x"][b].rearrange("(t p) d -> p t d", p=P)).then_inc(x_in, 16)

            for s in v_stored:
                sp.sem_inc(s, 16)
            for s in parts_stored:
                sp.sem_inc(s, 32)
            load_x(0)
            load_x(1)
            for b in range(B):
                for t in range(NT):
                    sp.wait_ge(v_copied.sem, v_copied.of(b, t))
                    sp.dma_start(a["v_scratch"][b * NG:(b + 1) * NG, :, t, :].rearrange("g p n -> p g n"),
                                 v_out[:, t % 2].rearrange("p (g h) w -> p g (h w)", g=NG)).then_inc(v_stored[t % 2], 16)
                    if t % 4 == 3:
                        if t == 3 and b + 2 < B:
                            load_x(b + 2)
                        for m in range(2 * KD):
                            i = (t // 4) * 2 * KD + m
                            sp.wait_ge(low_ready.sem, low_ready.of(b, i))
                            c0 = (t // 4) * CH
                            for half in range(2):
                                g = b * NG + (m % KD) * 2 + half
                                sp.dma_start(a["qk_scratch"][m // KD, g, :, :, c0:c0 + CH].rearrange("s f t -> f s t"),
                                             parts[half * GF:(half + 1) * GF, i % 4]).then_inc(parts_stored[i % 4], 16)
            for s in v_stored:
                sp.wait_ge(s, 16 * (B * NT // 2 + 1))
            for s in parts_stored:
                sp.wait_ge(s, 32 * (B * NI // 4 + 1))

        @block.vector
        def _(dve):
            dve.sem_inc(xn_ready.sem, xn_ready.credit)
            dve.sem_inc(v_copied.sem, v_copied.credit)
            dve.sem_inc(high_ready.sem, high_ready.credit)
            dve.sem_inc(mid_ready.sem, mid_ready.credit)
            dve.memset(v_out[:, :, :, HD1:VW], 1.0).then_inc(ones_set, 1)
            dve.wait_ge(weights_in, 96)
            dve.tensor_scalar(b_qk[:, 0:KD], b_qk[:, 0:KD], HD1 ** -0.5, None, ALU.mult).then_inc(scaled_bias, 1)
            with dve.Fori(0, B) as b:
                dve.wait_ge(x_in, b * 16 + 16)
                for t in range(NT):
                    dve.bn_stats(stats[:, t, :], x_all[:, bass.ds(b * NT + t, 1), :]).then_inc(counted.sem, 1)
                wait_apart(dve, passed, counted.sem, counted.of(b, NT - 1))
                for t in range(NT):
                    dve.bn_aggr(mean_var[:, t, :], stats[:, t, :]).then_inc(averaged.sem, 1)
                dve.wait_ge(averaged.sem, averaged.of(b, NT - 1))
                dve.wait_ge(rstd_ready.sem, rstd_ready.of(b, 0))

                def normalise(t):
                    dve.wait_ge(turned_ready.sem, turned_ready.of(b, t - 2))
                    dve.tensor_scalar(xn[:, t % 2, :], x_all[:, bass.ds(b * NT + t, 1), :], mean_var[:, t, 0:1],
                                      rstd[:, t:t + 1], ALU.subtract, ALU.mult).then_inc(xn_ready.sem, 1)

                def copy_v(t):
                    dve.wait_ge(v_ready.sem, v_ready.of(b, t))
                    dve.wait_ge(v_stored[t % 2], b * (16 * NT // 2) + 16 * (t // 2 + 1))
                    dve.tensor_tensor(v_out[:, t % 2, :, 0:HD1], v_ps[t % 2][:, 0:D].rearrange("p (h d) -> p h d", h=H1),
                                      b_v[:, :].rearrange("p (h d) -> p h d", h=H1), ALU.add).then_inc(v_copied.sem, 1)

                def high(i):
                    dve.wait_ge(full_ready.sem, full_ready.of(b, i))
                    dve.wait_ge(parts_stored[i % 4], b * (32 * NI // 4) + 32 * (i // 4 + 1))
                    dve.tensor_copy(parts[:, i % 4, 0, :], full[:, i % 2, :]).then_inc(high_ready.sem, 1)

                def mid(i):
                    dve.wait_ge(rest_ready.sem, rest_ready.of(b, i))
                    dve.tensor_copy(parts[:, i % 4, 1, :], rest[:, i % 2, :]).then_inc(mid_ready.sem, 1)

                for t in range(6):
                    normalise(t)
                    if t >= 2:
                        copy_v(t - 2)
                for i in range(4):
                    high(i)
                    if i >= 1:
                        mid(i - 1)
                mid(3)
                for t in range(6, NT + 2):
                    if t < NT:
                        normalise(t)
                    copy_v(t - 2)
                for i in range(4, 8):
                    high(i)
                    if i >= 5:
                        mid(i - 1)
                mid(7)

        @block.gpsimd
        def _(pool):
            pool.sem_inc(rest_ready.sem, rest_ready.credit)
            pool.sem_inc(low_ready.sem, low_ready.credit)
            with pool.Fori(0, B) as b:
                pool.wait_ge(averaged.sem, averaged.of(b, NT - 1))
                wait_apart(pool, passed, xn_ready.sem, xn_ready.of(b, -1))
                pool.tensor_scalar(var_eps[:, :], mean_var[:, :, 1], EPS, None, ALU.add).then_inc(var_ready.sem, 1)
                pool.wait_ge(var_ready.sem, var_ready.of(b, 0))
                pool.tensor_tensor(rstd[:, :], var_eps[:, :], neg_half[:, 0:NT], ALU.pow).then_inc(rstd_ready.sem, 1)

                def low(i):
                    pool.wait_ge(mid_ready.sem, mid_ready.of(b, i))
                    pool.tensor_tensor(parts[:, i % 4, 2, :], rest[:, i % 2, :], parts[:, i % 4, 1, :],
                                       ALU.subtract).then_inc(low_ready.sem, 1)

                for i in range(NI):
                    pool.wait_ge(high_ready.sem, high_ready.of(b, i))
                    pool.wait_ge(low_ready.sem, low_ready.of(b, i - 2))
                    pool.tensor_tensor(rest[:, i % 2, :], full[:, i % 2, :], parts[:, i % 4, 0, :],
                                       ALU.subtract).then_inc(rest_ready.sem, 1)
                    if i % 4 >= 1:
                        low(i - 1)
                    if i % 4 == 3:
                        low(i)

        @block.scalar
        def _(act):
            act.sem_inc(xn_t_ready.sem, xn_t_ready.credit)
            act.sem_inc(full_ready.sem, full_ready.credit)
            act.wait_ge(scaled_bias, 1)
            with act.Fori(0, B) as b:
                def copy_turned(t):
                    act.wait_ge(turned_ready.sem, turned_ready.of(b, t))
                    act.wait_ge(qk_ready.sem, qk_ready.of(b, (t // TC + 1) * 2 * KD - 1 - NI))
                    act.copy(xn_t[:, :, t * P:(t + 1) * P],
                             turned[t % 2][:, 0:D].rearrange("p (k t) -> p k t", k=KD)).then_inc(xn_t_ready.sem, 1)

                def copy_qk(i):
                    m = i % (2 * KD)
                    act.wait_ge(qk_ready.sem, qk_ready.of(b, i))
                    act.wait_ge(rest_ready.sem, rest_ready.of(b, i - 2))
                    act.activation(full[:, i % 2, :], qk_ps[i % 2][:, :], ACT.Identity, bias=b_qk[:, m:m + 1],
                                   scale=HD1 ** -0.5 if m < KD else 1.0).then_inc(full_ready.sem, 1)

                for c in range(NC):
                    for t in range(c * TC, (c + 1) * TC):
                        copy_turned(t)
                    for i in range(c * 2 * KD, (c + 1) * 2 * KD):
                        copy_qk(i)

        @block.tensor
        def _(pe):
            pe.sem_inc(turned_ready.sem, turned_ready.credit)
            pe.sem_inc(v_ready.sem, v_ready.credit)
            pe.sem_inc(qk_ready.sem, qk_ready.credit)
            pe.wait_ge(weights_in, 96)
            with pe.Fori(0, B) as b:
                def turn(t):
                    pe.wait_ge(xn_ready.sem, xn_ready.of(b, t))
                    pe.wait_ge(xn_t_ready.sem, xn_t_ready.of(b, t - 2))
                    for k in range(KD):
                        mm = pe.transpose(turned[t % 2][:, k * P:(k + 1) * P], xn[:, t % 2, k * P:(k + 1) * P], ident[:, :])
                    mm.then_inc(turned_ready.sem, 1)

                def project_v(t):
                    pe.wait_ge(xn_t_ready.sem, xn_t_ready.of(b, t))
                    pe.wait_ge(v_copied.sem, v_copied.of(b, t - 2))
                    for k in range(KD):
                        mm = pe.matmul(v_ps[t % 2][:, 0:D], xn_t[:, k, t * P:(t + 1) * P], w_v[:, k, :],
                                       start=k == 0, stop=k == KD - 1)
                    mm.then_inc(v_ready.sem, 1)

                def project_qk(c, m):
                    i = c * 2 * KD + m
                    pe.wait_ge(full_ready.sem, full_ready.of(b, i - 2))
                    for k in range(KD):
                        mm = pe.matmul(qk_ps[i % 2][:, :], w_qk[:, k, m * P:(m + 1) * P], xn_t[:, k, c * CH:(c + 1) * CH],
                                       start=k == 0, stop=k == KD - 1)
                    mm.then_inc(qk_ready.sem, 1)

                for c in range(NC):
                    turn(c * TC)
                    for t in range(c * TC + 1, (c + 1) * TC):
                        turn(t)
                        project_v(t - 1)
                    project_v((c + 1) * TC - 1)
                    for m in range(2 * KD):
                        project_qk(c, m)


SETS = [(c, kt) for c in range(NC) for kt in range((c + 1) * TC)]
NS = len(SETS)
DIAGONAL = [n for n, (c, kt) in enumerate(SETS) if kt >= c * TC]


def first_query(c, kt):
    return max(0, kt - c * TC) * P


PIECES = [(qt, k0, min(CH, (qt + 1) * P - k0)) for qt in range(NT) for k0 in range(0, (qt + 1) * P, CH)]
NP = len(PIECES)
SHIFT = 2
SLOTS = 4
HALF = HG // 2
SR = SHIFT * HALF * NT


def beside():
    columns = [CH - first_query(*SETS[n]) for n in range(NS) for h in range(HG)]
    pieces, shift, taken, upto, i = [], {}, 0, 0, 0
    for at, cols in enumerate(columns):
        upto += cols * 1.14
        first = i
        while i < NP * HG and taken < upto:
            taken += PIECES[i % NP][2]
            i += 1
            if i == NP * HALF:
                shift[at + 6] = 0
            if i == NP * HG:
                shift[min(at + 5, NS * HG - 1)] = 1
        pieces.append(i - first)
    return pieces, shift


PIECES_AT, SHIFT_AT = beside()


def causal_attention(nc, ident, ident_b, causal_b, passed, a):
    with ExitStack() as ctx:
        sb = lambda name, shape, dt=F32: ctx.enter_context(nc.sbuf_tensor(name, shape, dt))
        ps = lambda name: ctx.enter_context(nc.psum_tensor(name, [P, CH], F32))
        sem = lambda name: ctx.enter_context(nc.semaphore(name))

        q_stack = sb("q_stack", [P, SLOTS, HG, T], BF16)
        k_stack = sb("k_stack", [P, SLOTS, HG, T], BF16)
        v_sb = sb("v_sb", [P, SLOTS, NT, HG * VW])
        probs = sb("probs", [P, 3, HG, CH])
        piece_negmax = sb("piece_negmax", [P, HG, NP])
        negmax = sb("negmax", [P, HG, NT])
        negmax_parts = sb("negmax_parts", [P, 2, SHIFT, HALF, NT], BF16)
        shift_sb = sb("shift_sb", [SR, 2, P], BF16)
        o_sb = sb("o_sb", [P, NC, CH])
        inv_sum = sb("inv_sum", [P, NC, TC, HG])
        att = sb("att", [P, NC, TC, HG, HD1])
        st_ps = [ps(f"st_ps{i}") for i in range(3)]
        s_ps = [ps(f"s_ps{i}") for i in range(3)]
        o_ps, ot_ps = ps("o_ps"), ps("ot_ps")
        shift_ps = ot_ps

        def count(name, items, credit=0):
            return Count(sem(name), SLOTS * items, credit)

        st_ready = count("st_ready", NS * HG)
        exp_done = count("exp_done", NS * HG, 8)
        masked = count("masked", len(DIAGONAL))
        pv_done = count("pv_done", NS, 3)
        s_ready = count("s_ready", NP * HG)
        piece_done = count("piece_done", NP * HG, 3)
        joined = count("joined", 2 * 2)
        parts_done = count("parts_done", 2 * 2)
        shift_ready = count("shift_ready", 2, 2)
        shift_copied = count("shift_copied", 2)
        shift_in = [sem(f"shift_in{i}") for i in range(2)]
        o_copied = count("o_copied", NC, 1)
        ot_ready = count("ot_ready", NC)
        summed = count("summed", NC)
        att_ready = count("att_ready", NC, 1)
        att_stored = [sem(f"att_stored{c}") for c in range(NC)]
        stack_in = [sem(f"stack_in{s}") for s in range(SLOTS)]
        shift_ones = sem("shift_ones")
        LOAD = 16 * (2 * len(TERMS) + 1)
        block = ctx.enter_context(nc.Block())

        def groups(eng, group, first):
            first((0, 0))
            group((0, 0), None, (0, 1))
            with eng.Fori(0, B - 1) as r:
                for s in range(1, SLOTS + 1):
                    at = lambda s: (r + s // SLOTS, s % SLOTS)
                    group(at(s), at(s - 1), at(s + 1))
            for s in range(1, SLOTS):
                group((B - 1, s), (B - 1, s - 1), (B - 1, s + 1) if s + 1 < SLOTS else None)

        def shift_there(eng, group, half):
            eng.wait_ge(shift_in[half], (group[0] * SLOTS + group[1]) * (16 * SHIFT) + 16 * SHIFT)

        def when(count, group, items, i):
            return count.of(group[0], group[1] * items + i)

        @block.sync
        def _(sp):
            for c in range(NC):
                sp.sem_inc(att_stored[c], 16)

            def load(g):
                slot = g % SLOTS
                if g >= SLOTS:
                    sp.wait_ge(pv_done.sem, when(pv_done, (g // SLOTS - 1, slot), NS, NS - 1))
                for r, (qp, kp) in enumerate(TERMS):
                    for stack, which, part in ((q_stack, 0, qp), (k_stack, 1, kp)):
                        sp.dma_start(stack[r * HD1:(r + 1) * HD1, slot, :, :],
                                     a["qk_scratch"][which, g, part].rearrange("(h d) t -> d h t", d=HD1))\
                            .then_inc(stack_in[slot], 16)
                sp.dma_start(v_sb[:, slot], a["v_scratch"][g]).then_inc(stack_in[slot], 16)

            def store(g, c):
                sp.wait_ge(att_ready.sem, when(att_ready, (g // SLOTS, g % SLOTS), NC, c))
                sp.dma_start(a["att_scratch"][g, c * CH:(c + 1) * CH, :].rearrange("(t p) n -> p t n", p=P),
                             att[:, c].rearrange("p t h d -> p t (h d)")).then_inc(att_stored[c], 16)

            def spread_shift(g, half):
                sp.wait_ge(shift_copied.sem, when(shift_copied, (g // SLOTS, g % SLOTS), 2, half))
                for part in range(SHIFT):
                    sp.dma_start(q_stack[STK + part:STK + part + 1, g % SLOTS, half * HALF:(half + 1) * HALF, :],
                                 shift_sb[part * HALF * NT:(part + 1) * HALF * NT, half, :]).then_inc(shift_in[half], 16)

            for g in range(SLOTS):
                load(g)
            spread_shift(0, 0)
            spread_shift(0, 1)
            for g in range(B * NG):
                if g >= 1:
                    store(g - 1, 1)
                    if g - 1 + SLOTS < B * NG:
                        load(g - 1 + SLOTS)
                if g + 1 < B * NG:
                    spread_shift(g + 1, 0)
                store(g, 0)
                if g + 1 < B * NG:
                    spread_shift(g + 1, 1)
            store(B * NG - 1, 1)
            for c in range(NC):
                sp.wait_ge(att_stored[c], 16 * (B * NG + 1))

        @block.tensor
        def _(pe):
            for c in (pv_done, shift_ready):
                pe.sem_inc(c.sem, c.credit)
            pe.wait_ge(shift_ones, 1)

            def loaded(group):
                pe.wait_ge(stack_in[group[1]], group[0] * LOAD + LOAD)

            def score_piece(group, i):
                slot, h, (qt, k0, kw) = group[1], i // NP, PIECES[i % NP]
                pe.wait_ge(piece_done.sem, when(piece_done, group, NP * HG, i - 3))
                last = k0 + kw == (qt + 1) * P
                mm = pe.matmul(s_ps[i % 3][:, 0:kw], q_stack[0:STK, slot, h, qt * P:(qt + 1) * P],
                               k_stack[0:STK, slot, h, k0:k0 + kw], start=True, stop=not last)
                if last:
                    mm = pe.matmul(s_ps[i % 3][:, kw - P:kw], ident_b[:, :], causal_b[:, :], start=False, stop=True)
                mm.then_inc(s_ready.sem, 1)

            def shift_rows(group, half):
                pe.wait_ge(parts_done.sem, when(parts_done, group, 2 * 2, 2 * half + 1))
                pe.matmul(shift_ps[0:SR, 0:P], negmax_parts[:, half].rearrange("p s h t -> p (s h t)"), ident_b[:, :],
                          start=True, stop=True).then_inc(shift_ready.sem, 1)

            def shifted_score(group, i):
                slot, n, h = group[1], i // HG, i % HG
                c, kt = SETS[n]
                q0 = first_query(c, kt)
                if n == 0 and h % HALF == 0:
                    shift_there(pe, group, h // HALF)
                pe.wait_ge(exp_done.sem, when(exp_done, group, NS * HG, i - 3))
                pe.matmul(st_ps[i % 3][:, q0:CH], k_stack[0:STK + SHIFT, slot, h, kt * P:(kt + 1) * P],
                          q_stack[0:STK + SHIFT, slot, h, c * CH + q0:(c + 1) * CH],
                          start=True, stop=True).then_inc(st_ready.sem, 1)

            def add_values(group, n):
                r, slot = group
                c, kt = SETS[n]
                q0 = first_query(c, kt)
                pe.wait_ge(exp_done.sem, when(exp_done, group, NS * HG, n * HG + HG - 1))
                if n in DIAGONAL:
                    pe.wait_ge(masked.sem, when(masked, group, len(DIAGONAL), DIAGONAL.index(n)))
                if kt == 0:
                    pe.wait_ge(o_copied.sem, when(o_copied, group, NC, c - 1))
                for h in range(HG):
                    mm = pe.matmul(o_ps[h * VW:(h + 1) * VW, q0:CH], v_sb[:, slot, kt, h * VW:(h + 1) * VW],
                                   probs[:, n % 3, h, q0:CH], start=kt == 0, stop=kt == (c + 1) * TC - 1,
                                   tile_position=(0, h * VW))
                mm.then_inc(pv_done.sem, 1)

            def turn_output(group, c):
                pe.wait_ge(o_copied.sem, when(o_copied, group, NC, c))
                for j in range(TC):
                    mm = pe.transpose(ot_ps[:, j * P:(j + 1) * P], o_sb[:, c, j * P:(j + 1) * P], ident[:, :])
                mm.then_inc(ot_ready.sem, 1)

            def first(group):
                loaded(group)
                for i in range(NP * HG):
                    score_piece(group, i)
                shift_rows(group, 0)
                pe.wait_ge(shift_copied.sem, when(shift_copied, group, 2, 0))
                shift_rows(group, 1)

            def group_work(group, previous, following):
                if following:
                    loaded(following)
                piece = 0
                for i in range(NS * HG):
                    n = i // HG
                    shifted_score(group, i)
                    if following:
                        for _ in range(PIECES_AT[i]):
                            score_piece(following, piece)
                            piece += 1
                        if i in SHIFT_AT:
                            pe.wait_ge(att_ready.sem, when(att_ready, group, NC, SHIFT_AT[i] - 1))
                            shift_rows(following, SHIFT_AT[i])
                    if i % HG == HG - 1:
                        if n >= 1:
                            add_values(group, n - 1)
                        elif previous:
                            add_values(previous, NS - 1)
                        if n == 2 and previous:
                            pe.wait_ge(shift_copied.sem, when(shift_copied, group, 2, 1))
                            turn_output(previous, 1)
                        if n == 7:
                            if following:
                                pe.wait_ge(shift_copied.sem, when(shift_copied, following, 2, 0))
                            else:
                                pe.wait_ge(att_ready.sem, when(att_ready, group, NC, -1))
                            turn_output(group, 0)
                if not following:
                    add_values(group, NS - 1)
                    pe.wait_ge(att_ready.sem, when(att_ready, group, NC, 0))
                    turn_output(group, 1)

            groups(pe, group_work, first)

        @block.scalar
        def _(act):
            for c in (exp_done, o_copied):
                act.sem_inc(c.sem, c.credit)

            def copy_shift(group, half):
                act.wait_ge(shift_ready.sem, when(shift_ready, group, 2, half))
                act.copy(shift_sb[:, half, :], shift_ps[0:SR, 0:P]).then_inc(shift_copied.sem, 1)

            def exponential(group, i):
                n, h = i // HG, i % HG
                q0 = first_query(*SETS[n])
                if h == 0:
                    act.wait_ge(pv_done.sem, when(pv_done, group, NS, n - 3))
                act.wait_ge(st_ready.sem, when(st_ready, group, NS * HG, i))
                act.activation(probs[:, n % 3, h, q0:CH], st_ps[i % 3][:, q0:CH], ACT.Exp).then_inc(exp_done.sem, 1)

            def copy_output(group, c):
                act.wait_ge(pv_done.sem, when(pv_done, group, NS, (NS if c else TC) - 1))
                act.copy(o_sb[:, c, :], o_ps[:, :]).then_inc(o_copied.sem, 1)

            def first(group):
                copy_shift(group, 0)
                copy_shift(group, 1)

            def group_work(group, previous, following):
                for i in range(NS * HG):
                    if i == HG + 1 and previous:
                        copy_output(previous, 1)
                    if i == 5 * HG + 1:
                        copy_output(group, 0)
                    exponential(group, i)
                    if following and i in SHIFT_AT:
                        copy_shift(following, SHIFT_AT[i])
                if not following:
                    copy_output(group, 1)

            groups(act, group_work, first)

        @block.vector
        def _(dve):
            for c in (piece_done, att_ready):
                dve.sem_inc(c.sem, c.credit)

            def reduce_piece(group, i):
                h, (qt, k0, kw) = i // NP, PIECES[i % NP]
                dve.wait_ge(s_ready.sem, when(s_ready, group, NP * HG, i))
                dve.tensor_reduce(piece_negmax[:, h, i % NP:i % NP + 1], s_ps[i % 3][:, 0:kw], AX.X, ALU.max,
                                  negate=True).then_inc(piece_done.sem, 1)
                if (i + 1) % (NP * HALF) == 0:
                    join(group, h // HALF)

            def join(group, half):
                h = slice(half * HALF, (half + 1) * HALF)
                dve.wait_ge(piece_done.sem, when(piece_done, group, NP * HG, (half + 1) * HALF * NP - 1))
                dve.tensor_copy(negmax[:, h, 0:TC], piece_negmax[:, h, 0:TC]).then_inc(joined.sem, 1)
                dve.tensor_tensor(negmax[:, h, TC:NT], piece_negmax[:, h, TC:NP:2], piece_negmax[:, h, TC + 1:NP:2],
                                  ALU.min).then_inc(joined.sem, 1)
                dve.wait_ge(joined.sem, when(joined, group, 2 * 2, 2 * half + 1))
                dve.wait_ge(shift_ready.sem, when(shift_ready, group, 2, half - 2))
                dve.tensor_copy(negmax_parts[:, half, 0], negmax[:, h, :]).then_inc(parts_done.sem, 1)
                dve.wait_ge(parts_done.sem, when(parts_done, group, 2 * 2, 2 * half))
                dve.tensor_tensor(negmax_parts[:, half, 1], negmax[:, h, :], negmax_parts[:, half, 0],
                                  ALU.subtract).then_inc(parts_done.sem, 1)

            def normalise(group, c):
                ot = ot_ps[:, :].rearrange("p (t h w) -> p t h w", t=TC, h=HG)
                dve.wait_ge(ot_ready.sem, when(ot_ready, group, NC, c))
                dve.reciprocal(inv_sum[:, c], ot[:, :, :, HD1]).then_inc(summed.sem, 1)
                dve.wait_ge(summed.sem, when(summed, group, NC, c))
                dve.wait_ge(att_stored[c], (group[0] * SLOTS + group[1]) * 16 + 16)
                dve.tensor_tensor(att[:, c], ot[:, :, :, 0:HD1],
                                  inv_sum[:, c].unsqueeze(3).to_broadcast([P, TC, HG, HD1]),
                                  ALU.mult).then_inc(att_ready.sem, 1)

            def first(group):
                for i in range(NP * HG):
                    reduce_piece(group, i)

            def group_work(group, previous, following):
                piece = 0
                for i in range(NS * HG):
                    if following:
                        for _ in range(PIECES_AT[i]):
                            reduce_piece(following, piece)
                            piece += 1
                    if i == 2 * HG + HG - 1 and previous:
                        normalise(previous, 1)
                    if i == 7 * HG + HG - 1:
                        normalise(group, 0)
                if not following:
                    normalise(group, 1)

            groups(dve, group_work, first)

        @block.gpsimd
        def _(pool):
            pool.memset(k_stack[STK:STK + SHIFT, :, :, :], 1.0).then_inc(shift_ones, 1)

            def group_work(group, previous, following):
                for n in DIAGONAL:
                    q0 = first_query(*SETS[n])
                    wait_apart(pool, passed, exp_done.sem, when(exp_done, group, NS * HG, n * HG + HG - 1))
                    diagonal = probs[:, n % 3, :, q0:q0 + P]
                    pool.affine_select(out=diagonal, in_=diagonal, compare_op=ALU.is_ge, fill=0.0, base=0,
                                       pattern=[[0, HG], [1, P]], channel_multiplier=-1).then_inc(masked.sem, 1)

            groups(pool, group_work, lambda group: None)


def project_causal(nc, x_all, ident, neg_half, passed, a):
    with ExitStack() as ctx:
        sb = lambda name, shape, dt=F32: ctx.enter_context(nc.sbuf_tensor(name, shape, dt))
        ps = lambda name: ctx.enter_context(nc.psum_tensor(name, [P, CH], F32))
        sem = lambda name: ctx.enter_context(nc.semaphore(name))
        count = lambda name, credit=0, per=NT: Count(sem(name), per, credit)

        w_o = sb("w_o", [P, KD, D])
        b_o = sb("b_o", [P, D])
        att = sb("att_in", [P, 4, NG, GF])
        att_t = sb("att_t", [P, 2, KD, P])
        x_bias = sb("x_bias", [P, 2, D])
        x1 = sb("x1", [P, 4, D])
        stats = sb("stats1", [P, 2, 6])
        mean_var = sb("mean_var1", [P, 4, 2])
        var_eps = sb("var_eps1", [P, 2])
        rstd = sb("rstd1", [P, 4])
        xn = sb("xn1", [P, 2, D])
        xn_t = sb("xn1_t", [P, NC, KD, CH])
        at_ps = [ps(f"at_ps{i}") for i in range(2)]
        y_ps = [ps(f"y_ps{i}") for i in range(2)]
        xt_ps = [ps(f"xt_ps{i}") for i in range(2)]

        weights_in = sem("w_o_in")
        att_in = [sem(f"att_in{i}") for i in range(4)]
        at_ready = count("at_ready", 4)
        att_t_ready = count("att_t_ready", 2)
        y_ready = count("y_ready", 2)
        x_bias_ready = count("x_bias_ready")
        x1_ready = count("x1_ready", 2)
        counted = count("counted1")
        averaged = count("averaged1")
        var_ready = count("var_ready1")
        rstd_ready = count("rstd_ready1")
        xn_ready = count("xn1_ready", 4)
        xt_ready = count("xt_ready", 2)
        xt_copied = count("xt_copied", 2)
        x1_stored = [sem(f"x1_stored{i}") for i in range(4)]
        xt_stored = [sem(f"xt_stored{i}") for i in range(NC)]
        block = ctx.enter_context(nc.Block())

        @block.sync
        def _(sp):
            sp.dma_start(w_o[:, :, :], a["wo"].rearrange("(k p) n -> p k n", p=P)).then_inc(weights_in, 16)
            sp.dma_start(b_o[:, :], a["bo"].partition_broadcast(P)).then_inc(weights_in, 16)
            for s in x1_stored + xt_stored:
                sp.sem_inc(s, 16)

            def load(i):
                b, t = i // NT, i % NT
                sp.wait_ge(at_ready.sem, at_ready.of(b, t - 4))
                sp.dma_start(att[:, t % 4], a["att_scratch"][b * NG:(b + 1) * NG, t * P:(t + 1) * P, :]
                             .rearrange("g p n -> p g n")).then_inc(att_in[t % 4], 16)

            for i in range(4):
                load(i)
            for i in range(B * NT):
                b, t = i // NT, i % NT
                sp.wait_ge(x1_ready.sem, x1_ready.of(b, t))
                sp.dma_start(a["x1_scratch"][b, t * P:(t + 1) * P, :], x1[:, t % 4]).then_inc(x1_stored[t % 4], 16)
                if i + 4 < B * NT:
                    load(i + 4)
                if t % TC == TC - 1:
                    c = t // TC
                    sp.wait_ge(xt_copied.sem, xt_copied.of(b, t))
                    sp.dma_start(a["xt_scratch"][b, :, :, c * CH:(c + 1) * CH].rearrange("k p t -> p k t"),
                                 xn_t[:, c]).then_inc(xt_stored[c], 16)
            for s in x1_stored:
                sp.wait_ge(s, 16 * (B * NT // 4 + 1))
            for s in xt_stored:
                sp.wait_ge(s, 16 * (B + 1))

        @block.tensor
        def _(pe):
            for c in (at_ready, y_ready, xt_ready):
                pe.sem_inc(c.sem, c.credit)
            pe.wait_ge(weights_in, 32)
            with pe.Fori(0, B) as b:
                def turn_att(t):
                    pe.wait_ge(att_in[t % 4], b * (16 * NT // 4) + 16 * (t // 4 + 1))
                    pe.wait_ge(att_t_ready.sem, att_t_ready.of(b, t - 2))
                    for k in range(KD):
                        mm = pe.transpose(at_ps[t % 2][:, k * P:(k + 1) * P], att[:, t % 4, 2 * k:2 * k + 2, :], ident[:, :])
                    mm.then_inc(at_ready.sem, 1)

                def project(t):
                    pe.wait_ge(att_t_ready.sem, att_t_ready.of(b, t))
                    pe.wait_ge(x1_ready.sem, x1_ready.of(b, t - 2))
                    for k in range(KD):
                        mm = pe.matmul(y_ps[t % 2][:, 0:D], att_t[:, t % 2, k, :], w_o[:, k, :],
                                       start=k == 0, stop=k == KD - 1)
                    mm.then_inc(y_ready.sem, 1)

                def turn_x(t):
                    pe.wait_ge(xn_ready.sem, xn_ready.of(b, t))
                    pe.wait_ge(xt_copied.sem, xt_copied.of(b, t - 2))
                    for k in range(KD):
                        mm = pe.transpose(xt_ps[t % 2][:, k * P:(k + 1) * P], xn[:, t % 2, k * P:(k + 1) * P], ident[:, :])
                    mm.then_inc(xt_ready.sem, 1)

                for s in range(NT + 3):
                    if s < NT:
                        turn_att(s)
                    if 1 <= s <= NT:
                        project(s - 1)
                    if s >= 3:
                        turn_x(s - 3)

        @block.scalar
        def _(act):
            for c in (att_t_ready, xt_copied):
                act.sem_inc(c.sem, c.credit)
            with act.Fori(0, B) as b:
                for s in range(NT + 3):
                    if s < NT:
                        act.wait_ge(at_ready.sem, at_ready.of(b, s))
                        act.wait_ge(y_ready.sem, y_ready.of(b, s - 2))
                        act.copy(att_t[:, s % 2], at_ps[s % 2][:, 0:D].rearrange("p (k t) -> p k t", k=KD))\
                           .then_inc(att_t_ready.sem, 1)
                    if s >= 3:
                        t = s - 3
                        c = t // TC
                        act.wait_ge(xt_ready.sem, xt_ready.of(b, t))
                        act.wait_ge(xt_stored[c], b * 16 + 16)
                        act.copy(xn_t[:, c, :, (t % TC) * P:(t % TC + 1) * P],
                                 xt_ps[t % 2][:, 0:D].rearrange("p (k t) -> p k t", k=KD)).then_inc(xt_copied.sem, 1)

        @block.gpsimd
        def _(pool):
            pool.wait_ge(weights_in, 32)
            with pool.Fori(0, B) as b:
                for s in range(NT + 1):
                    if s < NT:
                        pool.wait_ge(x1_ready.sem, x1_ready.of(b, s - 2))
                        pool.tensor_tensor(x_bias[:, s % 2, :].unsqueeze(1), x_all[:, bass.ds(b * NT + s, 1), :],
                                           b_o[:, :].unsqueeze(1), ALU.add).then_inc(x_bias_ready.sem, 1)
                    if s >= 1:
                        t = s - 1
                        wait_apart(pool, passed, averaged.sem, averaged.of(b, t))
                        pool.tensor_scalar(var_eps[:, t % 2:t % 2 + 1], mean_var[:, t % 4, 1:2], EPS, None, ALU.add)\
                            .then_inc(var_ready.sem, 1)
                        pool.wait_ge(xn_ready.sem, xn_ready.of(b, t - 4))
                        pool.wait_ge(var_ready.sem, var_ready.of(b, t))
                        pool.tensor_tensor(rstd[:, t % 4:t % 4 + 1], var_eps[:, t % 2:t % 2 + 1], neg_half[:, 0:1],
                                           ALU.pow).then_inc(rstd_ready.sem, 1)

        @block.vector
        def _(dve):
            for c in (x1_ready, xn_ready):
                dve.sem_inc(c.sem, c.credit)
            with dve.Fori(0, B) as b:
                def residual(t):
                    dve.wait_ge(x_bias_ready.sem, x_bias_ready.of(b, t))
                    dve.wait_ge(y_ready.sem, y_ready.of(b, t))
                    dve.wait_ge(x1_stored[t % 4], b * (16 * NT // 4) + 16 * (t // 4 + 1))
                    dve.tensor_tensor(x1[:, t % 4, :], y_ps[t % 2][:, 0:D], x_bias[:, t % 2, :], ALU.add)\
                       .then_inc(x1_ready.sem, 1)
                    dve.wait_ge(x1_ready.sem, x1_ready.of(b, t))
                    dve.bn_stats(stats[:, t % 2, :], x1[:, t % 4, :]).then_inc(counted.sem, 1)
                    wait_apart(dve, passed, counted.sem, counted.of(b, t))
                    dve.bn_aggr(mean_var[:, t % 4, :], stats[:, t % 2, :]).then_inc(averaged.sem, 1)

                def normalise(t):
                    dve.wait_ge(rstd_ready.sem, rstd_ready.of(b, t))
                    dve.wait_ge(xt_ready.sem, xt_ready.of(b, t - 2))
                    dve.tensor_scalar(xn[:, t % 2, :], x1[:, t % 4, :], mean_var[:, t % 4, 0:1], rstd[:, t % 4:t % 4 + 1],
                                      ALU.subtract, ALU.mult).then_inc(xn_ready.sem, 1)

                for s in range(NT + 1):
                    if s < NT:
                        residual(s)
                    if s >= 1:
                        normalise(s - 1)



PAIRS = H2 // 2
PW = 2 * WIN
WPC = CH // WIN
UNITS = NT * PAIRS
GROUPS = UNITS // 2
AHEAD = 3
HT = -(-HID // P)
HL = HID - (HT - 1) * P
LAST = DEPTH * B - 1


def place(u, h):
    q = u % PAIRS
    return q // 2 * 2 + h, q % 2


def layers(nc, ident, neg_half, passed, a):
    with ExitStack() as ctx:
        sb = lambda name, shape, dt=F32: ctx.enter_context(nc.sbuf_tensor(name, shape, dt))
        sem = lambda name: ctx.enter_context(nc.semaphore(name))
        count = lambda name, per, credit=0: Count(sem(name), per, credit)
        qkv_ps = ctx.enter_context(nc.psum_tensor("qkv_ps", [P, 3 * CH], F32))
        turn_ps, s0, s1, pt_ps, o_ps = [ctx.enter_context(nc.psum_tensor(n, [P, CH], F32))
                                        for n in ("turn_ps2", "s2_ps0", "s2_ps1", "pt_ps2", "o_ps2")]
        q_ps, v_ps, s_ps = qkv_ps[:, 0:2 * CH], qkv_ps[:, 2 * CH:3 * CH], (s0, s1)
        pair = ((s0, s1), (pt_ps, o_ps))
        up_pair = lambda c, j: pair[(c + j) % 2]

        w_qkv = sb("w_qkv", [P, KD, 3 * INNER])
        w_out = sb("w_out", [P, INNER // P, D])
        w_up = sb("w_up", [P, KD, 2 * HID])
        w_down = sb("w_down", [P, HT, D])
        b_up = sb("b_up", [P, 2, HT])
        b_down = sb("b_down", [P, KD])
        ln_g = sb("ln_g", [P, KD])
        ln_b = sb("ln_b", [P, KD])
        head_scale = sb("head_scale", [P, 4, HD2])
        rotary = sb("rotary", [P, NT, 4, HD2])
        turn_by = sb("turn_by", [P, NT, 4, HD2])
        band = sb("band", [P, PW])
        x_in = sb("x_in", [P, KD, T + 1])
        x_mid = sb("x_mid", [P, KD, T + 1])
        squares = sb("squares", [P, 2 * INNER])
        inv_norm = sb("inv_norm", [P, 2 * H2])
        sum_sq = sb("sum_sq", [P, 2, 2 * H2])
        qn = sb("qn", [P, 2 * INNER])
        rot_c = sb("rot_c", [P, 2 * INNER])
        rot_s = sb("rot_s", [P, 2 * INNER])
        q_t = sb("q_t", [P, 2, PAIRS, P])
        k_t = sb("k_t", [P, PAIRS, T])
        v_sb = sb("v_tok", [P, NT, INNER])
        p_sb = sb("p_sb", [P, 4, 2, PW])
        negmax = sb("negmax2", [P, 4, 2])
        total = sb("total", [P, 4, 2])
        inv_total = sb("inv_total", [P, 4, 2])
        p_t = sb("p_t", [P, 4, 2, 2, P])
        o_t = sb("o_t", [P, PAIRS, T])
        stats = sb("stats2", [P, NT, 6])
        mean_var = sb("mean_var2", [P, NT, 2])
        var_eps = sb("var_eps2", [P, NT])
        rstd = sb("rstd2", [P, NT])
        hn = sb("hn", [P, NT, D])
        hn_t = sb("hn_t", [P, NC, KD, CH])
        gate = sb("gate", [P, 2, CH])
        hidden = sb("hidden", [P, HT, CH])
        x_out = sb("x_out", [P, KD, CH])

        qkv_weights_in = sem("qkv_weights_in")
        ffn_weights_in = sem("ffn_weights_in")
        qkv_go = count("qkv_go", 1)
        ffn_go = count("ffn_go", 1)
        x_loaded = sem("x_loaded")
        pads = sem("pads")
        scaled_tables = count("scaled_tables", 1, 1)
        q_ready = count("q_ready", NT)
        v_ready = count("v_ready2", NT, 1)
        squared = count("squared", NT, 1)
        v_copied = count("v_copied2", NT, 1)
        summed = count("summed2", NT)
        clamped = count("clamped", NT, 1)
        inv_ready = count("inv_ready", NT)
        qn_ready = count("qn_ready", NT, 1)
        cos_ready = count("cos_ready", NT, 1)
        sin_ready = count("sin_ready", 4 * NT, 4)
        rot_ready = count("rot_ready", NT, 2)
        turned = count("turned2", 2 * NT, 4)
        turn_copied = count("turn_copied", 2 * NT, 1)
        s_ready = count("s_ready2", UNITS, 8)
        s_masked = count("s_masked", 2 * UNITS, 4)
        exp_done = count("exp_done2", 2 * UNITS)
        inv_sum = count("inv_sum", UNITS)
        scaled = count("scaled", 2 * UNITS)
        pt_ready = count("pt_ready", UNITS, 4)
        pt_copied = count("pt_copied", UNITS, 1)
        pv_done = count("pv_done2", GROUPS, 2)
        o_copied = count("o_copied2", NT, 1)
        wo_ready = count("wo_ready", NC * KD, 4)
        mid_ready = count("mid_ready2", NC * KD, 4)
        ln_ready = count("ln_ready", NC * 2)
        counted = count("counted2", NT)
        averaged = count("averaged2", NT)
        var_ready = count("var_ready2", NC)
        rstd_ready = count("rstd_ready2", NC)
        hn_ready = count("hn_ready", NT)
        back_ready = count("back_ready", NC * KD)
        hn_t_ready = count("hn_t_ready", NC * KD)
        up_ready = count("up_ready", NC * HT)
        gelu_done = count("gelu_done", NC * HT)
        hidden_ready = count("hidden_ready", NC * HT, 2)
        down_ready = count("down_ready", NC * KD)
        out_ready = count("out_ready", NC * KD, 2)
        out_stored = [sem(f"out_stored{k}") for k in range(KD)]
        block = ctx.enter_context(nc.Block())

        @block.sync
        def _(sp):
            def load_qkv_weights(l):
                dmas = [(w_qkv[:, :, :], a["wqkv"][l].rearrange("(k p) n -> p k n", p=P))]
                half = HD2 // 2
                for j, name in ((0, "q_scale"), (2, "k_scale")):
                    dmas += [(head_scale[:, j, :], a[name][l].partition_broadcast(P)),
                             (head_scale[:, j + 1, 0:half], a[name][l, half:HD2].partition_broadcast(P)),
                             (head_scale[:, j + 1, half:HD2], a[name][l, 0:half].partition_broadcast(P))]
                for dst, src in dmas:
                    sp.dma_start(dst, src).then_inc(qkv_weights_in, 16)
                return 16 * len(dmas)

            def load_ffn_weights(l):
                dmas = [(w_out[:, :, :], a["wo2"][l].rearrange("(k p) n -> p k n", p=P)),
                        (w_up[:, :, :], a["w1"][l].rearrange("(k p) n -> p k n", p=P)),
                        (w_down[:, 0:HT - 1, :], a["w2"][l, 0:(HT - 1) * P, :].rearrange("(k p) n -> p k n", p=P)),
                        (w_down[0:HL, HT - 1, :], a["w2"][l, (HT - 1) * P:HID, :])]
                for j in range(2):
                    whole = a["b1"][l, j * HID:j * HID + (HT - 1) * P]
                    rest = a["b1"][l, j * HID + (HT - 1) * P:(j + 1) * HID]
                    dmas += [(b_up[:, j, 0:HT - 1], whole.rearrange("(k p) -> p k", p=P)),
                             (b_up[0:HL, j, HT - 1:HT], rest.rearrange("(p k) -> p k", k=1))]
                dmas += [(dst[:, :], a[name][l].rearrange("(k p) -> p k", p=P))
                         for dst, name in ((b_down, "b2"), (ln_g, "ln_g"), (ln_b, "ln_b"))]
                for dst, src in dmas:
                    sp.dma_start(dst, src, allow_slow_non_contiguous=True).then_inc(ffn_weights_in, 16)
                return 16 * len(dmas)

            def load_x(it):
                if it >= B:
                    for s in out_stored:
                        sp.wait_ge(s, 16 * (NC * (it - B + 1) + 1))
                for k in range(KD):
                    sp.dma_start(x_in[:, k, k:k + T], a["xt_scratch"][it % B, k]).then_inc(x_loaded, 16)

            for s in out_stored:
                sp.sem_inc(s, 16)
            load_x(0)
            per_layer = load_qkv_weights(0)
            sp.dma_start(rotary[:, :, :, :].rearrange("p t j d -> p t (j d)"),
                         a["rotary"].rearrange("(t p) j d -> p t (j d)", p=P)).then_inc(qkv_weights_in, 16)
            sp.wait_ge(x_loaded, 16 * KD)
            sp.wait_ge(qkv_weights_in, per_layer + 16)
            sp.sem_inc(qkv_go.sem, 1)
            per_layer_ffn = load_ffn_weights(0)
            for it in range(DEPTH * B):
                layer_ends = it == B - 1
                if it % B == 0:
                    sp.wait_ge(ffn_weights_in, per_layer_ffn * (it // B + 1))
                sp.sem_inc(ffn_go.sem, 1)
                if layer_ends:
                    sp.wait_ge(v_ready.sem, v_ready.of(it, NT - 1))
                    load_qkv_weights(1)
                if it < LAST:
                    sp.wait_ge(mid_ready.sem, mid_ready.of(it, NC * KD - 1))
                    load_x(it + 1)
                    sp.wait_ge(x_loaded, 16 * KD * (it + 2))
                    if layer_ends:
                        sp.wait_ge(qkv_weights_in, 2 * per_layer + 16)
                    sp.sem_inc(qkv_go.sem, 1)
                for c in range(NC):
                    for k in range(KD):
                        sp.wait_ge(out_ready.sem, out_ready.of(it, c * KD + k))
                        sp.dma_start(a["xt_scratch"][it % B, k, :, c * CH:(c + 1) * CH], x_out[:, k, :])\
                            .then_inc(out_stored[k], 16)
                if layer_ends:
                    load_ffn_weights(1)
            for s in out_stored:
                sp.wait_ge(s, 16 * (NC * DEPTH * B + 1))

        @block.tensor
        def _(pe):
            for c in (v_ready, turned, s_ready, pt_ready, pv_done, wo_ready):
                pe.sem_inc(c.sem, c.credit)
            pe.wait_ge(pads, 3)

            def project(it, w, part):
                if w == 0 and part == 0:
                    pe.wait_ge(qkv_go.sem, qkv_go.of(it, 0))
                if part < 2:
                    pe.wait_ge(qn_ready.sem, qn_ready.of(it, w - 1))
                else:
                    pe.wait_ge(v_copied.sem, v_copied.of(it, w - 1))
                for k in range(KD):
                    mm = pe.matmul(qkv_ps[:, part * CH:(part + 1) * CH], x_in[:, k, w * P:(w + 1) * P],
                                   w_qkv[:, k, part * INNER:(part + 1) * INNER], start=k == 0, stop=k == KD - 1)
                if part == 1:
                    mm.then_inc(q_ready.sem, 1)
                if part == 2:
                    mm.then_inc(v_ready.sem, 1)

            def turn(it, w, j):
                pe.wait_ge(rot_ready.sem, rot_ready.of(it, w))
                pe.wait_ge(turn_copied.sem, turn_copied.of(it, 2 * w + j - 1))
                for p in range(PAIRS):
                    mm = pe.transpose(turn_ps[:, p * P:(p + 1) * P],
                                      rot_c[:, j * INNER + p * P:j * INNER + (p + 1) * P], ident[:, :])
                mm.then_inc(turned.sem, 1)

            def attention(it):
                def scores(u):
                    w = u // PAIRS
                    pe.wait_ge(turn_copied.sem, turn_copied.of(it, 2 * w + 1))
                    pe.wait_ge(s_masked.sem, s_masked.of(it, 2 * u - 3))
                    if u == 0:
                        pe.wait_ge(hidden_ready.sem, hidden_ready.of(it, -1))
                    k0 = max(0, w - 1) * P
                    for h in range(2):
                        p, side = place(u, h)
                        r = slice(side * HD2, (side + 1) * HD2)
                        mm = pe.matmul(s_ps[u % 2][:, (h + 1) * PW - ((w + 1) * P - k0):(h + 1) * PW],
                                       q_t[r, w % 2, p, :], k_t[r, p, k0:(w + 1) * P], start=True, stop=True)
                    mm.then_inc(s_ready.sem, 1)

                def turn_probs(u):
                    w = u // PAIRS
                    pe.wait_ge(scaled.sem, scaled.of(it, 2 * u + 1))
                    pe.wait_ge(pt_copied.sem, pt_copied.of(it, u - 1))
                    if u == 0:
                        pe.wait_ge(out_ready.sem, out_ready.of(it, -1))
                    for h in range(2):
                        for kt in range(0 if w else 1, 2):
                            mm = pe.transpose(pt_ps[:, (h * 2 + kt) * P:(h * 2 + kt + 1) * P],
                                              p_sb[:, u % 4, h, kt * P:(kt + 1) * P], ident[:, :])
                    mm.then_inc(pt_ready.sem, 1)

                def values(g):
                    w = 2 * g // PAIRS
                    pe.wait_ge(pt_copied.sem, pt_copied.of(it, 2 * g + 1))
                    pe.wait_ge(v_copied.sem, v_copied.of(it, w))
                    if 2 * g % PAIRS == 0:
                        pe.wait_ge(o_copied.sem, o_copied.of(it, w - 1))
                    for h in range(2):
                        for kt in range(0 if w else 1, 2):
                            for u in (2 * g, 2 * g + 1):
                                p, side = place(u, h)
                                head = 2 * p + side
                                mm = pe.matmul(o_ps[side * HD2:(side + 1) * HD2, p * P:(p + 1) * P],
                                               v_sb[:, w - 1 + kt, head * HD2:(head + 1) * HD2],
                                               p_t[:, u % 4, h, kt, :], start=kt == (0 if w else 1), stop=kt == 1,
                                               tile_position=(0, side * HD2))
                    mm.then_inc(pv_done.sem, 1)

                for u in range(UNITS + 3):
                    w, p = u // PAIRS, u % PAIRS
                    if u < UNITS:
                        scores(u)
                    if 2 <= u < UNITS + 2:
                        turn_probs(u - 2)
                    if p < 2 and w + 1 < NT:
                        turn(it, w + 1, p)
                    if p >= 1 and w + AHEAD < NT:
                        project(it, w + AHEAD, p - 1)
                    if u >= 4 and u % 2 == 0:
                        values((u - 4) // 2)

            def feed_forward(it, more):
                def project_out(c, m):
                    if c == 0 and m == 0:
                        pe.wait_ge(ffn_go.sem, ffn_go.of(it, 0))
                        pe.wait_ge(s_masked.sem, s_masked.of(it, 2 * UNITS - 1))
                    if c == 1:
                        pe.wait_ge(pt_copied.sem, pt_copied.of(it, UNITS - 1))
                    pe.wait_ge(o_copied.sem, o_copied.of(it, (c + 1) * WPC - 1))
                    for k in range(INNER // P):
                        mm = pe.matmul(pair[c][m][:, :], w_out[:, k, m * P:(m + 1) * P],
                                       o_t[:, k, c * CH:(c + 1) * CH], start=k == 0, stop=k == INNER // P - 1)
                    mm.then_inc(wo_ready.sem, 1)

                def tokens_first(c):
                    pe.wait_ge(mid_ready.sem, mid_ready.of(it, (c + 1) * KD - 1))
                    for t in range(TC):
                        for k in range(KD):
                            mm = pe.transpose(pair[c][t // 2][:, (t % 2) * D + k * P:(t % 2) * D + (k + 1) * P],
                                              x_mid[:, k, c * CH + t * P:c * CH + (t + 1) * P], ident[:, :])
                        if t % 2:
                            mm.then_inc(ln_ready.sem, 1)

                def features_first(c):
                    pe.wait_ge(hn_ready.sem, hn_ready.of(it, (c + 1) * TC - 1))
                    for k in range(KD):
                        for t in range(TC):
                            mm = pe.transpose(pair[c][k][:, t * P:(t + 1) * P], hn[:, c * TC + t, k * P:(k + 1) * P],
                                              ident[:, :])
                        mm.then_inc(back_ready.sem, 1)

                def up(c, j):
                    i = c * HT + j
                    pe.wait_ge(hn_t_ready.sem, hn_t_ready.of(it, (c + 1) * KD - 1))
                    if i == 1:
                        pe.wait_ge(hn_t_ready.sem, hn_t_ready.of(it, 2 * KD - 1))
                    elif i == HT:
                        pe.wait_ge(hidden_ready.sem, hidden_ready.of(it, i - 1))
                    elif i == HT + 1:
                        pe.wait_ge(out_ready.sem, out_ready.of(it, KD - 1))
                    elif i > 1:
                        pe.wait_ge(hidden_ready.sem, hidden_ready.of(it, i - 2))
                    rows = P if j < HT - 1 else HL
                    for part in range(2):
                        f0 = part * HID + j * P
                        for k in range(KD):
                            mm = pe.matmul(up_pair(c, j)[part][0:rows, :], w_up[:, k, f0:f0 + rows], hn_t[:, c, k, :],
                                           start=k == 0, stop=k == KD - 1)
                    mm.then_inc(up_ready.sem, 1)

                def down(c, m):
                    pe.wait_ge(hidden_ready.sem, hidden_ready.of(it, (c + 1) * HT - 1))
                    for j in range(HT):
                        rows = P if j < HT - 1 else HL
                        mm = pe.matmul(pair[c][m][:, :], w_down[0:rows, j, m * P:(m + 1) * P], hidden[0:rows, j, :],
                                       start=j == 0, stop=j == HT - 1)
                    mm.then_inc(down_ready.sem, 1)

                for c in range(NC):
                    for m in range(KD):
                        project_out(c, m)
                tokens_first(0)
                tokens_first(1)
                features_first(0)
                up(0, 0)
                features_first(1)
                up(0, 1)
                if more:
                    for part in range(3):
                        project(it + 1, 0, part)
                for j in range(2, HT):
                    up(0, j)
                if more:
                    for part in range(3):
                        project(it + 1, 1, part)
                down(0, 0)
                down(0, 1)
                up(1, 0)
                if more:
                    turn(it + 1, 0, 0)
                up(1, 1)
                if more:
                    turn(it + 1, 0, 1)
                    for part in range(3):
                        project(it + 1, 2, part)
                for j in range(2, HT):
                    up(1, j)
                down(1, 0)
                down(1, 1)

            for w in range(AHEAD):
                for part in range(3):
                    project(0, w, part)
                if w == 0:
                    turn(0, 0, 0)
                    turn(0, 0, 1)
            with pe.Fori(0, LAST) as it:
                attention(it)
                feed_forward(it, True)
            attention(LAST)
            feed_forward(LAST, False)

        @block.scalar
        def _(act):
            for c in (squared, v_copied, turn_copied, pt_copied, o_copied):
                act.sem_inc(c.sem, c.credit)

            def square(it, w):
                act.wait_ge(q_ready.sem, q_ready.of(it, w))
                act.wait_ge(clamped.sem, clamped.of(it, w - 1))
                act.activation(squares[:, :], q_ps, ACT.Square).then_inc(squared.sem, 1)

            def copy_v(it, w):
                act.wait_ge(v_ready.sem, v_ready.of(it, w))
                act.copy(v_sb[:, w, :], v_ps).then_inc(v_copied.sem, 1)

            def copy_turned(it, w, j):
                act.wait_ge(turned.sem, turned.of(it, 2 * w + j))
                if j == 0:
                    act.wait_ge(s_ready.sem, s_ready.of(it, (w - 1) * PAIRS - 1))
                dst = q_t[:, w % 2, :, :] if j == 0 else k_t[:, :, w * P:(w + 1) * P]
                act.copy(dst, turn_ps[:, :].rearrange("p (h t) -> p h t", h=PAIRS)).then_inc(turn_copied.sem, 1)

            def attention(it):
                def exponentials(u):
                    k0 = 0 if u // PAIRS else WIN
                    for h in range(2):
                        act.wait_ge(s_masked.sem, s_masked.of(it, 2 * u + h))
                        act.activation(p_sb[:, u % 4, h, k0:PW], p_sb[:, u % 4, h, k0:PW], ACT.Exp, scale=-1.0,
                                       bias=negmax[:, u % 4, h:h + 1],
                                       accum_out=total[:, u % 4, h:h + 1]).then_inc(exp_done.sem, 1)

                def copy_probs(u):
                    k0 = 0 if u // PAIRS else 1
                    act.wait_ge(pt_ready.sem, pt_ready.of(it, u))
                    act.wait_ge(pv_done.sem, pv_done.of(it, u // 2 - 2))
                    act.copy(p_t[:, u % 4, :, k0:2, :],
                             pt_ps[:, :].rearrange("p (h k t) -> p h k t", h=2, k=2)[:, :, k0:2, :])\
                       .then_inc(pt_copied.sem, 1)

                def copy_output(w):
                    act.wait_ge(pv_done.sem, pv_done.of(it, (w + 1) * PAIRS // 2 - 1))
                    if w == 0:
                        act.wait_ge(wo_ready.sem, wo_ready.of(it, -1))
                    act.copy(o_t[:, :, w * P:(w + 1) * P], o_ps[:, :].rearrange("p (h t) -> p h t", h=PAIRS))\
                       .then_inc(o_copied.sem, 1)

                for u in range(UNITS + 3):
                    w, p = u // PAIRS, u % PAIRS
                    if 2 <= u < UNITS + 2:
                        copy_probs(u - 2)
                    if u < UNITS:
                        exponentials(u)
                    if p < 2 and w + 1 < NT:
                        copy_turned(it, w + 1, p)
                    if p == 2 and w + AHEAD < NT:
                        square(it, w + AHEAD)
                    if p == 3 and w + AHEAD < NT:
                        copy_v(it, w + AHEAD)
                    if u >= PAIRS + 2 and (u - 2) % PAIRS == 0:
                        copy_output((u - 2) // PAIRS - 1)

            def feed_forward(it, more):
                def scale_norm(c):
                    for k in range(KD):
                        act.wait_ge(back_ready.sem, back_ready.of(it, c * KD + k))
                        act.activation(hn_t[:, c, k, :], pair[c][k][:, :], ACT.Identity, bias=ln_b[:, k:k + 1],
                                       scale=ln_g[:, k:k + 1]).then_inc(hn_t_ready.sem, 1)

                def gelu(c, j):
                    i = c * HT + j
                    rows = P if j < HT - 1 else HL
                    act.wait_ge(up_ready.sem, up_ready.of(it, i))
                    act.wait_ge(hidden_ready.sem, hidden_ready.of(it, i - 2))
                    act.activation(gate[0:rows, i % 2, :], up_pair(c, j)[1][0:rows, :], ACT.Gelu,
                                   bias=b_up[0:rows, 1, j:j + 1]).then_inc(gelu_done.sem, 1)

                scale_norm(0)
                scale_norm(1)
                gelu(0, 0)
                gelu(0, 1)
                if more:
                    square(it + 1, 0)
                    copy_v(it + 1, 0)
                for j in range(2, HT):
                    gelu(0, j)
                if more:
                    square(it + 1, 1)
                    copy_v(it + 1, 1)
                gelu(1, 0)
                if more:
                    copy_turned(it + 1, 0, 0)
                gelu(1, 1)
                if more:
                    copy_turned(it + 1, 0, 1)
                    square(it + 1, 2)
                    copy_v(it + 1, 2)
                for j in range(2, HT):
                    gelu(1, j)

            for w in range(AHEAD):
                square(0, w)
                copy_v(0, w)
                if w == 0:
                    copy_turned(0, 0, 0)
                    copy_turned(0, 0, 1)
            with act.Fori(0, LAST) as it:
                attention(it)
                feed_forward(it, True)
            attention(LAST)
            feed_forward(LAST, False)

        @block.gpsimd
        def _(pool):
            for c in (scaled_tables, clamped, cos_ready, rot_ready):
                pool.sem_inc(c.sem, c.credit)
            pool.memset(x_in[:, 1, 0:1], 0.0).then_inc(pads, 1)
            pool.memset(x_mid[:, 1, 0:1], 0.0).then_inc(pads, 1)
            pool.memset(band[:, :], 0.0).then_inc(pads, 1)
            pool.wait_ge(pads, 3)
            pool.affine_select(out=band[:, 0:WIN], in_=band[:, 0:WIN], compare_op=ALU.is_ge, fill=BIG, base=0,
                               pattern=[[1, WIN]], channel_multiplier=-1).then_inc(pads, 1)
            pool.affine_select(out=band[:, WIN:PW], in_=band[:, WIN:PW], compare_op=ALU.is_ge, fill=BIG, base=0,
                               pattern=[[-1, WIN]], channel_multiplier=1).then_inc(pads, 1)

            def scale_tables(it):
                pool.wait_ge(qkv_go.sem, qkv_go.of(it, 0))
                pool.wait_ge(sin_ready.sem, sin_ready.of(it, -1))
                for w in range(NT):
                    ins = pool.tensor_tensor(turn_by[:, w], rotary[:, w], head_scale[:, :, :], ALU.mult)
                ins.then_inc(scaled_tables.sem, 1)
                pool.wait_ge(scaled_tables.sem, scaled_tables.of(it, 0))

            def norms(it, w):
                wait_apart(pool, passed, summed.sem, summed.of(it, w))
                pool.tensor_scalar(sum_sq[:, 1, :], sum_sq[:, 0, :], 1e-24, None, ALU.max).then_inc(clamped.sem, 1)
                pool.wait_ge(clamped.sem, clamped.of(it, w))
                pool.tensor_tensor(inv_norm[:, :], sum_sq[:, 1, :], neg_half[:, 0:2 * H2], ALU.pow)\
                    .then_inc(inv_ready.sem, 1)

            def rotate(it, w):
                pool.wait_ge(qn_ready.sem, qn_ready.of(it, w))
                pool.wait_ge(turned.sem, turned.of(it, 2 * w - 1))
                heads = lambda t, j: t[:, j * INNER:(j + 1) * INNER].rearrange("p (h d) -> p h d", h=H2)
                for j in range(2):
                    ins = pool.tensor_tensor(heads(rot_c, j), heads(qn, j), turn_by[:, w, 2 * j, :].unsqueeze(1)
                                             .to_broadcast([P, H2, HD2]), ALU.mult)
                ins.then_inc(cos_ready.sem, 1)
                pool.wait_ge(cos_ready.sem, cos_ready.of(it, w))
                pool.wait_ge(sin_ready.sem, sin_ready.of(it, 4 * w + 3))
                pool.tensor_tensor(rot_c[:, :], rot_c[:, :], rot_s[:, :], ALU.add).then_inc(rot_ready.sem, 1)

            def first_windows(it):
                scale_tables(it)
                for w in range(AHEAD):
                    norms(it, w)
                    if w < AHEAD - 1:
                        rotate(it, w)

            def attention(it):
                for w in range(NT):
                    if w + 2 < NT:
                        rotate(it, w + 2)
                    if w + AHEAD < NT:
                        norms(it, w + AHEAD)

            def feed_forward(it, more):
                for c in range(NC):
                    t = slice(c * TC, (c + 1) * TC)
                    wait_apart(pool, passed, averaged.sem, averaged.of(it, (c + 1) * TC - 1))
                    pool.tensor_scalar(var_eps[:, t], mean_var[:, t, 1], EPS, None, ALU.add).then_inc(var_ready.sem, 1)
                    pool.wait_ge(var_ready.sem, var_ready.of(it, c))
                    pool.tensor_tensor(rstd[:, t], var_eps[:, t], neg_half[:, 0:TC], ALU.pow).then_inc(rstd_ready.sem, 1)
                if more:
                    first_windows(it + 1)

            first_windows(0)
            with pool.Fori(0, LAST) as it:
                attention(it)
                feed_forward(it, True)
            attention(LAST)
            feed_forward(LAST, False)

        @block.vector
        def _(dve):
            for c in (qn_ready, sin_ready, s_masked, mid_ready, hidden_ready, out_ready):
                dve.sem_inc(c.sem, c.credit)
            dve.wait_ge(pads, 5)
            heads = lambda t: t.rearrange("p (h d) -> p h d", d=HD2)

            def sums(it, w):
                dve.wait_ge(squared.sem, squared.of(it, w))
                dve.wait_ge(clamped.sem, clamped.of(it, w - 1))
                dve.tensor_reduce(sum_sq[:, 0, :], heads(squares[:, :]), AX.X, ALU.add).then_inc(summed.sem, 1)

            def unit_vectors(it, w):
                dve.wait_ge(inv_ready.sem, inv_ready.of(it, w))
                dve.wait_ge(cos_ready.sem, cos_ready.of(it, w - 1))
                dve.wait_ge(sin_ready.sem, sin_ready.of(it, 4 * w - 1))
                dve.tensor_tensor(heads(qn[:, :]), heads(q_ps), inv_norm[:, :].unsqueeze(2)
                                  .to_broadcast([P, 2 * H2, HD2]), ALU.mult).then_inc(qn_ready.sem, 1)

            def times_sin(it, w):
                if w == 0:
                    dve.wait_ge(scaled_tables.sem, scaled_tables.of(it, 0))
                dve.wait_ge(qn_ready.sem, qn_ready.of(it, w))
                dve.wait_ge(rot_ready.sem, rot_ready.of(it, w - 1))
                half = HD2 // 2
                for j in range(2):
                    src = heads(qn[:, j * INNER:(j + 1) * INNER])
                    dst = heads(rot_s[:, j * INNER:(j + 1) * INNER])
                    for to in range(2):
                        o, i = slice(to * half, (to + 1) * half), slice((1 - to) * half, (2 - to) * half)
                        dve.tensor_tensor(dst[:, :, o], src[:, :, i], turn_by[:, w, 2 * j + 1, o].unsqueeze(1)
                                          .to_broadcast([P, H2, half]), ALU.mult).then_inc(sin_ready.sem, 1)

            def attention(it):
                def mask_scores(u):
                    k0 = 0 if u // PAIRS else WIN
                    for h in range(2):
                        if h == 0:
                            wait_apart(dve, passed, s_ready.sem, s_ready.of(it, u))
                            wait_apart(dve, passed, pt_ready.sem, pt_ready.of(it, u - 4))
                        dve.tensor_tensor_reduce(p_sb[:, u % 4, h, k0:PW], s_ps[u % 2][:, h * PW + k0:(h + 1) * PW],
                                                 band[:, k0:PW], 1.0, BIG, ALU.add, ALU.min,
                                                 negmax[:, u % 4, h:h + 1]).then_inc(s_masked.sem, 1)

                def invert_sums(u):
                    dve.wait_ge(exp_done.sem, exp_done.of(it, 2 * u + 1))
                    dve.reciprocal(inv_total[:, u % 4, :], total[:, u % 4, :]).then_inc(inv_sum.sem, 1)

                def scale_probs(u):
                    k0 = 0 if u // PAIRS else WIN
                    wait_apart(dve, passed, inv_sum.sem, inv_sum.of(it, u))
                    for h in range(2):
                        dve.tensor_scalar(p_sb[:, u % 4, h, k0:PW], p_sb[:, u % 4, h, k0:PW],
                                          inv_total[:, u % 4, h:h + 1], None, ALU.mult).then_inc(scaled.sem, 1)

                for u in range(UNITS + 1):
                    w, p = u // PAIRS, u % PAIRS
                    if u < UNITS:
                        mask_scores(u)
                    if u:
                        invert_sums(u - 1)
                        scale_probs(u - 1)
                    if p == 0 and w + 2 < NT:
                        unit_vectors(it, w + 2)
                    if p == 1 and w + 2 < NT:
                        times_sin(it, w + 2)
                    if p == 3 and w + AHEAD < NT:
                        sums(it, w + AHEAD)

            def feed_forward(it, more):
                def residual(c, m):
                    dve.wait_ge(wo_ready.sem, wo_ready.of(it, c * KD + m))
                    if c == 0:
                        dve.wait_ge(out_ready.sem, out_ready.of(it, -1))
                    s = slice(m + c * CH, m + (c + 1) * CH)
                    dve.tensor_tensor(x_mid[:, m, s], pair[c][m][:, :], x_in[:, m, s], ALU.add).then_inc(mid_ready.sem, 1)

                tile = lambda t: pair[t // TC][t % TC // 2][:, (t % 2) * D:(t % 2 + 1) * D]

                def statistics(c):
                    for t in range(c * TC, (c + 1) * TC):
                        dve.wait_ge(ln_ready.sem, ln_ready.of(it, t // 2))
                        dve.bn_stats(stats[:, t, :], tile(t)).then_inc(counted.sem, 1)
                    wait_apart(dve, passed, counted.sem, counted.of(it, (c + 1) * TC - 1))
                    for t in range(c * TC, (c + 1) * TC):
                        dve.bn_aggr(mean_var[:, t, :], stats[:, t, :]).then_inc(averaged.sem, 1)

                def normalise(c):
                    dve.wait_ge(averaged.sem, averaged.of(it, (c + 1) * TC - 1))
                    dve.wait_ge(rstd_ready.sem, rstd_ready.of(it, c))
                    for t in range(c * TC, (c + 1) * TC):
                        dve.tensor_scalar(hn[:, t, :], tile(t), mean_var[:, t, 0:1], rstd[:, t:t + 1],
                                          ALU.subtract, ALU.mult).then_inc(hn_ready.sem, 1)

                def gated(c, j):
                    rows = P if j < HT - 1 else HL
                    dve.wait_ge(gelu_done.sem, gelu_done.of(it, c * HT + j))
                    if c and j == 0:
                        dve.wait_ge(down_ready.sem, down_ready.of(it, c * KD - 1))
                    dve.scalar_tensor_tensor(out=hidden[0:rows, j, :], in0=up_pair(c, j)[0][0:rows, :],
                                             scalar=b_up[0:rows, 0, j:j + 1], in1=gate[0:rows, (c * HT + j) % 2, :],
                                             op0=ALU.add, op1=ALU.mult).then_inc(hidden_ready.sem, 1)

                def output(c, m):
                    dve.wait_ge(down_ready.sem, down_ready.of(it, c * KD + m))
                    dve.wait_ge(out_stored[m], it * (16 * NC) + 16 * (c + 1))
                    s = slice(m + c * CH, m + (c + 1) * CH)
                    dve.scalar_tensor_tensor(out=x_out[:, m, :], in0=pair[c][m][:, :], scalar=b_down[:, m:m + 1],
                                             in1=x_mid[:, m, s], op0=ALU.add, op1=ALU.add).then_inc(out_ready.sem, 1)

                for c in range(NC):
                    for m in range(KD):
                        residual(c, m)
                statistics(0)
                statistics(1)
                normalise(0)
                normalise(1)
                for j in range(HT):
                    gated(0, j)
                    if more and j == 2:
                        sums(it + 1, 0)
                    if more and j == 3:
                        unit_vectors(it + 1, 0)
                    if more and j == 4:
                        times_sin(it + 1, 0)
                if more:
                    sums(it + 1, 1)
                output(0, 0)
                if more:
                    unit_vectors(it + 1, 1)
                output(0, 1)
                for j in range(HT):
                    gated(1, j)
                    if more and j == 0:
                        times_sin(it + 1, 1)
                    if more and j == 3:
                        sums(it + 1, 2)
                for m in range(KD):
                    output(1, m)

            for w in range(AHEAD):
                sums(0, w)
                if w < AHEAD - 1:
                    unit_vectors(0, w)
                    times_sin(0, w)
            with dve.Fori(0, LAST) as it:
                attention(it)
                feed_forward(it, True)
            attention(LAST)
            feed_forward(LAST, False)


def finish(nc, ident, a):
    with ExitStack() as ctx:
        sb = lambda name, shape, dt=F32: ctx.enter_context(nc.sbuf_tensor(name, shape, dt))
        sem = lambda name: ctx.enter_context(nc.semaphore(name))
        y_t = sb("y_t", [P, NC, KD, CH])
        x1 = sb("x1_f", [P, NC, TC, D])
        out = sb("out_f", [P, NC, TC, D])
        y_ps = [ctx.enter_context(nc.psum_tensor(f"yt_ps{i}", [P, CH], F32)) for i in range(4)]
        loaded = [sem(f"loaded_f{c}") for c in range(NC)]
        turned = Count(sem("turned_f"), NT, NT)
        added = Count(sem("added_f"), NT, NT)
        stored = [sem(f"stored_f{c}") for c in range(NC)]
        block = ctx.enter_context(nc.Block())

        @block.sync
        def _(sp):
            for s in stored:
                sp.sem_inc(s, 16)

            def load(i):
                b, c = i // NC, i % NC
                if b:
                    sp.wait_ge(added.sem, added.of(b - 1, (c + 1) * TC - 1))
                sp.dma_start(y_t[:, c], a["xt_scratch"][b, :, :, c * CH:(c + 1) * CH].rearrange("k p t -> p k t"))\
                    .then_inc(loaded[c], 16)
                sp.dma_start(x1[:, c], a["x1_scratch"][b, c * CH:(c + 1) * CH, :].rearrange("(t p) d -> p t d", p=P))\
                    .then_inc(loaded[c], 16)

            for i in range(NC):
                load(i)
            for i in range(B * NC):
                b, c = i // NC, i % NC
                sp.wait_ge(added.sem, added.of(b, (c + 1) * TC - 1))
                sp.dma_start(a["out"][b, c * CH:(c + 1) * CH, :].rearrange("(t p) d -> p t d", p=P), out[:, c])\
                    .then_inc(stored[c], 16)
                if i + NC < B * NC:
                    load(i + NC)
            for s in stored:
                sp.wait_ge(s, 16 * (B + 1))

        @block.tensor
        def _(pe):
            pe.sem_inc(turned.sem, turned.credit)
            with pe.Fori(0, B) as b:
                for t in range(NT):
                    if t % TC == 0:
                        pe.wait_ge(loaded[t // TC], b * 32 + 32)
                    pe.wait_ge(added.sem, added.of(b, t - 4))
                    for k in range(KD):
                        mm = pe.transpose(y_ps[t % 4][:, k * P:(k + 1) * P],
                                          y_t[:, t // TC, k, (t % TC) * P:(t % TC + 1) * P], ident[:, :])
                    mm.then_inc(turned.sem, 1)

        @block.vector
        def _(dve):
            dve.sem_inc(added.sem, added.credit)
            with dve.Fori(0, B) as b:
                for t in range(NT):
                    dve.wait_ge(turned.sem, turned.of(b, t))
                    if t % TC == 0:
                        dve.wait_ge(loaded[t // TC], b * 32 + 32)
                        dve.wait_ge(stored[t // TC], b * 16 + 16)
                    dve.tensor_tensor(out[:, t // TC, t % TC, :], y_ps[t % 4][:, 0:D], x1[:, t // TC, t % TC, :],
                                      ALU.add).then_inc(added.sem, 1)


def build(nc, a):
    with ExitStack() as ctx:
        sb = lambda name, shape, dt=F32: ctx.enter_context(nc.sbuf_tensor(name, shape, dt))
        ident = sb("ident", [P, P])
        ident_b = sb("ident_b", [P, P], BF16)
        causal_b = sb("causal_b", [P, P], BF16)
        neg_half = sb("neg_half", [P, 2 * H2])
        passed = ctx.enter_context(nc.semaphore("passed"))
        zeroed = ctx.enter_context(nc.semaphore("zeroed"))
        drawn = ctx.enter_context(nc.semaphore("drawn"))
        with nc.Block() as block:
            @block.gpsimd
            def _(pool):
                pool.memset(ident[:, :], 0.0).then_inc(zeroed, 1)
                pool.memset(ident_b[:, :], 0.0).then_inc(zeroed, 1)
                pool.memset(causal_b[:, :], 0.0).then_inc(zeroed, 1)
                pool.memset(neg_half[:, :], -0.5).then_inc(zeroed, 1)
                pool.wait_ge(zeroed, 4)
                for m in (ident, ident_b):
                    pool.affine_select(out=m[:, :], in_=m[:, :], compare_op=ALU.not_equal, fill=1.0, base=0,
                                       pattern=[[-1, P]], channel_multiplier=1).then_inc(drawn, 1)
                pool.affine_select(out=causal_b[:, :], in_=causal_b[:, :], compare_op=ALU.is_ge, fill=-1e30, base=0,
                                   pattern=[[-1, P]], channel_multiplier=1).then_inc(drawn, 1)
                pool.wait_ge(drawn, 3)
        with nc.sbuf_tensor("x_all", [P, B * NT, D], F32) as x_all:
            prepare(nc, x_all, ident, neg_half, passed, a)
            causal_attention(nc, ident, ident_b, causal_b, passed, a)
            project_causal(nc, x_all, ident, neg_half, passed, a)
        layers(nc, ident, neg_half, passed, a)
        finish(nc, ident, a)


def rotary_tables():
    f = np.float32
    half = np.arange(0, HD2, 2, dtype=f)
    inv_freq = (f(1.0) / f(10000.0) ** (half / f(HD2))).astype(f)
    t = np.arange(T, dtype=f)
    angle = t[:, None] * inv_freq[None, :]
    base = ((half + f(0.4 * HD2)) / f(1.4 * HD2)).astype(f)
    power = ((t - f(T // 2)) / f(WIN // 2)).astype(f)
    scale = base[None, :] ** power[:, None]
    twice = lambda x: np.concatenate([x, x], axis=-1)
    sign = np.where(np.arange(HD2) < HD2 // 2, f(-1), f(1))
    cos, sin, scale = np.cos(twice(angle)), np.sin(twice(angle)) * sign, twice(scale)
    q = f(-QK_SCALE)
    return np.stack([q * cos * scale, q * sin * scale, cos / scale, sin / scale], axis=1).astype(f)


_NAMES = {"x": "L0_attn_x", "wq": "L0_attn_wq", "bq": "L0_attn_bq", "wk": "L0_attn_wk", "bk": "L0_attn_bk",
          "wv": "L0_attn_wv", "bv": "L0_attn_bv", "wo": "L0_attn_wo", "bo": "L0_attn_bo", "wqkv": "L0_ffn_wqkv",
          "q_scale": "L0_ffn_q_scale", "k_scale": "L0_ffn_k_scale", "wo2": "L0_ffn_wo", "ln_g": "L0_ffn_ln_g",
          "ln_b": "L0_ffn_ln_b", "w1": "L0_ffn_w1", "b1": "L0_ffn_b1", "w2": "L0_ffn_w2", "b2": "L0_ffn_b2"}


def kernel(**inputs):
    import concourse.bacc as bacc
    from concourse.bass_utils import run_bass_kernel_spmd

    nc = bacc.Bacc("TRN2", target_bir_lowering=False, num_devices=1)
    nc.disable_value_cache = True
    arrays = {short: np.ascontiguousarray(inputs[name]) for short, name in _NAMES.items()}
    arrays["rotary"] = rotary_tables()
    a = {n: nc.dram_tensor(f"in_{n}", list(x.shape), mybir.dt.from_np(x.dtype), kind="ExternalInput").ap()
         for n, x in arrays.items()}
    scratch = {"v_scratch": ([B * NG, P, NT, HG * VW], F32), "qk_scratch": ([2, B * NG, 3, GF, T], BF16),
               "att_scratch": ([B * NG, T, GF], F32), "x1_scratch": ([B, T, D], F32), "xt_scratch": ([B, KD, P, T], F32)}
    for n, (shape, dt) in scratch.items():
        a[n] = nc.dram_tensor(n, shape, dt, kind="Internal").ap()
    a["out"] = nc.dram_tensor("out", [B, T, D], F32, kind="ExternalOutput").ap()
    build(nc, a)
    r = run_bass_kernel_spmd(nc, [{f"in_{n}": x for n, x in arrays.items()}], core_ids=[0])
    return r.results[0]["out"]
```

```python
import concourse.bass as bass
import numpy as np
from concourse import mybir
from contextlib import ExitStack

F32 = mybir.dt.float32
F32R = mybir.dt.float32r
BF16 = mybir.dt.bfloat16
ALU = mybir.AluOpType
ACT = mybir.ActivationFunctionType
AX = mybir.AxisListType

P = 128
B, T, D = 4, 1024, 256
KD = D // P
NT = T // P
CH = 512
NC = T // CH
TC = CH // P

H1, HD1 = 16, 16
HG = 4
NG = H1 // HG
GF = HG * HD1
VW = 32
TERMS = ((0, 0), (0, 1), (0, 2), (1, 0), (1, 1), (2, 0))
STK = len(TERMS) * HD1

DEPTH, H2, HD2, WIN = 2, 8, 64, 128
INNER = H2 * HD2
HID = int(D * 4 * 2 / 3)
QK_SCALE = 8.0
HT = -(-HID // P)
HL = HID - (HT - 1) * P
GL = P // 2
UT = 2 * HT - 1
DOWN0 = KD * UT * P
WCOLS = DOWN0 + HT * D
EPS = 1e-5
BIG = 3.0e38


def as_fast(ap):
    return ap.bitcast(F32R)


def as_float(ap):
    return ap.bitcast(F32)


class Count:

    def __init__(self, sem, per, credit=0):
        self.sem, self.per, self.credit = sem, per, credit

    def of(self, iteration, item):
        return iteration * self.per + (item + 1 + self.credit)


def wait_apart(eng, passed, sem, value):
    eng.wait_ge(sem, value)
    eng.sem_inc(passed, 1)


def prepare(nc, x_all, ident, neg_half, passed, a):
    with ExitStack() as ctx:
        sb = lambda name, shape, dt=F32: ctx.enter_context(nc.sbuf_tensor(name, shape, dt))
        ps = lambda name, shape: ctx.enter_context(nc.psum_tensor(name, shape, F32))
        sem = lambda name: ctx.enter_context(nc.semaphore(name))

        w_qk = sb("w_qk", [P, KD, 2 * D])
        w_v = sb("w_v", [P, KD, D])
        b_qk = sb("b_qk", [P, 2 * KD])
        b_v = sb("b_v", [P, D])
        stats = sb("stats", [P, NT, 6])
        mean_var = sb("mean_var", [P, NT, 2])
        mean = sb("mean", [P, NT])
        var_eps = sb("var_eps", [P, NT])
        rstd_next = sb("rstd_next", [P, NT])
        rstd = sb("rstd", [P, NT])
        xn = sb("xn", [P, 2, D])
        xn_t = sb("xn_t", [P, KD, T])
        full = sb("full", [P, 4, CH])
        rest = sb("rest", [P, 4, CH])
        parts = sb("parts", [P, 4, 3, CH], BF16)
        v_out = sb("v_out", [P, 2, H1, VW])
        turned = [ps(f"turned{i}", [P, CH]) for i in range(2)]
        v_ps = [ps(f"v_ps{i}", [P, CH]) for i in range(2)]
        qk_ps = [ps(f"qk_ps{i}", [P, CH]) for i in range(2)]

        weights_in = sem("weights_in")
        x_in = sem("x_in")
        scaled_bias = sem("scaled_bias")
        ones_set = sem("ones_set")
        counted = Count(sem("counted"), NT)
        averaged = Count(sem("averaged"), NT)
        var_ready = Count(sem("var_ready"), 1)
        rstd_ready = Count(sem("rstd_ready"), 1)
        moved = Count(sem("moved"), 2, 2)
        xn_ready = Count(sem("xn_ready"), NT, 8)
        turned_ready = Count(sem("turned_ready"), NT, 2)
        xn_t_ready = Count(sem("xn_t_ready"), NT, 2)
        v_ready = Count(sem("v_ready"), NT, 8)
        v_copied = Count(sem("v_copied"), NT, 2)
        NI = NC * 2 * KD
        qk_ready = Count(sem("qk_ready"), NI, 8)
        full_ready = Count(sem("full_ready"), NI, 2)
        high_ready = Count(sem("high_ready"), NI, 2)
        rest_ready = Count(sem("rest_ready"), NI, 4)
        mid_ready = Count(sem("mid_ready"), NI, 2)
        low_ready = Count(sem("low_ready"), NI, 4)
        v_stored = [sem(f"v_stored{i}") for i in range(2)]
        parts_stored = [sem(f"parts_stored{i}") for i in range(4)]
        block = ctx.enter_context(nc.Block())

        @block.sync
        def _(sp):
            def load_x(b):
                if b >= 1:
                    sp.wait_ge(x_in, 16 * b)
                sp.dma_start(x_all[:, b * NT:(b + 1) * NT, :],
                             a["x"][b].rearrange("(t p) d -> p t d", p=P)).then_inc(x_in, 16)

            for s in v_stored:
                sp.sem_inc(s, 16)
            for s in parts_stored:
                sp.sem_inc(s, 32)
            load_x(0)
            w_dma = [
                sp.dma_start(w_qk[:, :, 0:D], a["wq"].rearrange("(k p) n -> p k n", p=P)),
                sp.dma_start(w_qk[:, :, D:2 * D], a["wk"].rearrange("(k p) n -> p k n", p=P)),
                sp.dma_start(w_v[:, :, :], a["wv"].rearrange("(k p) n -> p k n", p=P)),
                sp.dma_start(b_qk[:, 0:KD], a["bq"].rearrange("(m p) -> p m", p=P), allow_slow_non_contiguous=True),
                sp.dma_start(b_qk[:, KD:2 * KD], a["bk"].rearrange("(m p) -> p m", p=P), allow_slow_non_contiguous=True),
                sp.dma_start(b_v[:, :], a["bv"].partition_broadcast(P)),
            ]
            for d in w_dma:
                d.then_inc(weights_in, 16)
            load_x(1)
            for b in range(B):
                for t in range(NT):
                    sp.wait_ge(v_copied.sem, v_copied.of(b, t))
                    sp.dma_start(a["v_scratch"][b * NG:(b + 1) * NG, :, t, :].rearrange("g p n -> p g n"),
                                 v_out[:, t % 2].rearrange("p (g h) w -> p g (h w)", g=NG)).then_inc(v_stored[t % 2], 16)
                    if t % 4 == 3:
                        if t == 3 and b + 2 < B:
                            load_x(b + 2)
                        for m in range(2 * KD):
                            i = (t // 4) * 2 * KD + m
                            sp.wait_ge(low_ready.sem, low_ready.of(b, i))
                            c0 = (t // 4) * CH
                            for half in range(2):
                                g = b * NG + (m % KD) * 2 + half
                                sp.dma_start(a["qk_scratch"][m // KD, g, :, :, c0:c0 + CH].rearrange("s f t -> f s t"),
                                             parts[half * GF:(half + 1) * GF, i % 4]).then_inc(parts_stored[i % 4], 16)
            for s in v_stored:
                sp.wait_ge(s, 16 * (B * NT // 2 + 1))
            for s in parts_stored:
                sp.wait_ge(s, 32 * (B * NI // 4 + 1))

        @block.vector
        def _(dve):
            dve.sem_inc(xn_ready.sem, xn_ready.credit)
            dve.sem_inc(v_copied.sem, v_copied.credit)
            dve.sem_inc(high_ready.sem, high_ready.credit)
            dve.sem_inc(mid_ready.sem, mid_ready.credit)
            dve.sem_inc(low_ready.sem, low_ready.credit)
            dve.sem_inc(moved.sem, moved.credit)
            dve.memset(v_out[:, :, :, HD1:VW], 1.0).then_inc(ones_set, 1)

            def statistics(b, tiles):
                dve.wait_ge(x_in, b * 16 + 16)
                for t in tiles:
                    dve.bn_stats(stats[:, t, :], x_all[:, bass.ds(b * NT + t, 1), :]).then_inc(counted.sem, 1)

            def averages(b):
                wait_apart(dve, passed, counted.sem, counted.of(b, NT - 1))
                for t in range(NT):
                    dve.bn_aggr(mean_var[:, t, :], stats[:, t, :]).then_inc(averaged.sem, 1)

            def take_over(b):
                dve.wait_ge(averaged.sem, averaged.of(b, NT - 1))
                dve.wait_ge(rstd_ready.sem, rstd_ready.of(b, 0))
                dve.wait_ge(xn_ready.sem, xn_ready.of(b, -1))
                dve.tensor_copy(mean[:, :], mean_var[:, :, 0]).then_inc(moved.sem, 1)
                dve.tensor_copy(rstd[:, :], rstd_next[:, :]).then_inc(moved.sem, 1)
                wait_apart(dve, passed, moved.sem, moved.of(b, 1))

            def normalise(b, t):
                dve.wait_ge(turned_ready.sem, turned_ready.of(b, t - 2))
                dve.tensor_scalar(xn[:, t % 2, :], x_all[:, bass.ds(b * NT + t, 1), :], mean[:, t:t + 1],
                                  rstd[:, t:t + 1], ALU.subtract, ALU.mult).then_inc(xn_ready.sem, 1)

            def copy_v(b, t):
                dve.wait_ge(v_ready.sem, v_ready.of(b, t))
                dve.wait_ge(v_stored[t % 2], b * (16 * NT // 2) + 16 * (t // 2 + 1))
                dve.tensor_tensor(v_out[:, t % 2, :, 0:HD1], v_ps[t % 2][:, 0:D].rearrange("p (h d) -> p h d", h=H1),
                                  b_v[:, :].rearrange("p (h d) -> p h d", h=H1), ALU.add).then_inc(v_copied.sem, 1)

            def high(b, i):
                dve.wait_ge(full_ready.sem, full_ready.of(b, i))
                dve.wait_ge(parts_stored[i % 4], b * (32 * NI // 4) + 32 * (i // 4 + 1))
                dve.tensor_copy(parts[:, i % 4, 0, :], full[:, i % 4, :]).then_inc(high_ready.sem, 1)

            def mid_low(b, i):
                dve.wait_ge(rest_ready.sem, rest_ready.of(b, i))
                dve.tensor_copy(parts[:, i % 4, 1, :], rest[:, i % 4, :]).then_inc(mid_ready.sem, 1)
                dve.wait_ge(mid_ready.sem, mid_ready.of(b, i))
                dve.tensor_tensor(parts[:, i % 4, 2, :], rest[:, i % 4, :], parts[:, i % 4, 1, :],
                                  ALU.subtract).then_inc(low_ready.sem, 1)

            def batch(b, more):
                for t in range(TC):
                    copy_v(b, t)
                for i in range(NI):
                    if i == TC:
                        mid_low(b, i - 1)
                        for t in range(TC, NT):
                            copy_v(b, t)
                        if more:
                            take_over(b + 1)
                    if i < TC:
                        normalise(b, TC + i)
                        if more:
                            statistics(b + 1, (2 * i, 2 * i + 1))
                            if i == TC - 1:
                                averages(b + 1)
                    elif more:
                        normalise(b + 1, i - TC)
                    high(b, i)
                    if i % TC:
                        mid_low(b, i - 1)
                mid_low(b, NI - 1)

            statistics(0, range(NT))
            averages(0)
            take_over(0)
            for t in range(TC):
                normalise(0, t)
            dve.wait_ge(weights_in, 96)
            dve.tensor_scalar(b_qk[:, 0:KD], b_qk[:, 0:KD], HD1 ** -0.5, None, ALU.mult).then_inc(scaled_bias, 1)
            with dve.Fori(0, B - 1) as b:
                batch(b, True)
            batch(B - 1, False)

        @block.gpsimd
        def _(pool):
            pool.sem_inc(rest_ready.sem, rest_ready.credit)

            def deviations(b):
                pool.wait_ge(averaged.sem, averaged.of(b, NT - 1))
                wait_apart(pool, passed, moved.sem, moved.of(b, -1))
                pool.tensor_scalar(var_eps[:, :], mean_var[:, :, 1], EPS, None, ALU.add).then_inc(var_ready.sem, 1)
                pool.wait_ge(var_ready.sem, var_ready.of(b, 0))
                pool.tensor_tensor(rstd_next[:, :], var_eps[:, :], neg_half[:, 0:NT], ALU.pow).then_inc(rstd_ready.sem, 1)

            def batch(b, more):
                for i in range(NI):
                    if more and i == TC:
                        deviations(b + 1)
                    pool.wait_ge(high_ready.sem, high_ready.of(b, i))
                    pool.wait_ge(low_ready.sem, low_ready.of(b, i - 4))
                    pool.tensor_tensor(rest[:, i % 4, :], full[:, i % 4, :], parts[:, i % 4, 0, :],
                                       ALU.subtract).then_inc(rest_ready.sem, 1)

            deviations(0)
            with pool.Fori(0, B - 1) as b:
                batch(b, True)
            batch(B - 1, False)

        @block.scalar
        def _(act):
            act.sem_inc(xn_t_ready.sem, xn_t_ready.credit)
            act.sem_inc(full_ready.sem, full_ready.credit)
            act.wait_ge(scaled_bias, 1)

            def copy_turned(b, t):
                act.wait_ge(turned_ready.sem, turned_ready.of(b, t))
                act.wait_ge(qk_ready.sem, qk_ready.of(b, (t // TC + 1) * 2 * KD - 1 - NI))
                act.copy(xn_t[:, :, t * P:(t + 1) * P],
                         turned[t % 2][:, 0:D].rearrange("p (k t) -> p k t", k=KD)).then_inc(xn_t_ready.sem, 1)

            def copy_qk(b, i):
                m = i % (2 * KD)
                act.wait_ge(qk_ready.sem, qk_ready.of(b, i))
                act.wait_ge(rest_ready.sem, rest_ready.of(b, i - 4))
                act.activation(full[:, i % 4, :], qk_ps[i % 2][:, :], ACT.Identity, bias=b_qk[:, m:m + 1],
                               scale=HD1 ** -0.5 if m < KD else 1.0).then_inc(full_ready.sem, 1)

            def batch(b, more):
                for i in range(NI):
                    copy_qk(b, i)
                    if i < TC:
                        copy_turned(b, TC + i)
                    elif more:
                        copy_turned(b + 1, i - TC)

            for t in range(TC):
                copy_turned(0, t)
            with act.Fori(0, B - 1) as b:
                batch(b, True)
            batch(B - 1, False)

        @block.tensor
        def _(pe):
            pe.sem_inc(turned_ready.sem, turned_ready.credit)
            pe.sem_inc(v_ready.sem, v_ready.credit)
            pe.sem_inc(qk_ready.sem, qk_ready.credit)

            def turn(b, t):
                pe.wait_ge(xn_ready.sem, xn_ready.of(b, t))
                pe.wait_ge(xn_t_ready.sem, xn_t_ready.of(b, t - 2))
                for k in range(KD):
                    mm = pe.transpose(turned[t % 2][:, k * P:(k + 1) * P], xn[:, t % 2, k * P:(k + 1) * P], ident[:, :])
                mm.then_inc(turned_ready.sem, 1)

            def project_v(b, t):
                pe.wait_ge(xn_t_ready.sem, xn_t_ready.of(b, t))
                pe.wait_ge(v_copied.sem, v_copied.of(b, t - 2))
                for k in range(KD):
                    mm = pe.matmul(v_ps[t % 2][:, 0:D], xn_t[:, k, t * P:(t + 1) * P], w_v[:, k, :],
                                   start=k == 0, stop=k == KD - 1)
                mm.then_inc(v_ready.sem, 1)

            def project_qk(b, i):
                c, m = i // (2 * KD), i % (2 * KD)
                pe.wait_ge(full_ready.sem, full_ready.of(b, i - 2))
                for k in range(KD):
                    mm = pe.matmul(qk_ps[i % 2][:, :], w_qk[:, k, m * P:(m + 1) * P], xn_t[:, k, c * CH:(c + 1) * CH],
                                   start=k == 0, stop=k == KD - 1)
                mm.then_inc(qk_ready.sem, 1)

            def batch(b, more):
                for i in range(NI):
                    if i % TC == 0:
                        for t in range(i, i + TC):
                            project_v(b, t)
                    project_qk(b, i)
                    if i < TC:
                        turn(b, TC + i)
                    elif more:
                        turn(b + 1, i - TC)

            for t in range(TC):
                turn(0, t)
            pe.wait_ge(weights_in, 96)
            with pe.Fori(0, B - 1) as b:
                batch(b, True)
            batch(B - 1, False)


SETS = [(c, kt) for c in range(NC) for kt in range((c + 1) * TC)]
NS = len(SETS)
DIAGONAL = [n for n, (c, kt) in enumerate(SETS) if kt >= c * TC]


def first_query(c, kt):
    return max(0, kt - c * TC) * P


PIECES = [(qt, k0, min(CH, (qt + 1) * P - k0)) for qt in range(NT) for k0 in range(0, (qt + 1) * P, CH)]
NP = len(PIECES)
SHIFT = 2
SLOTS = 4
SPLIT_SLOT = 1
HALF = HG // 2
SR = SHIFT * HALF * NT


def beside():
    columns = [CH - first_query(*SETS[n]) for n in range(NS) for h in range(HG)]
    pieces, shift, taken, upto, i = [], {}, 0, 0, 0
    for at, cols in enumerate(columns):
        upto += cols * 1.08
        first = i
        while i < NP * HG and taken < upto:
            taken += PIECES[i % NP][2]
            i += 1
            if i == NP * HALF:
                shift[at + 3] = 0
            if i == NP * HG:
                shift[min(at + 3, NS * HG - 1)] = 1
        pieces.append(i - first)
    return pieces, shift


PIECES_AT, SHIFT_AT = beside()


def causal_attention(nc, x_all, ident, ident_b, causal_b, passed, a):
    with ExitStack() as ctx:
        sb = lambda name, shape, dt=F32: ctx.enter_context(nc.sbuf_tensor(name, shape, dt))
        ps = lambda name: ctx.enter_context(nc.psum_tensor(name, [P, CH], F32))
        sem = lambda name: ctx.enter_context(nc.semaphore(name))

        q_stack = sb("q_stack", [P, SLOTS, HG, T], BF16)
        k_stack = sb("k_stack", [P, SLOTS, HG, T], BF16)
        v_sb = sb("v_sb", [P, SLOTS, NT, HG * VW])
        probs = sb("probs", [P, 3, HG, CH])
        piece_negmax = sb("piece_negmax", [P, HG, NP])
        negmax = sb("negmax", [P, HG, NT])
        negmax_parts = sb("negmax_parts", [P, 2, SHIFT, HALF, NT], BF16)
        shift_sb = sb("shift_sb", [SR, 2, P], BF16)
        o_sb = sb("o_sb", [P, NC, CH])
        inv_sum = sb("inv_sum", [P, NC, TC, HG])
        att = sb("att", [P, NC, TC, HG, HD1])
        w_raw = sb("w_raw", [P, WCOLS])
        w_high = sb("w_high", [P, WCOLS])
        b_o = sb("b_o", [P, D])
        bias_in, biased = sem("bias_in"), sem("biased")
        w_zeroed, w_in, w_stored = sem("w_zeroed"), sem("w_in"), sem("w_stored")
        PIECE = WCOLS // 4
        w_high_done = Count(sem("w_high_done"), 4)
        w_low_done = Count(sem("w_low_done"), 4)
        st_ps = [ps(f"st_ps{i}") for i in range(3)]
        s_ps = [ps(f"s_ps{i}") for i in range(3)]
        o_ps, ot_ps = ps("o_ps"), ps("ot_ps")
        shift_ps = ot_ps

        def count(name, items, credit=0):
            return Count(sem(name), SLOTS * items, credit)

        st_ready = count("st_ready", NS * HG)
        exp_done = count("exp_done", NS * HG, 8)
        masked = count("masked", len(DIAGONAL))
        pv_done = count("pv_done", NS, 3)
        s_ready = count("s_ready", NP * HG)
        piece_done = count("piece_done", NP * HG, 3)
        joined = count("joined", 2 * 2)
        parts_done = count("parts_done", 2 * 2)
        shift_ready = count("shift_ready", 2, 2)
        shift_copied = count("shift_copied", 2)
        shift_in = [sem(f"shift_in{i}") for i in range(2)]
        o_copied = count("o_copied", NC, 1)
        ot_ready = count("ot_ready", NC)
        summed = count("summed", NC)
        att_ready = count("att_ready", NC, 1)
        att_stored = [sem(f"att_stored{c}") for c in range(NC)]
        stack_in = [sem(f"stack_in{s}") for s in range(SLOTS)]
        shift_ones = sem("shift_ones")
        LOAD = 16 * (2 * len(TERMS) + 1)
        block = ctx.enter_context(nc.Block())

        def groups(eng, group, first):
            first((0, 0))
            group((0, 0), None, (0, 1))
            with eng.Fori(0, B - 1) as r:
                for s in range(1, SLOTS + 1):
                    at = lambda s: (r + s // SLOTS, s % SLOTS)
                    group(at(s), at(s - 1), at(s + 1))
            for s in range(1, SLOTS):
                group((B - 1, s), (B - 1, s - 1), (B - 1, s + 1) if s + 1 < SLOTS else None)

        def shift_there(eng, group, half):
            eng.wait_ge(shift_in[half], (group[0] * SLOTS + group[1]) * (16 * SHIFT) + 16 * SHIFT)

        def splits(group):
            return isinstance(group[0], int) and group == (B - 1, SPLIT_SLOT)

        def when(count, group, items, i):
            return count.of(group[0], group[1] * items + i)

        @block.sync
        def _(sp):
            for c in range(NC):
                sp.sem_inc(att_stored[c], 16)

            def load(g):
                slot = g % SLOTS
                if g >= SLOTS:
                    sp.wait_ge(pv_done.sem, when(pv_done, (g // SLOTS - 1, slot), NS, NS - 1))
                for r, (qp, kp) in enumerate(TERMS):
                    for stack, which, part in ((q_stack, 0, qp), (k_stack, 1, kp)):
                        sp.dma_start(stack[r * HD1:(r + 1) * HD1, slot, :, :],
                                     a["qk_scratch"][which, g, part].rearrange("(h d) t -> d h t", d=HD1))\
                            .then_inc(stack_in[slot], 16)
                sp.dma_start(v_sb[:, slot], a["v_scratch"][g]).then_inc(stack_in[slot], 16)

            def store(g, c):
                sp.wait_ge(att_ready.sem, when(att_ready, (g // SLOTS, g % SLOTS), NC, c))
                sp.dma_start(a["att_scratch"][g, c * CH:(c + 1) * CH, :].rearrange("(t p) n -> p t n", p=P),
                             att[:, c].rearrange("p t h d -> p t (h d)")).then_inc(att_stored[c], 16)

            def spread_shift(g, half):
                sp.wait_ge(shift_copied.sem, when(shift_copied, (g // SLOTS, g % SLOTS), 2, half))
                for part in range(SHIFT):
                    sp.dma_start(q_stack[STK + part:STK + part + 1, g % SLOTS, half * HALF:(half + 1) * HALF, :],
                                 shift_sb[part * HALF * NT:(part + 1) * HALF * NT, half, :]).then_inc(shift_in[half], 16)

            def load_ffn_weights(l):
                up = w_raw[:, 0:DOWN0].rearrange("p (k n) -> p k n", k=KD)
                down = w_raw[:, DOWN0:WCOLS].rearrange("p (j n) -> p j n", j=HT)
                w1 = a["w1"][l].rearrange("(k p) n -> p k n", p=P)
                whole = (HT - 1) * P
                dmas = [(up[:, :, 0:whole], w1[:, :, 0:whole]),
                        (up[:, :, whole:2 * whole], w1[:, :, HID:HID + whole]),
                        (up[:, :, 2 * whole:2 * whole + HL], w1[:, :, whole:HID]),
                        (up[:, :, 2 * whole + GL:2 * whole + GL + HL], w1[:, :, HID + whole:2 * HID]),
                        (down[:, 0:HT - 1, :], a["w2"][l, 0:whole, :].rearrange("(j p) n -> p j n", p=P)),
                        (down[0:HL, HT - 1, :], a["w2"][l, whole:HID, :])]
                for dst, src in dmas:
                    sp.dma_start(dst, src).then_inc(w_in, 16)

            def store_ffn_weights(l):
                sp.wait_ge(w_low_done.sem, w_low_done.of(l, 3))
                for part, tile in enumerate((w_high, w_raw)):
                    sp.dma_start(a["ffn_weights"][l, part], tile[:, :]).then_inc(w_stored, 16)

            for g in range(SLOTS):
                load(g)
            sp.dma_start(b_o[:, :], a["bo"].partition_broadcast(P)).then_inc(bias_in, 16)
            sp.wait_ge(w_zeroed, 2)
            load_ffn_weights(0)
            spread_shift(0, 0)
            spread_shift(0, 1)
            store_ffn_weights(0)
            for g in range(B * NG):
                if g >= 1:
                    store(g - 1, 1)
                    if g - 1 + SLOTS < B * NG:
                        load(g - 1 + SLOTS)
                if g + 1 < B * NG:
                    spread_shift(g + 1, 0)
                if g == SPLIT_SLOT + (B - 1) * SLOTS - 2:
                    sp.wait_ge(w_stored, 32)
                    load_ffn_weights(1)
                if g == SPLIT_SLOT + (B - 1) * SLOTS:
                    store_ffn_weights(1)
                store(g, 0)
                if g + 1 < B * NG:
                    spread_shift(g + 1, 1)
            store(B * NG - 1, 1)
            sp.wait_ge(w_stored, 32 * DEPTH)
            for c in range(NC):
                sp.wait_ge(att_stored[c], 16 * (B * NG + 1))

        @block.tensor
        def _(pe):
            for c in (pv_done, shift_ready):
                pe.sem_inc(c.sem, c.credit)

            def loaded(group):
                pe.wait_ge(stack_in[group[1]], group[0] * LOAD + LOAD)

            def score_piece(group, i):
                slot, h, (qt, k0, kw) = group[1], i // NP, PIECES[i % NP]
                pe.wait_ge(piece_done.sem, when(piece_done, group, NP * HG, i - 3))
                last = k0 + kw == (qt + 1) * P
                mm = pe.matmul(s_ps[i % 3][:, 0:kw], q_stack[0:STK, slot, h, qt * P:(qt + 1) * P],
                               k_stack[0:STK, slot, h, k0:k0 + kw], start=True, stop=not last)
                if last:
                    mm = pe.matmul(s_ps[i % 3][:, kw - P:kw], ident_b[:, :], causal_b[:, :], start=False, stop=True)
                mm.then_inc(s_ready.sem, 1)

            def shift_rows(group, half):
                pe.wait_ge(parts_done.sem, when(parts_done, group, 2 * 2, 2 * half + 1))
                pe.matmul(shift_ps[0:SR, 0:P], negmax_parts[:, half].rearrange("p s h t -> p (s h t)"), ident_b[:, :],
                          start=True, stop=True).then_inc(shift_ready.sem, 1)

            def shifted_score(group, i):
                slot, n, h = group[1], i // HG, i % HG
                c, kt = SETS[n]
                q0 = first_query(c, kt)
                if n == 0 and h % HALF == 0:
                    shift_there(pe, group, h // HALF)
                pe.wait_ge(exp_done.sem, when(exp_done, group, NS * HG, i - 3))
                pe.matmul(st_ps[i % 3][:, q0:CH], k_stack[0:STK + SHIFT, slot, h, kt * P:(kt + 1) * P],
                          q_stack[0:STK + SHIFT, slot, h, c * CH + q0:(c + 1) * CH],
                          start=True, stop=True).then_inc(st_ready.sem, 1)

            def add_values(group, n):
                r, slot = group
                c, kt = SETS[n]
                q0 = first_query(c, kt)
                pe.wait_ge(exp_done.sem, when(exp_done, group, NS * HG, n * HG + HG - 1))
                if n in DIAGONAL:
                    pe.wait_ge(masked.sem, when(masked, group, len(DIAGONAL), DIAGONAL.index(n)))
                if kt == 0:
                    pe.wait_ge(o_copied.sem, when(o_copied, group, NC, c - 1))
                for h in range(HG):
                    mm = pe.matmul(o_ps[h * VW:(h + 1) * VW, q0:CH], v_sb[:, slot, kt, h * VW:(h + 1) * VW],
                                   probs[:, n % 3, h, q0:CH], start=kt == 0, stop=kt == (c + 1) * TC - 1,
                                   tile_position=(0, h * VW))
                mm.then_inc(pv_done.sem, 1)

            def turn_output(group, c):
                pe.wait_ge(o_copied.sem, when(o_copied, group, NC, c))
                for j in range(TC):
                    mm = pe.transpose(ot_ps[:, j * P:(j + 1) * P], o_sb[:, c, j * P:(j + 1) * P], ident[:, :])
                mm.then_inc(ot_ready.sem, 1)

            def first(group):
                loaded(group)
                for i in range(NP * HG):
                    score_piece(group, i)
                shift_rows(group, 0)
                pe.wait_ge(shift_copied.sem, when(shift_copied, group, 2, 0))
                shift_rows(group, 1)
                pe.wait_ge(shift_ones, 1)

            def group_work(group, previous, following):
                if following:
                    loaded(following)
                piece = 0
                for i in range(NS * HG):
                    n = i // HG
                    shifted_score(group, i)
                    if following:
                        for _ in range(PIECES_AT[i]):
                            score_piece(following, piece)
                            piece += 1
                        if i in SHIFT_AT:
                            pe.wait_ge(att_ready.sem, when(att_ready, group, NC, SHIFT_AT[i] - 1))
                            shift_rows(following, SHIFT_AT[i])
                    if i % HG == HG - 1:
                        if n >= 1:
                            add_values(group, n - 1)
                        elif previous:
                            add_values(previous, NS - 1)
                        if n == 2 and previous:
                            pe.wait_ge(shift_copied.sem, when(shift_copied, group, 2, 1))
                            turn_output(previous, 1)
                        if n == 7:
                            if following:
                                pe.wait_ge(shift_copied.sem, when(shift_copied, following, 2, 0))
                            else:
                                pe.wait_ge(att_ready.sem, when(att_ready, group, NC, -1))
                            turn_output(group, 0)
                if not following:
                    add_values(group, NS - 1)
                    pe.wait_ge(att_ready.sem, when(att_ready, group, NC, 0))
                    turn_output(group, 1)

            groups(pe, group_work, first)

        @block.scalar
        def _(act):
            for c in (exp_done, o_copied):
                act.sem_inc(c.sem, c.credit)

            def copy_shift(group, half):
                act.wait_ge(shift_ready.sem, when(shift_ready, group, 2, half))
                act.copy(shift_sb[:, half, :], shift_ps[0:SR, 0:P]).then_inc(shift_copied.sem, 1)

            def exponential(group, i):
                n, h = i // HG, i % HG
                q0 = first_query(*SETS[n])
                if h == 0:
                    act.wait_ge(pv_done.sem, when(pv_done, group, NS, n - 3))
                act.wait_ge(st_ready.sem, when(st_ready, group, NS * HG, i))
                act.activation(probs[:, n % 3, h, q0:CH], st_ps[i % 3][:, q0:CH], ACT.Exp).then_inc(exp_done.sem, 1)

            def copy_output(group, c):
                act.wait_ge(pv_done.sem, when(pv_done, group, NS, (NS if c else TC) - 1))
                act.copy(o_sb[:, c, :], o_ps[:, :]).then_inc(o_copied.sem, 1)

            def high_parts(l):
                act.wait_ge(w_in, 16 * 6 * (l + 1))
                if l:
                    act.wait_ge(w_stored, 32 * l)
                for i in range(4):
                    cols = slice(i * PIECE, (i + 1) * PIECE)
                    act.copy(as_fast(w_high[:, cols]), w_raw[:, cols]).then_inc(w_high_done.sem, 1)

            def first(group):
                high_parts(0)
                copy_shift(group, 0)
                copy_shift(group, 1)

            def group_work(group, previous, following):
                for i in range(NS * HG):
                    if i == HG + 1 and previous:
                        copy_output(previous, 1)
                    if i == 5 * HG + 1:
                        copy_output(group, 0)
                    exponential(group, i)
                    if splits(group) and i == 4 * HG:
                        high_parts(1)
                    if following and i in SHIFT_AT:
                        copy_shift(following, SHIFT_AT[i])
                if not following:
                    copy_output(group, 1)

            groups(act, group_work, first)

        @block.vector
        def _(dve):
            for c in (piece_done, att_ready):
                dve.sem_inc(c.sem, c.credit)

            def reduce_piece(group, i):
                h, (qt, k0, kw) = i // NP, PIECES[i % NP]
                dve.wait_ge(s_ready.sem, when(s_ready, group, NP * HG, i))
                dve.tensor_reduce(piece_negmax[:, h, i % NP:i % NP + 1], s_ps[i % 3][:, 0:kw], AX.X, ALU.max,
                                  negate=True).then_inc(piece_done.sem, 1)
                if (i + 1) % (NP * HALF) == 0:
                    join(group, h // HALF)

            def join(group, half):
                h = slice(half * HALF, (half + 1) * HALF)
                dve.wait_ge(piece_done.sem, when(piece_done, group, NP * HG, (half + 1) * HALF * NP - 1))
                dve.tensor_copy(negmax[:, h, 0:TC], piece_negmax[:, h, 0:TC]).then_inc(joined.sem, 1)
                dve.tensor_tensor(negmax[:, h, TC:NT], piece_negmax[:, h, TC:NP:2], piece_negmax[:, h, TC + 1:NP:2],
                                  ALU.min).then_inc(joined.sem, 1)
                dve.wait_ge(joined.sem, when(joined, group, 2 * 2, 2 * half + 1))
                dve.wait_ge(shift_ready.sem, when(shift_ready, group, 2, half - 2))
                dve.tensor_copy(negmax_parts[:, half, 0], negmax[:, h, :]).then_inc(parts_done.sem, 1)
                dve.wait_ge(parts_done.sem, when(parts_done, group, 2 * 2, 2 * half))
                dve.tensor_tensor(negmax_parts[:, half, 1], negmax[:, h, :], negmax_parts[:, half, 0],
                                  ALU.subtract).then_inc(parts_done.sem, 1)

            def normalise(group, c):
                ot = ot_ps[:, :].rearrange("p (t h w) -> p t h w", t=TC, h=HG)
                dve.wait_ge(ot_ready.sem, when(ot_ready, group, NC, c))
                dve.reciprocal(inv_sum[:, c], ot[:, :, :, HD1]).then_inc(summed.sem, 1)
                dve.wait_ge(summed.sem, when(summed, group, NC, c))
                dve.wait_ge(att_stored[c], (group[0] * SLOTS + group[1]) * 16 + 16)
                dve.tensor_tensor(att[:, c], ot[:, :, :, 0:HD1],
                                  inv_sum[:, c].unsqueeze(3).to_broadcast([P, TC, HG, HD1]),
                                  ALU.mult).then_inc(att_ready.sem, 1)

            def first(group):
                for i in range(NP * HG):
                    reduce_piece(group, i)

            def group_work(group, previous, following):
                piece = 0
                for i in range(NS * HG):
                    if following:
                        for _ in range(PIECES_AT[i]):
                            reduce_piece(following, piece)
                            piece += 1
                    if i == 2 * HG + HG - 1 and previous:
                        normalise(previous, 1)
                    if i == 7 * HG + HG - 1:
                        normalise(group, 0)
                if not following:
                    normalise(group, 1)

            groups(dve, group_work, first)

        @block.gpsimd
        def _(pool):
            pool.memset(w_raw[:, 0:DOWN0].rearrange("p (k n) -> p k n", k=KD)[:, :, (UT - 1) * P:UT * P], 0.0)\
                .then_inc(w_zeroed, 1)
            pool.wait_ge(w_zeroed, 1)
            pool.memset(w_raw[:, WCOLS - D:WCOLS], 0.0).then_inc(w_zeroed, 1)
            pool.wait_ge(w_zeroed, 2)
            pool.memset(k_stack[STK:STK + SHIFT, :, :, :], 1.0).then_inc(shift_ones, 1)
            pool.wait_ge(shift_ones, 1)

            pool.wait_ge(bias_in, 16)

            def low_parts(l):
                for i in range(4):
                    cols = slice(i * PIECE, (i + 1) * PIECE)
                    pool.wait_ge(w_high_done.sem, w_high_done.of(l, i))
                    pool.tensor_tensor(as_fast(w_raw[:, cols]), w_raw[:, cols], w_high[:, cols], ALU.subtract)\
                        .then_inc(w_low_done.sem, 1)

            def group_work(group, previous, following):
                for n in DIAGONAL:
                    q0 = first_query(*SETS[n])
                    wait_apart(pool, passed, exp_done.sem, when(exp_done, group, NS * HG, n * HG + HG - 1))
                    diagonal = probs[:, n % 3, :, q0:q0 + P]
                    pool.affine_select(out=diagonal, in_=diagonal, compare_op=ALU.is_ge, fill=0.0, base=0,
                                       pattern=[[0, HG], [1, P]], channel_multiplier=-1).then_inc(masked.sem, 1)
                    if n == DIAGONAL[TC - 1]:
                        for k in range(2):
                            x_tile = x_all[:, bass.ds((group[0] * SLOTS + group[1]) * 2 + k, 1), :]
                            pool.tensor_tensor(x_tile, x_tile, b_o[:, :].unsqueeze(1), ALU.add).then_inc(biased, 1)
                    if splits(group) and n == DIAGONAL[TC - 1]:
                        low_parts(1)

            groups(pool, group_work, lambda group: low_parts(0))


def project_causal(nc, x_all, ident, neg_half, passed, a):
    with ExitStack() as ctx:
        sb = lambda name, shape, dt=F32: ctx.enter_context(nc.sbuf_tensor(name, shape, dt))
        ps = lambda name: ctx.enter_context(nc.psum_tensor(name, [P, CH], F32))
        sem = lambda name: ctx.enter_context(nc.semaphore(name))
        count = lambda name, credit=0, per=NT: Count(sem(name), per, credit)

        w_o = sb("w_o", [P, KD, D])
        att = sb("att_in", [P, 4, NG, GF])
        att_t = sb("att_t", [P, 2, KD, P])
        x1 = sb("x1", [P, 4, D])
        stats = sb("stats1", [P, 2, 6])
        mean_var = sb("mean_var1", [P, 4, 2])
        var_eps = sb("var_eps1", [P, 2])
        rstd = sb("rstd1", [P, 4])
        xn = sb("xn1", [P, 2, D])
        xn_t = sb("xn1_t", [P, NC, KD, CH])
        at_ps = [ps(f"at_ps{i}") for i in range(2)]
        y_ps = [ps(f"y_ps{i}") for i in range(2)]
        xt_ps = [ps(f"xt_ps{i}") for i in range(2)]

        weights_in = sem("w_o_in")
        att_in = [sem(f"att_in{i}") for i in range(4)]
        at_ready = count("at_ready", 4)
        att_t_ready = count("att_t_ready", 2)
        y_ready = count("y_ready", 2)
        x1_ready = count("x1_ready", 2)
        counted = count("counted1")
        averaged = count("averaged1")
        var_ready = count("var_ready1")
        rstd_ready = count("rstd_ready1")
        xn_ready = count("xn1_ready", 4)
        xt_ready = count("xt_ready", 2)
        xt_copied = count("xt_copied", 2)
        x1_stored = [sem(f"x1_stored{i}") for i in range(4)]
        xt_stored = [sem(f"xt_stored{i}") for i in range(NC)]
        block = ctx.enter_context(nc.Block())

        STAGES_DEEP = 6

        def run(eng, step):
            for s in range(NT):
                step(0, lambda lag: s - lag if s >= lag else None)
            with eng.Fori(0, B - 1) as b:
                for s in range(NT):
                    step(b + 1, lambda lag: s - lag)
            for s in range(NT, NT + STAGES_DEEP - 1):
                step(B - 1, lambda lag: s - lag if s - lag < NT else None)

        @block.sync
        def _(sp):
            sp.dma_start(w_o[:, :, :], a["wo"].rearrange("(k p) n -> p k n", p=P)).then_inc(weights_in, 16)
            for s in x1_stored + xt_stored:
                sp.sem_inc(s, 16)

            def load(i):
                b, t = i // NT, i % NT
                sp.wait_ge(at_ready.sem, at_ready.of(b, t - 4))
                sp.dma_start(att[:, t % 4], a["att_scratch"][b * NG:(b + 1) * NG, t * P:(t + 1) * P, :]
                             .rearrange("g p n -> p g n")).then_inc(att_in[t % 4], 16)

            def store_xt(i):
                b, t = i // NT, i % NT
                if i >= 0 and t % TC == TC - 1:
                    c = t // TC
                    sp.wait_ge(xt_copied.sem, xt_copied.of(b, t))
                    sp.dma_start(a["xt_scratch"][b, :, :, c * CH:(c + 1) * CH].rearrange("k p t -> p k t"),
                                 xn_t[:, c]).then_inc(xt_stored[c], 16)

            for i in range(4):
                load(i)
            for i in range(B * NT):
                b, t = i // NT, i % NT
                sp.wait_ge(x1_ready.sem, x1_ready.of(b, t))
                sp.dma_start(a["x1_scratch"][b, t * P:(t + 1) * P, :], x1[:, t % 4]).then_inc(x1_stored[t % 4], 16)
                if i + 4 < B * NT:
                    load(i + 4)
                store_xt(i - 3)
            for i in range(B * NT - 3, B * NT):
                store_xt(i)
            for s in x1_stored:
                sp.wait_ge(s, 16 * (B * NT // 4 + 1))
            for s in xt_stored:
                sp.wait_ge(s, 16 * (B + 1))

        @block.tensor
        def _(pe):
            for c in (at_ready, y_ready, xt_ready):
                pe.sem_inc(c.sem, c.credit)
            pe.wait_ge(weights_in, 16)

            def turn_att(b, t):
                pe.wait_ge(att_in[t % 4], b * (16 * NT // 4) + 16 * (t // 4 + 1))
                pe.wait_ge(att_t_ready.sem, att_t_ready.of(b, t - 2))
                for k in range(KD):
                    mm = pe.transpose(at_ps[t % 2][:, k * P:(k + 1) * P], att[:, t % 4, 2 * k:2 * k + 2, :], ident[:, :])
                mm.then_inc(at_ready.sem, 1)

            def project(b, t):
                pe.wait_ge(att_t_ready.sem, att_t_ready.of(b, t))
                pe.wait_ge(x1_ready.sem, x1_ready.of(b, t - 2))
                for k in range(KD):
                    mm = pe.matmul(y_ps[t % 2][:, 0:D], att_t[:, t % 2, k, :], w_o[:, k, :],
                                   start=k == 0, stop=k == KD - 1)
                mm.then_inc(y_ready.sem, 1)

            def turn_x(b, t):
                pe.wait_ge(xn_ready.sem, xn_ready.of(b, t))
                pe.wait_ge(xt_copied.sem, xt_copied.of(b, t - 2))
                for k in range(KD):
                    mm = pe.transpose(xt_ps[t % 2][:, k * P:(k + 1) * P], xn[:, t % 2, k * P:(k + 1) * P], ident[:, :])
                mm.then_inc(xt_ready.sem, 1)

            def step(b, tile):
                for stage, lag in ((turn_att, 0), (project, 1), (turn_x, 5)):
                    if tile(lag) is not None:
                        stage(b, tile(lag))

            run(pe, step)

        @block.scalar
        def _(act):
            for c in (att_t_ready, xt_copied):
                act.sem_inc(c.sem, c.credit)

            def copy_att(b, t):
                act.wait_ge(at_ready.sem, at_ready.of(b, t))
                act.wait_ge(y_ready.sem, y_ready.of(b, t - 2))
                act.copy(att_t[:, t % 2], at_ps[t % 2][:, 0:D].rearrange("p (k t) -> p k t", k=KD))\
                   .then_inc(att_t_ready.sem, 1)

            def copy_xt(b, t):
                c = t // TC % NC
                act.wait_ge(xt_ready.sem, xt_ready.of(b, t))
                act.wait_ge(xt_stored[c], (b + t // NT) * 16 + 16)
                act.copy(xn_t[:, c, :, (t % TC) * P:(t % TC + 1) * P],
                         xt_ps[t % 2][:, 0:D].rearrange("p (k t) -> p k t", k=KD)).then_inc(xt_copied.sem, 1)

            def step(b, tile):
                for stage, lag in ((copy_att, 0), (copy_xt, 5)):
                    if tile(lag) is not None:
                        stage(b, tile(lag))

            run(act, step)

        @block.gpsimd
        def _(pool):
            def deviation(b, t):
                wait_apart(pool, passed, averaged.sem, averaged.of(b, t))
                pool.tensor_scalar(var_eps[:, t % 2:t % 2 + 1], mean_var[:, t % 4, 1:2], EPS, None, ALU.add)\
                    .then_inc(var_ready.sem, 1)
                pool.wait_ge(xn_ready.sem, xn_ready.of(b, t - 4))
                pool.wait_ge(var_ready.sem, var_ready.of(b, t))
                pool.tensor_tensor(rstd[:, t % 4:t % 4 + 1], var_eps[:, t % 2:t % 2 + 1], neg_half[:, 0:1],
                                   ALU.pow).then_inc(rstd_ready.sem, 1)

            def step(b, tile):
                if tile(2) is not None:
                    deviation(b, tile(2))

            run(pool, step)

        @block.vector
        def _(dve):
            for c in (x1_ready, xn_ready):
                dve.sem_inc(c.sem, c.credit)

            def residual(b, t):
                dve.wait_ge(y_ready.sem, y_ready.of(b, t))
                dve.wait_ge(x1_stored[t % 4], b * (16 * NT // 4) + 16 * (t // 4 + 1))
                dve.wait_ge(xn_ready.sem, xn_ready.of(b, t - 4))
                dve.tensor_tensor(x1[:, t % 4, :].unsqueeze(1), y_ps[t % 2][:, 0:D].unsqueeze(1),
                                  x_all[:, bass.ds(b * NT + t, 1), :], ALU.add).then_inc(x1_ready.sem, 1)

            def statistics(b, t):
                dve.wait_ge(x1_ready.sem, x1_ready.of(b, t))
                dve.bn_stats(stats[:, t % 2, :], x1[:, t % 4, :]).then_inc(counted.sem, 1)

            def average(b, t):
                wait_apart(dve, passed, counted.sem, counted.of(b, t))
                dve.bn_aggr(mean_var[:, t % 4, :], stats[:, t % 2, :]).then_inc(averaged.sem, 1)

            def normalise(b, t):
                dve.wait_ge(rstd_ready.sem, rstd_ready.of(b, t))
                dve.wait_ge(xt_ready.sem, xt_ready.of(b, t - 2))
                dve.tensor_scalar(xn[:, t % 2, :], x1[:, t % 4, :], mean_var[:, t % 4, 0:1], rstd[:, t % 4:t % 4 + 1],
                                  ALU.subtract, ALU.mult).then_inc(xn_ready.sem, 1)

            def step(b, tile):
                for stage, lag in ((residual, 0), (average, 2), (statistics, 1), (normalise, 3)):
                    if tile(lag) is not None:
                        stage(b, tile(lag))

            run(dve, step)



PAIRS = H2 // 2
PW = 2 * WIN
WPC = CH // WIN
UNITS = NT * PAIRS
GROUPS = UNITS // 2
AHEAD = 3
PARTS = ((0, 0), (0, 1), (1, 0))
GS = 4
EARLY = 2
OUT_AT, NORM_AT = 5 * PAIRS + 1, 6 * PAIRS
LAST = DEPTH * B - 1


def place(u, h):
    q = u % PAIRS
    return q // 2 * 2 + h, q % 2


def layers(nc, ident, neg_half, passed, a):
    with ExitStack() as ctx:
        sb = lambda name, shape, dt=F32: ctx.enter_context(nc.sbuf_tensor(name, shape, dt))
        sem = lambda name: ctx.enter_context(nc.semaphore(name))
        count = lambda name, per, credit=0: Count(sem(name), per, credit)
        qkv_ps = ctx.enter_context(nc.psum_tensor("qkv_ps", [P, 3 * CH], F32))
        turn_ps, s0, s1, pt_ps, o_ps = [ctx.enter_context(nc.psum_tensor(n, [P, CH], F32))
                                        for n in ("turn_ps2", "s2_ps0", "s2_ps1", "pt_ps2", "o_ps2")]
        q_ps, v_ps, s_ps = qkv_ps[:, 0:2 * CH], qkv_ps[:, 2 * CH:3 * CH], (s0, s1)
        ln_ps = (qkv_ps[:, 0:CH], qkv_ps[:, CH:2 * CH])
        pair = ((s0, s1), (pt_ps, o_ps))
        up_pair = lambda c, j: pair[(c + j) % 2]

        w_qkv = sb("w_qkv", [P, KD, 3 * INNER])
        w_out = sb("w_out", [P, INNER // P, D])
        w_ffn = sb("w_ffn", [P, 2, WCOLS], F32R)
        w_up = lambda part, k, tile: w_ffn[:, part, (k * UT + tile) * P:(k * UT + tile + 1) * P]
        w_down = lambda part, j, m: w_ffn[:, part, DOWN0 + j * D + m * P:DOWN0 + j * D + (m + 1) * P]
        b_up = sb("b_up", [P, 2, HT])
        b_down = sb("b_down", [P, KD])
        ln_g = sb("ln_g", [P, KD])
        ln_b = sb("ln_b", [P, KD])
        head_scale = sb("head_scale", [P, 4, HD2])
        turn_by = sb("turn_by", [P, NT, 4, HD2])
        band = sb("band", [P, PW])
        x_in = sb("x_in", [P, KD, T + 1])
        x_mid = sb("x_mid", [P, KD, T + 1])
        squares = sb("squares", [P, 2 * INNER])
        inv_norm = sb("inv_norm", [P, 2 * H2])
        sum_sq = sb("sum_sq", [P, 2, 2 * H2])
        qn = sb("qn", [P, 2 * INNER])
        rot_c = sb("rot_c", [P, 2 * INNER])
        rot_s = sb("rot_s", [P, 2 * INNER])
        q_t = sb("q_t", [P, 2, PAIRS, P])
        k_t = sb("k_t", [P, PAIRS, T])
        v_sb = sb("v_tok", [P, NT, INNER])
        p_sb = sb("p_sb", [P, 4, 2, PW])
        negmax = sb("negmax2", [P, 4, 2])
        total = sb("total", [P, 4, 2])
        inv_total = sb("inv_total", [P, 4, 2])
        p_t = sb("p_t", [P, 4, 2, 2, P])
        o_t = sb("o_t", [P, PAIRS, T])
        stats = sb("stats2", [P, NT, 6])
        mean_var = sb("mean_var2", [P, NT, 2])
        var_eps = sb("var_eps2", [P, NT])
        rstd = sb("rstd2", [P, NT])
        hn = sb("hn", [P, TC, D])
        full_t = lambda k: hn[:, :, :].rearrange("p t d -> p (t d)")[:, k * CH:(k + 1) * CH]
        hn_t = sb("hn_t", [P, 2, KD, CH], F32R)
        gate = sb("gate", [P, GS, CH])
        hidden = sb("hidden", [P, 2, HT, CH], F32R)

        qkv_weights_in = sem("qkv_weights_in")
        ffn_weights_in = sem("ffn_weights_in")
        parts_in = sem("parts_in")
        qkv_go = count("qkv_go", 1)
        tables_go = count("tables_go", 1)
        ffn_go = count("ffn_go", 1)
        x_loaded = sem("x_loaded")
        tables_in = sem("tables_in")
        pads = sem("pads")
        scaled_tables = count("scaled_tables", 1, 1)
        q_ready = count("q_ready", NT)
        v_ready = count("v_ready2", NT, 1)
        squared = count("squared", NT, 1)
        v_copied = count("v_copied2", NT, 1)
        summed = count("summed2", NT)
        clamped = count("clamped", NT, 1)
        inv_ready = count("inv_ready", NT)
        qn_ready = count("qn_ready", NT, 1)
        cos_ready = count("cos_ready", NT, 1)
        sin_ready = count("sin_ready", 4 * NT, 4)
        rot_ready = count("rot_ready", NT, 2)
        turned = count("turned2", 2 * NT, 4)
        turn_copied = count("turn_copied", 2 * NT, 1)
        s_ready = count("s_ready2", UNITS, 8)
        s_masked = count("s_masked", 2 * UNITS, 4)
        exp_done = count("exp_done2", 2 * UNITS)
        inv_sum = count("inv_sum", UNITS)
        scaled = count("scaled", 2 * UNITS)
        pt_ready = count("pt_ready", UNITS, 4)
        pt_copied = count("pt_copied", UNITS, 1)
        pv_done = count("pv_done2", GROUPS, 2)
        o_copied = count("o_copied2", NT, 1)
        wo_ready = count("wo_ready", NC * KD, 4)
        mid_ready = count("mid_ready2", NC * KD, 4)
        ln_ready = count("ln_ready", NC * 2)
        counted = count("counted2", NT)
        averaged = count("averaged2", NT)
        var_ready = count("var_ready2", NC)
        rstd_ready = count("rstd_ready2", NC)
        hn_ready = count("hn_ready", NT)
        back_ready = count("back_ready", NC * KD, 1)
        hn_t_ready = count("hn_t_ready", NC * KD, 1)
        hn_t_split = count("hn_t_split", NC * KD, 1)
        up_ready = count("up_ready", NC * HT)
        gelu_done = count("gelu_done", NC * HT)
        hidden_ready = count("hidden_ready", NC * HT, 2)
        hidden_high = count("hidden_high", NC * HT)
        hidden_split = count("hidden_split", NC * HT, GS)
        down_ready = count("down_ready", NC * KD)
        out_ready = count("out_ready", NC * KD, 2)
        out_stored = [sem(f"out_stored{k}") for k in range(KD)]
        block = ctx.enter_context(nc.Block())

        @block.sync
        def _(sp):
            def load_qkv_weights(l):
                dmas = [(w_qkv[:, :, :], a["wqkv"][l].rearrange("(k p) n -> p k n", p=P))]
                half = HD2 // 2
                for j, name in ((0, "q_scale"), (2, "k_scale")):
                    dmas += [(head_scale[:, j, :], a[name][l].partition_broadcast(P)),
                             (head_scale[:, j + 1, 0:half], a[name][l, half:HD2].partition_broadcast(P)),
                             (head_scale[:, j + 1, half:HD2], a[name][l, 0:half].partition_broadcast(P))]
                for dst, src in dmas:
                    sp.dma_start(dst, src).then_inc(qkv_weights_in, 16)
                return 16 * len(dmas)

            def load_ffn_weights(l):
                dmas = [(w_out[:, :, :], a["wo2"][l].rearrange("(k p) n -> p k n", p=P))]
                for j in range(2):
                    whole = a["b1"][l, j * HID:j * HID + (HT - 1) * P]
                    rest = a["b1"][l, j * HID + (HT - 1) * P:(j + 1) * HID]
                    dmas += [(b_up[:, j, 0:HT - 1], whole.rearrange("(k p) -> p k", p=P)),
                             (b_up[j * GL:j * GL + HL, j, HT - 1:HT], rest.rearrange("(p k) -> p k", k=1))]
                dmas += [(dst[:, :], a[name][l].rearrange("(k p) -> p k", p=P))
                         for dst, name in ((b_down, "b2"), (ln_g, "ln_g"), (ln_b, "ln_b"))]
                for dst, src in dmas:
                    sp.dma_start(dst, src, allow_slow_non_contiguous=True).then_inc(ffn_weights_in, 16)
                return 16 * len(dmas)

            def load_x(it):
                if it >= B:
                    for s in out_stored:
                        sp.wait_ge(s, 16 * (NC * (it - B + 1) + 1))
                for k in range(KD):
                    sp.dma_start(x_in[:, k, k:k + T], a["xt_scratch"][it % B, k]).then_inc(x_loaded, 16)

            for s in out_stored:
                sp.sem_inc(s, 16)
            def load_tables():
                sp.dma_start(turn_by[:, :, :, :].rearrange("p t j d -> p t (j d)"),
                             a["rotary"].rearrange("(t p) j d -> p t (j d)", p=P)).then_inc(tables_in, 16)

            load_x(0)
            per_layer = load_qkv_weights(0)
            load_tables()
            sp.wait_ge(x_loaded, 16 * KD)
            sp.wait_ge(qkv_weights_in, per_layer)
            sp.sem_inc(qkv_go.sem, 1)
            sp.wait_ge(tables_in, 16)
            sp.sem_inc(tables_go.sem, 1)
            per_layer_ffn = load_ffn_weights(0)
            for it in range(DEPTH * B):
                layer_ends = it == B - 1
                if it % B == 0:
                    sp.wait_ge(ffn_weights_in, per_layer_ffn * (it // B + 1))
                    sp.wait_ge(parts_in, 32 * (it // B + 1))
                sp.sem_inc(ffn_go.sem, 1)
                if layer_ends:
                    sp.wait_ge(v_ready.sem, v_ready.of(it, NT - 1))
                    load_qkv_weights(1)
                if it < LAST:
                    sp.wait_ge(rot_ready.sem, rot_ready.of(it, NT - 1))
                    load_tables()
                    sp.wait_ge(mid_ready.sem, mid_ready.of(it, NC * KD - 1))
                    load_x(it + 1)
                    sp.wait_ge(x_loaded, 16 * KD * (it + 2))
                    if layer_ends:
                        sp.wait_ge(qkv_weights_in, 2 * per_layer)
                    sp.sem_inc(qkv_go.sem, 1)
                    sp.wait_ge(tables_in, 16 * (it + 2))
                    sp.sem_inc(tables_go.sem, 1)
                for c in range(NC):
                    for k in range(KD):
                        sp.wait_ge(out_ready.sem, out_ready.of(it, c * KD + k))
                        sp.dma_start(a["xt_scratch"][it % B, k, :, c * CH:(c + 1) * CH],
                                     x_mid[:, k, k + c * CH:k + (c + 1) * CH])\
                            .then_inc(out_stored[k], 16)
                if layer_ends:
                    load_ffn_weights(1)
            for s in out_stored:
                sp.wait_ge(s, 16 * (NC * DEPTH * B + 1))

        @block.tensor
        def _(pe):
            for c in (v_ready, turned, s_ready, pt_ready, pv_done, wo_ready, back_ready):
                pe.sem_inc(c.sem, c.credit)
            pe.wait_ge(pads, 3)

            def project(it, w, part):
                if w == 0 and part == 0:
                    pe.wait_ge(qkv_go.sem, qkv_go.of(it, 0))
                    pe.wait_ge(hn_t_ready.sem, hn_t_ready.of(it, -1))
                if part < 2:
                    pe.wait_ge(qn_ready.sem, qn_ready.of(it, w - 1))
                else:
                    pe.wait_ge(v_copied.sem, v_copied.of(it, w - 1))
                for k in range(KD):
                    mm = pe.matmul(qkv_ps[:, part * CH:(part + 1) * CH], x_in[:, k, w * P:(w + 1) * P],
                                   w_qkv[:, k, part * INNER:(part + 1) * INNER], start=k == 0, stop=k == KD - 1)
                if part == 1:
                    mm.then_inc(q_ready.sem, 1)
                if part == 2:
                    mm.then_inc(v_ready.sem, 1)

            def turn(it, w, j):
                pe.wait_ge(rot_ready.sem, rot_ready.of(it, w))
                pe.wait_ge(turn_copied.sem, turn_copied.of(it, 2 * w + j - 1))
                for p in range(PAIRS):
                    mm = pe.transpose(turn_ps[:, p * P:(p + 1) * P],
                                      rot_c[:, j * INNER + p * P:j * INNER + (p + 1) * P], ident[:, :])
                mm.then_inc(turned.sem, 1)

            def scores(it, u):
                w = u // PAIRS
                pe.wait_ge(turn_copied.sem, turn_copied.of(it, 2 * w + 1))
                pe.wait_ge(s_masked.sem, s_masked.of(it, 2 * u - 3))
                if u == 0:
                    pe.wait_ge(hidden_ready.sem, hidden_ready.of(it, -1))
                k0 = max(0, w - 1) * P
                for h in range(2):
                    p, side = place(u, h)
                    r = slice(side * HD2, (side + 1) * HD2)
                    mm = pe.matmul(s_ps[u % 2][:, (h + 1) * PW - ((w + 1) * P - k0):(h + 1) * PW],
                                   q_t[r, w % 2, p, :], k_t[r, p, k0:(w + 1) * P], start=True, stop=True)
                mm.then_inc(s_ready.sem, 1)

            def project_out(it, c, m):
                if c == 0 and m == 0:
                    pe.wait_ge(ffn_go.sem, ffn_go.of(it, 0))
                    pe.wait_ge(qn_ready.sem, qn_ready.of(it, NT - 1))
                if c == 1 and m == 0:
                    pe.wait_ge(hn_t_ready.sem, hn_t_ready.of(it, KD - 1))
                pe.wait_ge(o_copied.sem, o_copied.of(it, (c + 1) * WPC - 1))
                for k in range(INNER // P):
                    mm = pe.matmul(ln_ps[m], w_out[:, k, m * P:(m + 1) * P],
                                   o_t[:, k, c * CH:(c + 1) * CH], start=k == 0, stop=k == INNER // P - 1)
                mm.then_inc(wo_ready.sem, 1)

            def tokens_first(it, c):
                pe.wait_ge(mid_ready.sem, mid_ready.of(it, (c + 1) * KD - 1))
                for t in range(TC):
                    for k in range(KD):
                        mm = pe.transpose(ln_ps[t // 2][:, (t % 2) * D + k * P:(t % 2) * D + (k + 1) * P],
                                          x_mid[:, k, c * CH + t * P:c * CH + (t + 1) * P], ident[:, :])
                    if t % 2:
                        mm.then_inc(ln_ready.sem, 1)

            def features_first(it, c):
                pe.wait_ge(hn_ready.sem, hn_ready.of(it, (c + 1) * TC - 1))
                for k in range(KD):
                    for t in range(TC):
                        mm = pe.transpose(ln_ps[k][:, t * P:(t + 1) * P], hn[:, t, k * P:(k + 1) * P],
                                          ident[:, :])
                    mm.then_inc(back_ready.sem, 1)

            def up(it, c, j):
                i = c * HT + j
                pe.wait_ge(hn_t_split.sem, hn_t_split.of(it, (c + 1) * KD - 1))
                if i == 0:
                    pe.wait_ge(s_masked.sem, s_masked.of(it, 2 * UNITS - 1))
                elif i == 1:
                    pe.wait_ge(pt_copied.sem, pt_copied.of(it, UNITS - 1))
                    pe.wait_ge(o_copied.sem, o_copied.of(it, NT - 1))
                elif i == HT:
                    pe.wait_ge(hidden_ready.sem, hidden_ready.of(it, i - 1))
                elif i == HT + 1:
                    pe.wait_ge(out_ready.sem, out_ready.of(it, KD - 1))
                elif i > 1:
                    pe.wait_ge(hidden_ready.sem, hidden_ready.of(it, i - 2))
                outs = [(0, j, P), (1, HT - 1 + j, P)] if j < HT - 1 else [(0, UT - 1, GL + HL)]
                for bank, tile, rows in outs:
                    steps = [(k, w, h) for k in range(KD) for w, h in PARTS]
                    for n, (k, w, h) in enumerate(steps):
                        mm = pe.matmul(up_pair(c, j)[bank][0:rows, :], w_up(w, k, tile)[:, 0:rows], hn_t[:, h, k, :],
                                       start=n == 0, stop=n == len(steps) - 1)
                mm.then_inc(up_ready.sem, 1)

            def attention(it):
                def turn_probs(u):
                    w = u // PAIRS
                    pe.wait_ge(scaled.sem, scaled.of(it, 2 * u + 1))
                    pe.wait_ge(pt_copied.sem, pt_copied.of(it, u - 1))
                    if u == 0:
                        pe.wait_ge(out_ready.sem, out_ready.of(it, -1))
                    for h in range(2):
                        for kt in range(0 if w else 1, 2):
                            mm = pe.transpose(pt_ps[:, (h * 2 + kt) * P:(h * 2 + kt + 1) * P],
                                              p_sb[:, u % 4, h, kt * P:(kt + 1) * P], ident[:, :])
                    mm.then_inc(pt_ready.sem, 1)

                def values(g):
                    w = 2 * g // PAIRS
                    pe.wait_ge(pt_copied.sem, pt_copied.of(it, 2 * g + 1))
                    pe.wait_ge(v_copied.sem, v_copied.of(it, w))
                    if 2 * g % PAIRS == 0:
                        pe.wait_ge(o_copied.sem, o_copied.of(it, w - 1))
                    for h in range(2):
                        for kt in range(0 if w else 1, 2):
                            for u in (2 * g, 2 * g + 1):
                                p, side = place(u, h)
                                head = 2 * p + side
                                mm = pe.matmul(o_ps[side * HD2:(side + 1) * HD2, p * P:(p + 1) * P],
                                               v_sb[:, w - 1 + kt, head * HD2:(head + 1) * HD2],
                                               p_t[:, u % 4, h, kt, :], start=kt == (0 if w else 1), stop=kt == 1,
                                               tile_position=(0, side * HD2))
                    mm.then_inc(pv_done.sem, 1)

                for u in range(UNITS + 3):
                    w, p = u // PAIRS, u % PAIRS
                    if EARLY <= u < UNITS:
                        scores(it, u)
                    if 2 <= u < UNITS + 2:
                        turn_probs(u - 2)
                    if p < 2 and w + 1 < NT:
                        turn(it, w + 1, p)
                    if p >= 1 and w + AHEAD < NT:
                        project(it, w + AHEAD, p - 1)
                    if OUT_AT <= u < OUT_AT + KD:
                        project_out(it, 0, u - OUT_AT)
                    if u == NORM_AT:
                        tokens_first(it, 0)
                    if u == NORM_AT + 5:
                        features_first(it, 0)
                    if u == UNITS:
                        up(it, 0, 0)
                    if u >= 4 and u % 2 == 0:
                        values((u - 4) // 2)

            def feed_forward(it, more):
                def down(c, m):
                    pe.wait_ge(hidden_split.sem, hidden_split.of(it, (c + 1) * HT - 2))
                    steps = [(j, w, h) for j in range(HT) for w, h in PARTS]
                    for n, (j, w, h) in enumerate(steps):
                        rows = P if j < HT - 1 else HL
                        if n == (HT - 1) * len(PARTS):
                            pe.wait_ge(hidden_split.sem, hidden_split.of(it, (c + 1) * HT - 1))
                        mm = pe.matmul(pair[c][m][:, :], w_down(w, j, m)[0:rows], hidden[0:rows, h, j, :],
                                       start=n == 0, stop=n == len(steps) - 1)
                    mm.then_inc(down_ready.sem, 1)

                def project_next(w):
                    if more:
                        for part in range(3):
                            project(it + 1, w, part)

                def turn_next(j):
                    if more:
                        turn(it + 1, 0, j)

                project_out(it, 1, 0)
                project_out(it, 1, 1)
                up(it, 0, 1)
                tokens_first(it, 1)
                for j in range(2, HT):
                    up(it, 0, j)
                features_first(it, 1)
                down(0, 0)
                project_next(0)
                down(0, 1)
                up(it, 1, 0)
                up(it, 1, 1)
                project_next(1)
                turn_next(0)
                up(it, 1, 2)
                turn_next(1)
                up(it, 1, 3)
                up(it, 1, 4)
                up(it, 1, 5)
                project_next(2)
                if more:
                    for u in range(EARLY):
                        scores(it + 1, u)
                down(1, 0)
                down(1, 1)

            for w in range(AHEAD):
                for part in range(3):
                    project(0, w, part)
                if w == 0:
                    turn(0, 0, 0)
                    turn(0, 0, 1)
            for u in range(EARLY):
                scores(0, u)
            with pe.Fori(0, LAST) as it:
                attention(it)
                feed_forward(it, True)
            attention(LAST)
            feed_forward(LAST, False)

        @block.scalar
        def _(act):
            for c in (squared, v_copied, turn_copied, pt_copied, o_copied, hn_t_ready):
                act.sem_inc(c.sem, c.credit)

            def square(it, w):
                act.wait_ge(q_ready.sem, q_ready.of(it, w))
                act.wait_ge(clamped.sem, clamped.of(it, w - 1))
                act.activation(squares[:, :], q_ps, ACT.Square).then_inc(squared.sem, 1)

            def copy_v(it, w):
                act.wait_ge(v_ready.sem, v_ready.of(it, w))
                act.copy(v_sb[:, w, :], v_ps).then_inc(v_copied.sem, 1)

            def copy_turned(it, w, j):
                act.wait_ge(turned.sem, turned.of(it, 2 * w + j))
                if j == 0:
                    act.wait_ge(s_ready.sem, s_ready.of(it, (w - 1) * PAIRS - 1))
                dst = q_t[:, w % 2, :, :] if j == 0 else k_t[:, :, w * P:(w + 1) * P]
                act.copy(dst, turn_ps[:, :].rearrange("p (h t) -> p h t", h=PAIRS)).then_inc(turn_copied.sem, 1)

            def exponentials(it, u):
                k0 = 0 if u // PAIRS else WIN
                for h in range(2):
                    act.wait_ge(s_masked.sem, s_masked.of(it, 2 * u + h))
                    act.activation(p_sb[:, u % 4, h, k0:PW], p_sb[:, u % 4, h, k0:PW], ACT.Exp, scale=-1.0,
                                   bias=negmax[:, u % 4, h:h + 1],
                                   accum_out=total[:, u % 4, h:h + 1]).then_inc(exp_done.sem, 1)

            def scale_norm(it, c):
                act.wait_ge(back_ready.sem, back_ready.of(it, (c + 1) * KD - 1))
                for k in range(KD):
                    for out in (full_t(k), hn_t[:, 0, k, :]):
                        ins = act.activation(out, ln_ps[k], ACT.Identity, bias=ln_b[:, k:k + 1], scale=ln_g[:, k:k + 1])
                    ins.then_inc(hn_t_ready.sem, 1)

            def attention(it):
                def copy_probs(u):
                    k0 = 0 if u // PAIRS else 1
                    act.wait_ge(pt_ready.sem, pt_ready.of(it, u))
                    act.wait_ge(pv_done.sem, pv_done.of(it, u // 2 - 2))
                    act.copy(p_t[:, u % 4, :, k0:2, :],
                             pt_ps[:, :].rearrange("p (h k t) -> p h k t", h=2, k=2)[:, :, k0:2, :])\
                       .then_inc(pt_copied.sem, 1)

                def copy_output(w):
                    act.wait_ge(pv_done.sem, pv_done.of(it, (w + 1) * PAIRS // 2 - 1))
                    if w == 0:
                        act.wait_ge(wo_ready.sem, wo_ready.of(it, -1))
                    act.copy(o_t[:, :, w * P:(w + 1) * P], o_ps[:, :].rearrange("p (h t) -> p h t", h=PAIRS))\
                       .then_inc(o_copied.sem, 1)

                for u in range(UNITS + 3):
                    w, p = u // PAIRS, u % PAIRS
                    if 2 <= u < UNITS + 2:
                        copy_probs(u - 2)
                    if EARLY <= u < UNITS:
                        exponentials(it, u)
                    if p < 2 and w + 1 < NT:
                        copy_turned(it, w + 1, p)
                    if p == 2 and w + AHEAD < NT:
                        square(it, w + AHEAD)
                    if p == 3 and w + AHEAD < NT:
                        copy_v(it, w + AHEAD)
                    if u >= PAIRS + 2 and (u - 2) % PAIRS == 0:
                        copy_output((u - 2) // PAIRS - 1)
                    if u == NORM_AT + 6:
                        scale_norm(it, 0)

            def feed_forward(it, more):
                def gelu(c, j):
                    i = c * HT + j
                    rows = P if j < HT - 1 else HL
                    act.wait_ge(up_ready.sem, up_ready.of(it, i))
                    act.wait_ge(hidden_split.sem, hidden_split.of(it, i - GS))
                    r0 = 0 if j < HT - 1 else GL
                    act.activation(gate[0:rows, i % GS, :], up_pair(c, j)[1 if j < HT - 1 else 0][r0:r0 + rows, :],
                                   ACT.Gelu, bias=b_up[r0:r0 + rows, 1, j:j + 1]).then_inc(gelu_done.sem, 1)

                def high(c, j):
                    rows = P if j < HT - 1 else HL
                    act.wait_ge(hidden_ready.sem, hidden_ready.of(it, c * HT + j))
                    if c and j == 0:
                        act.wait_ge(down_ready.sem, down_ready.of(it, c * KD - 1))
                    act.copy(hidden[0:rows, 0, j, :], gate[0:rows, (c * HT + j) % GS, :]).then_inc(hidden_high.sem, 1)

                for j in range(HT):
                    if j:
                        high(0, j - 1)
                    gelu(0, j)
                high(0, HT - 1)
                scale_norm(it, 1)
                if more:
                    square(it + 1, 0)
                    copy_v(it + 1, 0)
                for j in range(HT):
                    if j:
                        high(1, j - 1)
                    gelu(1, j)
                    if more and j == 1:
                        square(it + 1, 1)
                        copy_v(it + 1, 1)
                        copy_turned(it + 1, 0, 0)
                    if more and j == 2:
                        copy_turned(it + 1, 0, 1)
                high(1, HT - 1)
                if more:
                    square(it + 1, 2)
                    copy_v(it + 1, 2)
                if more:
                    for u in range(EARLY):
                        exponentials(it + 1, u)

            for w in range(AHEAD):
                square(0, w)
                copy_v(0, w)
                if w == 0:
                    copy_turned(0, 0, 0)
                    copy_turned(0, 0, 1)
            for u in range(EARLY):
                exponentials(0, u)
            with act.Fori(0, LAST) as it:
                attention(it)
                feed_forward(it, True)
            attention(LAST)
            feed_forward(LAST, False)

        @block.gpsimd
        def _(pool):
            for c in (scaled_tables, clamped, cos_ready, rot_ready):
                pool.sem_inc(c.sem, c.credit)
            pool.memset(x_in[:, 1, 0:1], 0.0).then_inc(pads, 1)
            pool.memset(x_mid[:, 1, 0:1], 0.0).then_inc(pads, 1)
            pool.memset(band[:, :], 0.0).then_inc(pads, 1)
            pool.wait_ge(pads, 3)
            pool.affine_select(out=band[:, 0:WIN], in_=band[:, 0:WIN], compare_op=ALU.is_ge, fill=BIG, base=0,
                               pattern=[[1, WIN]], channel_multiplier=-1).then_inc(pads, 1)
            pool.affine_select(out=band[:, WIN:PW], in_=band[:, WIN:PW], compare_op=ALU.is_ge, fill=BIG, base=0,
                               pattern=[[-1, WIN]], channel_multiplier=1).then_inc(pads, 1)

            def scale_tables(it):
                pool.wait_ge(tables_go.sem, tables_go.of(it, 0))
                for w in range(NT):
                    ins = pool.tensor_tensor(turn_by[:, w], turn_by[:, w], head_scale[:, :, :], ALU.mult)
                ins.then_inc(scaled_tables.sem, 1)
                pool.wait_ge(scaled_tables.sem, scaled_tables.of(it, 0))

            def norms(it, w):
                wait_apart(pool, passed, summed.sem, summed.of(it, w))
                pool.tensor_scalar(sum_sq[:, 1, :], sum_sq[:, 0, :], 1e-24, None, ALU.max).then_inc(clamped.sem, 1)
                pool.wait_ge(clamped.sem, clamped.of(it, w))
                pool.tensor_tensor(inv_norm[:, :], sum_sq[:, 1, :], neg_half[:, 0:2 * H2], ALU.pow)\
                    .then_inc(inv_ready.sem, 1)

            def rotate(it, w):
                pool.wait_ge(qn_ready.sem, qn_ready.of(it, w))
                pool.wait_ge(turned.sem, turned.of(it, 2 * w - 1))
                heads = lambda t, j: t[:, j * INNER:(j + 1) * INNER].rearrange("p (h d) -> p h d", h=H2)
                for j in range(2):
                    ins = pool.tensor_tensor(heads(rot_c, j), heads(qn, j), turn_by[:, w, 2 * j, :].unsqueeze(1)
                                             .to_broadcast([P, H2, HD2]), ALU.mult)
                ins.then_inc(cos_ready.sem, 1)
                pool.wait_ge(cos_ready.sem, cos_ready.of(it, w))
                pool.wait_ge(sin_ready.sem, sin_ready.of(it, 4 * w + 3))
                pool.tensor_tensor(rot_c[:, :], rot_c[:, :], rot_s[:, :], ALU.add).then_inc(rot_ready.sem, 1)

            def deviations(it, c):
                t = slice(c * TC, (c + 1) * TC)
                wait_apart(pool, passed, averaged.sem, averaged.of(it, (c + 1) * TC - 1))
                pool.tensor_scalar(var_eps[:, t], mean_var[:, t, 1], EPS, None, ALU.add).then_inc(var_ready.sem, 1)
                pool.wait_ge(var_ready.sem, var_ready.of(it, c))
                pool.tensor_tensor(rstd[:, t], var_eps[:, t], neg_half[:, 0:TC], ALU.pow).then_inc(rstd_ready.sem, 1)

            def first_windows(it):
                scale_tables(it)
                for w in range(AHEAD):
                    norms(it, w)
                    if w < AHEAD - 1:
                        rotate(it, w)

            def attention(it):
                for w in range(NT):
                    if w + 2 < NT:
                        rotate(it, w + 2)
                    if w + AHEAD < NT:
                        norms(it, w + AHEAD)
                deviations(it, 0)

            def feed_forward(it, more):
                deviations(it, 1)
                if more:
                    first_windows(it + 1)

            def load_ffn_weights(l):
                for part in range(2):
                    pool.dma_start(w_ffn[:, part, :], a["ffn_weights"][l, part]).then_inc(parts_in, 16)

            first_windows(0)
            load_ffn_weights(0)
            with pool.Fori(0, B - 1) as it:
                attention(it)
                feed_forward(it, True)
            attention(B - 1)
            feed_forward(B - 1, True)
            pool.wait_ge(down_ready.sem, down_ready.of(B - 1, NC * KD - 1))
            load_ffn_weights(1)
            with pool.Fori(0, B - 1) as b:
                attention(b + B)
                feed_forward(b + B, True)
            attention(LAST)
            feed_forward(LAST, False)

        @block.vector
        def _(dve):
            for c in (qn_ready, sin_ready, s_masked, mid_ready, hn_t_split, hidden_ready, hidden_split, out_ready):
                dve.sem_inc(c.sem, c.credit)
            dve.wait_ge(pads, 5)
            heads = lambda t: t.rearrange("p (h d) -> p h d", d=HD2)

            def sums(it, w):
                dve.wait_ge(squared.sem, squared.of(it, w))
                dve.wait_ge(clamped.sem, clamped.of(it, w - 1))
                dve.tensor_reduce(sum_sq[:, 0, :], heads(squares[:, :]), AX.X, ALU.add).then_inc(summed.sem, 1)

            def unit_vectors(it, w):
                dve.wait_ge(inv_ready.sem, inv_ready.of(it, w))
                dve.wait_ge(cos_ready.sem, cos_ready.of(it, w - 1))
                dve.wait_ge(sin_ready.sem, sin_ready.of(it, 4 * w - 1))
                dve.tensor_tensor(heads(qn[:, :]), heads(q_ps), inv_norm[:, :].unsqueeze(2)
                                  .to_broadcast([P, 2 * H2, HD2]), ALU.mult).then_inc(qn_ready.sem, 1)

            def times_sin(it, w):
                if w == 0:
                    dve.wait_ge(scaled_tables.sem, scaled_tables.of(it, 0))
                dve.wait_ge(qn_ready.sem, qn_ready.of(it, w))
                dve.wait_ge(rot_ready.sem, rot_ready.of(it, w - 1))
                half = HD2 // 2
                for j in range(2):
                    src = heads(qn[:, j * INNER:(j + 1) * INNER])
                    dst = heads(rot_s[:, j * INNER:(j + 1) * INNER])
                    for to in range(2):
                        o, i = slice(to * half, (to + 1) * half), slice((1 - to) * half, (2 - to) * half)
                        dve.tensor_tensor(dst[:, :, o], src[:, :, i], turn_by[:, w, 2 * j + 1, o].unsqueeze(1)
                                          .to_broadcast([P, H2, half]), ALU.mult).then_inc(sin_ready.sem, 1)

            def mask_scores(it, u):
                k0 = 0 if u // PAIRS else WIN
                for h in range(2):
                    if h == 0:
                        wait_apart(dve, passed, s_ready.sem, s_ready.of(it, u))
                        wait_apart(dve, passed, pt_ready.sem, pt_ready.of(it, u - 4))
                    dve.tensor_tensor_reduce(p_sb[:, u % 4, h, k0:PW], s_ps[u % 2][:, h * PW + k0:(h + 1) * PW],
                                             band[:, k0:PW], 1.0, BIG, ALU.add, ALU.min,
                                             negmax[:, u % 4, h:h + 1]).then_inc(s_masked.sem, 1)

            def residual(it, c, m):
                dve.wait_ge(wo_ready.sem, wo_ready.of(it, c * KD + m))
                if c == 0 and m == 0:
                    for stored in out_stored:
                        dve.wait_ge(stored, it * (16 * NC) + 16)
                s = slice(m + c * CH, m + (c + 1) * CH)
                dve.tensor_tensor(x_mid[:, m, s], ln_ps[m], x_in[:, m, s], ALU.add).then_inc(mid_ready.sem, 1)

            tile = lambda t: ln_ps[t % TC // 2][:, (t % 2) * D:(t % 2 + 1) * D]

            def statistics(it, c, half):
                tiles = range(c * TC + 2 * half, c * TC + 2 * half + 2)
                for t in tiles:
                    dve.wait_ge(ln_ready.sem, ln_ready.of(it, t // 2))
                    dve.bn_stats(stats[:, t, :], tile(t)).then_inc(counted.sem, 1)
                if half:
                    wait_apart(dve, passed, counted.sem, counted.of(it, (c + 1) * TC - 1))
                    for t in range(c * TC, (c + 1) * TC):
                        dve.bn_aggr(mean_var[:, t, :], stats[:, t, :]).then_inc(averaged.sem, 1)

            def normalise(it, c, half):
                dve.wait_ge(averaged.sem, averaged.of(it, (c + 1) * TC - 1))
                dve.wait_ge(rstd_ready.sem, rstd_ready.of(it, c))
                dve.wait_ge(hn_t_split.sem, hn_t_split.of(it, c * KD - 1))
                for t in range(c * TC + 2 * half, c * TC + 2 * half + 2):
                    dve.tensor_scalar(hn[:, t % TC, :], tile(t), mean_var[:, t, 0:1], rstd[:, t:t + 1],
                                      ALU.subtract, ALU.mult).then_inc(hn_ready.sem, 1)

            def split_norm(it, c):
                for k in range(KD):
                    dve.wait_ge(hn_t_ready.sem, hn_t_ready.of(it, c * KD + k))
                    dve.tensor_tensor(hn_t[:, 1, k, :], full_t(k), as_float(hn_t[:, 0, k, :]), ALU.subtract)\
                       .then_inc(hn_t_split.sem, 1)

            def attention(it):
                def invert_sums(u):
                    dve.wait_ge(exp_done.sem, exp_done.of(it, 2 * u + 1))
                    dve.reciprocal(inv_total[:, u % 4, :], total[:, u % 4, :]).then_inc(inv_sum.sem, 1)

                def scale_probs(u):
                    k0 = 0 if u // PAIRS else WIN
                    wait_apart(dve, passed, inv_sum.sem, inv_sum.of(it, u))
                    for h in range(2):
                        dve.tensor_scalar(p_sb[:, u % 4, h, k0:PW], p_sb[:, u % 4, h, k0:PW],
                                          inv_total[:, u % 4, h:h + 1], None, ALU.mult).then_inc(scaled.sem, 1)

                for u in range(UNITS + 1):
                    w, p = u // PAIRS, u % PAIRS
                    if p == 3 and w + AHEAD < NT:
                        sums(it, w + AHEAD)
                    if EARLY <= u < UNITS:
                        mask_scores(it, u)
                    if u:
                        invert_sums(u - 1)
                        scale_probs(u - 1)
                    if p == 0 and w + 2 < NT:
                        unit_vectors(it, w + 2)
                    if p == 1 and w + 2 < NT:
                        times_sin(it, w + 2)
                    if OUT_AT < u <= OUT_AT + KD:
                        residual(it, 0, u - OUT_AT - 1)
                    if u in (NORM_AT + 1, NORM_AT + 2):
                        statistics(it, 0, u - NORM_AT - 1)
                    if u in (NORM_AT + 3, NORM_AT + 4):
                        normalise(it, 0, u - NORM_AT - 3)
                    if u == NORM_AT + 7:
                        split_norm(it, 0)

            def feed_forward(it, more):
                def gated(c, j):
                    rows = P if j < HT - 1 else HL
                    dve.wait_ge(gelu_done.sem, gelu_done.of(it, c * HT + j))
                    slot = gate[0:rows, (c * HT + j) % GS, :]
                    dve.scalar_tensor_tensor(out=slot, in0=up_pair(c, j)[0][0:rows, :], scalar=b_up[0:rows, 0, j:j + 1],
                                             in1=slot, op0=ALU.add, op1=ALU.mult).then_inc(hidden_ready.sem, 1)

                def low(c, j):
                    rows = P if j < HT - 1 else HL
                    dve.wait_ge(hidden_high.sem, hidden_high.of(it, c * HT + j))
                    dve.tensor_tensor(hidden[0:rows, 1, j, :], gate[0:rows, (c * HT + j) % GS, :],
                                      as_float(hidden[0:rows, 0, j, :]), ALU.subtract).then_inc(hidden_split.sem, 1)

                def output(c, m):
                    dve.wait_ge(down_ready.sem, down_ready.of(it, c * KD + m))
                    s = slice(m + c * CH, m + (c + 1) * CH)
                    dve.scalar_tensor_tensor(out=x_mid[:, m, s], in0=pair[c][m][:, :], scalar=b_down[:, m:m + 1],
                                             in1=x_mid[:, m, s], op0=ALU.add, op1=ALU.add).then_inc(out_ready.sem, 1)

                residual(it, 1, 0)
                residual(it, 1, 1)
                for j in range(HT):
                    if j:
                        low(0, j - 1)
                    gated(0, j)
                    if j == 1:
                        statistics(it, 1, 0)
                        statistics(it, 1, 1)
                    if j == 2:
                        normalise(it, 1, 0)
                        normalise(it, 1, 1)
                low(0, HT - 1)
                split_norm(it, 1)
                output(0, 0)
                if more:
                    sums(it + 1, 0)
                output(0, 1)
                if more:
                    unit_vectors(it + 1, 0)
                for j in range(HT):
                    if j:
                        low(1, j - 1)
                    gated(1, j)
                    if more and j == 0:
                        times_sin(it + 1, 0)
                    if more and j == 2:
                        sums(it + 1, 1)
                    if more and j == 3:
                        unit_vectors(it + 1, 1)
                    if more and j == 4:
                        times_sin(it + 1, 1)
                low(1, HT - 1)
                if more:
                    mask_scores(it + 1, 0)
                    sums(it + 1, 2)
                output(1, 0)
                if more:
                    mask_scores(it + 1, 1)
                output(1, 1)

            for w in range(AHEAD):
                sums(0, w)
                if w < AHEAD - 1:
                    unit_vectors(0, w)
                    times_sin(0, w)
            for u in range(EARLY):
                mask_scores(0, u)
            with dve.Fori(0, LAST) as it:
                attention(it)
                feed_forward(it, True)
            attention(LAST)
            feed_forward(LAST, False)


def finish(nc, ident, a):
    with ExitStack() as ctx:
        sb = lambda name, shape, dt=F32: ctx.enter_context(nc.sbuf_tensor(name, shape, dt))
        sem = lambda name: ctx.enter_context(nc.semaphore(name))
        y_t = sb("y_t", [P, NC, KD, CH])
        x1 = sb("x1_f", [P, NC, TC, D])
        out = sb("out_f", [P, NC, TC, D])
        y_ps = [ctx.enter_context(nc.psum_tensor(f"yt_ps{i}", [P, CH], F32)) for i in range(4)]
        loaded = [sem(f"loaded_f{c}") for c in range(NC)]
        turned = Count(sem("turned_f"), NT, NT)
        added = Count(sem("added_f"), NT, NT)
        stored = [sem(f"stored_f{c}") for c in range(NC)]
        block = ctx.enter_context(nc.Block())

        @block.sync
        def _(sp):
            for s in stored:
                sp.sem_inc(s, 16)

            def load(i):
                b, c = i // NC, i % NC
                if b:
                    sp.wait_ge(added.sem, added.of(b - 1, (c + 1) * TC - 1))
                sp.dma_start(y_t[:, c], a["xt_scratch"][b, :, :, c * CH:(c + 1) * CH].rearrange("k p t -> p k t"))\
                    .then_inc(loaded[c], 16)
                sp.dma_start(x1[:, c], a["x1_scratch"][b, c * CH:(c + 1) * CH, :].rearrange("(t p) d -> p t d", p=P))\
                    .then_inc(loaded[c], 16)

            for i in range(NC):
                load(i)
            for i in range(B * NC):
                b, c = i // NC, i % NC
                sp.wait_ge(added.sem, added.of(b, (c + 1) * TC - 1))
                sp.dma_start(a["out"][b, c * CH:(c + 1) * CH, :].rearrange("(t p) d -> p t d", p=P), out[:, c])\
                    .then_inc(stored[c], 16)
                if i + NC < B * NC:
                    load(i + NC)
            for s in stored:
                sp.wait_ge(s, 16 * (B + 1))

        @block.tensor
        def _(pe):
            pe.sem_inc(turned.sem, turned.credit)
            with pe.Fori(0, B) as b:
                for t in range(NT):
                    if t % TC == 0:
                        pe.wait_ge(loaded[t // TC], b * 32 + 32)
                    pe.wait_ge(added.sem, added.of(b, t - 4))
                    for k in range(KD):
                        mm = pe.transpose(y_ps[t % 4][:, k * P:(k + 1) * P],
                                          y_t[:, t // TC, k, (t % TC) * P:(t % TC + 1) * P], ident[:, :])
                    mm.then_inc(turned.sem, 1)

        @block.vector
        def _(dve):
            dve.sem_inc(added.sem, added.credit)
            with dve.Fori(0, B) as b:
                for t in range(NT):
                    dve.wait_ge(turned.sem, turned.of(b, t))
                    if t % TC == 0:
                        dve.wait_ge(loaded[t // TC], b * 32 + 32)
                        dve.wait_ge(stored[t // TC], b * 16 + 16)
                    dve.tensor_tensor(out[:, t // TC, t % TC, :], y_ps[t % 4][:, 0:D], x1[:, t // TC, t % TC, :],
                                      ALU.add).then_inc(added.sem, 1)


def build(nc, a):
    with ExitStack() as ctx:
        sb = lambda name, shape, dt=F32: ctx.enter_context(nc.sbuf_tensor(name, shape, dt))
        ident = sb("ident", [P, P])
        ident_b = sb("ident_b", [P, P], BF16)
        causal_b = sb("causal_b", [P, P], BF16)
        neg_half = sb("neg_half", [P, 2 * H2])
        passed = ctx.enter_context(nc.semaphore("passed"))
        zeroed = ctx.enter_context(nc.semaphore("zeroed"))
        drawn = ctx.enter_context(nc.semaphore("drawn"))
        with nc.Block() as block:
            @block.gpsimd
            def _(pool):
                pool.memset(ident[:, :], 0.0).then_inc(zeroed, 1)
                pool.memset(ident_b[:, :], 0.0).then_inc(zeroed, 1)
                pool.memset(causal_b[:, :], 0.0).then_inc(zeroed, 1)
                pool.memset(neg_half[:, :], -0.5).then_inc(zeroed, 1)
                pool.wait_ge(zeroed, 4)
                for m in (ident, ident_b):
                    pool.affine_select(out=m[:, :], in_=m[:, :], compare_op=ALU.not_equal, fill=1.0, base=0,
                                       pattern=[[-1, P]], channel_multiplier=1).then_inc(drawn, 1)
                pool.affine_select(out=causal_b[:, :], in_=causal_b[:, :], compare_op=ALU.is_ge, fill=-1e30, base=0,
                                   pattern=[[-1, P]], channel_multiplier=1).then_inc(drawn, 1)
                pool.wait_ge(drawn, 3)
        with nc.sbuf_tensor("x_all", [P, B * NT, D], F32) as x_all:
            prepare(nc, x_all, ident, neg_half, passed, a)
            causal_attention(nc, x_all, ident, ident_b, causal_b, passed, a)
            project_causal(nc, x_all, ident, neg_half, passed, a)
        layers(nc, ident, neg_half, passed, a)
        finish(nc, ident, a)


def rotary_tables():
    f = np.float32
    half = np.arange(0, HD2, 2, dtype=f)
    inv_freq = (f(1.0) / f(10000.0) ** (half / f(HD2))).astype(f)
    t = np.arange(T, dtype=f)
    angle = t[:, None] * inv_freq[None, :]
    base = ((half + f(0.4 * HD2)) / f(1.4 * HD2)).astype(f)
    power = ((t - f(T // 2)) / f(WIN // 2)).astype(f)
    scale = base[None, :] ** power[:, None]
    twice = lambda x: np.concatenate([x, x], axis=-1)
    sign = np.where(np.arange(HD2) < HD2 // 2, f(-1), f(1))
    cos, sin, scale = np.cos(twice(angle)), np.sin(twice(angle)) * sign, twice(scale)
    q = f(-QK_SCALE)
    return np.stack([q * cos * scale, q * sin * scale, cos / scale, sin / scale], axis=1).astype(f)


_NAMES = {"x": "L0_attn_x", "wq": "L0_attn_wq", "bq": "L0_attn_bq", "wk": "L0_attn_wk", "bk": "L0_attn_bk",
          "wv": "L0_attn_wv", "bv": "L0_attn_bv", "wo": "L0_attn_wo", "bo": "L0_attn_bo", "wqkv": "L0_ffn_wqkv",
          "q_scale": "L0_ffn_q_scale", "k_scale": "L0_ffn_k_scale", "wo2": "L0_ffn_wo", "ln_g": "L0_ffn_ln_g",
          "ln_b": "L0_ffn_ln_b", "w1": "L0_ffn_w1", "b1": "L0_ffn_b1", "w2": "L0_ffn_w2", "b2": "L0_ffn_b2"}


def kernel(**inputs):
    import concourse.bacc as bacc
    from concourse.bass_utils import run_bass_kernel_spmd

    nc = bacc.Bacc("TRN2", target_bir_lowering=False, num_devices=1)
    nc.disable_value_cache = True
    arrays = {short: np.ascontiguousarray(inputs[name]) for short, name in _NAMES.items()}
    arrays["rotary"] = rotary_tables()
    a = {n: nc.dram_tensor(f"in_{n}", list(x.shape), mybir.dt.from_np(x.dtype), kind="ExternalInput").ap()
         for n, x in arrays.items()}
    scratch = {"v_scratch": ([B * NG, P, NT, HG * VW], F32), "qk_scratch": ([2, B * NG, 3, GF, T], BF16),
               "att_scratch": ([B * NG, T, GF], F32), "x1_scratch": ([B, T, D], F32), "xt_scratch": ([B, KD, P, T], F32),
               "ffn_weights": ([DEPTH, 2, P, WCOLS], F32)}
    for n, (shape, dt) in scratch.items():
        a[n] = nc.dram_tensor(n, shape, dt, kind="Internal").ap()
    a["out"] = nc.dram_tensor("out", [B, T, D], F32, kind="ExternalOutput").ap()
    build(nc, a)
    r = run_bass_kernel_spmd(nc, [{f"in_{n}": x for n, x in arrays.items()}], core_ids=[0])
    return r.results[0]["out"]
```
